# Optimizing a Trainium2 kernel written in Bass

```python
import numpy as np
import jax
import jax.numpy as jnp

def _softmax(x, axis=-1):
    return jax.nn.softmax(x, axis=axis)

def _gelu(x):
    return jax.nn.gelu(x, approximate=True)

def _silu(x):
    return jax.nn.silu(x)

def _sigmoid(x):
    return jax.nn.sigmoid(x)

def _layernorm(x, axis=-1, eps=1e-05):
    m = jnp.mean(x, axis=axis, keepdims=True)
    v = jnp.var(x, axis=axis, keepdims=True)
    return (x - m) / jnp.sqrt(v + eps)

def _scatter_add(tgt, idx, src, axis=0):
    return tgt.at[idx].add(src)

def _segment_sum(src, seg, n):
    return jax.ops.segment_sum(src, seg, n)
kernel_name = 'mk_conv_attn_hybrid_d2_conv_nhwc512_r4_e9dcb6'

def setup_inputs(seed: int=0):
    np.random.seed(seed)
    _w = jnp.asarray

    def _rec_inputs():
        import jax
        import jax.numpy as jnp
        _gk = jax.random.key(seed)
        x = 1.648e-05 + 1 * jax.random.normal(jax.random.fold_in(_gk, 1), (8, 48, 48, 128), jnp.float32)
        return x
    x = _rec_inputs()

    def _L0_conv_setup():
        import jax, jax.numpy as jnp
        import numpy as np
        D_MODEL = 128
        D_STATE = 16
        EXPAND = 2
        DT_RANK = 8
        D_INNER = EXPAND * D_MODEL
        LN_EPS = 1e-05

        def _ss2d(x, W_in, conv_k, W_xproj, W_dt, b_dt, A_log, Dskip, W_dtN, b_dtN, ln_g, ln_b, W_out, b_out):
            B, H, W_, _ = x.shape
            L = H * W_
            xz = x @ W_in
            xh, z = jnp.split(xz, 2, axis=-1)
            xc = jax.lax.conv_general_dilated(xh, conv_k, window_strides=(1, 1), padding='SAME', dimension_numbers=('NHWC', 'HWIO', 'NHWC'), feature_group_count=D_INNER)
            xp = xc @ W_xproj
            dt_r = xp[..., :DT_RANK]
            Bp = xp[..., DT_RANK:DT_RANK + D_STATE]
            Cp = xp[..., DT_RANK + D_STATE:]
            dt = dt_r @ W_dt + b_dt
            x_seq = xc.reshape(B, L, D_INNER)
            dt_seq = jax.nn.softplus(dt.reshape(B, L, D_INNER))
            B_seq = Bp.reshape(B, L, D_STATE)
            C_seq = Cp.reshape(B, L, D_STATE)
            A = -jnp.exp(A_log)
            dtN = dt_seq @ W_dtN + b_dtN

            def step(h, t):
                x_t, dt_t, dtN_t, B_t, C_t = t
                dA = jnp.exp(dt_t[:, :, None] * A)
                dB = dtN_t * B_t
                h = dA * h + dB[:, None, :] * x_t[:, :, None]
                y = jnp.einsum('bdn,bn->bd', h, C_t) + Dskip * x_t
                return (h, y)
            h0 = jnp.zeros((B, D_INNER, D_STATE), x.dtype)
            xs = (x_seq.transpose(1, 0, 2), dt_seq.transpose(1, 0, 2), dtN.transpose(1, 0, 2), B_seq.transpose(1, 0, 2), C_seq.transpose(1, 0, 2))
            _, ys = jax.lax.scan(step, h0, xs)
            y = ys.transpose(1, 0, 2).reshape(B, H, W_, D_INNER)
            mu = y.mean(-1, keepdims=True)
            var = ((y - mu) ** 2).mean(-1, keepdims=True)
            y = (y - mu) / jnp.sqrt(var + LN_EPS) * ln_g + ln_b
            y = y * jax.nn.silu(z)
            return y @ W_out + b_out
        key = jax.random.key(seed)
        ks = jax.random.split(key, 10)
        B, H, W = (8, 48, 48)
        inp = {'x': jax.random.normal(ks[0], (B, H, W, D_MODEL), jnp.float32), 'W_in': jax.random.normal(ks[1], (D_MODEL, 2 * D_INNER), jnp.float32) * 0.02, 'conv_k': jax.random.normal(ks[2], (3, 3, 1, D_INNER), jnp.float32) * 0.1, 'W_xproj': jax.random.normal(ks[3], (D_INNER, DT_RANK + 2 * D_STATE), jnp.float32) * 0.02, 'W_dt': jax.random.uniform(ks[4], (DT_RANK, D_INNER), jnp.float32, -0.1, 0.1), 'b_dt': jnp.full((D_INNER,), 0.1, jnp.float32), 'A_log': jax.random.normal(ks[5], (D_STATE,), jnp.float32) * 0.02, 'Dskip': jnp.ones((D_INNER,), jnp.float32), 'W_dtN': jax.random.normal(ks[6], (D_INNER, D_STATE), jnp.float32) * 0.02, 'b_dtN': jnp.zeros((D_STATE,), jnp.float32), 'ln_g': jnp.ones((D_INNER,), jnp.float32), 'ln_b': jnp.zeros((D_INNER,), jnp.float32), 'W_out': jax.random.normal(ks[7], (D_INNER, D_MODEL), jnp.float32) * 0.02, 'b_out': jnp.zeros((D_MODEL,), jnp.float32)}
        return inp
    _L0_conv_all = _L0_conv_setup()
    _L0_conv_in = {k: v for k, v in _L0_conv_all.items() if k in ('W_in', 'conv_k', 'W_xproj', 'W_dt', 'b_dt', 'A_log', 'Dskip', 'W_dtN', 'b_dtN', 'ln_g', 'ln_b', 'W_out', 'b_out')}
    del _L0_conv_all

    def _L1_attn_setup():
        import jax, jax.numpy as jnp
        import numpy as np
        HEADS = 8
        DIM_HEAD = 16
        EPS = 1e-05

        def layer_norm(x, gamma):
            mu = jnp.mean(x, axis=-1, keepdims=True)
            var = jnp.var(x, axis=-1, keepdims=True)
            return (x - mu) * jax.lax.rsqrt(var + EPS) * gamma
        key = jax.random.key(seed)
        k1, k2, k3 = jax.random.split(key, 3)
        b, n, dim = (4, 4096, 128)
        hidden = HEADS * DIM_HEAD
        x = jax.random.normal(k1, (b, n, dim), dtype=jnp.float32)
        norm_gamma = jnp.ones((dim,), dtype=jnp.float32)
        w_qkv = jax.random.normal(k2, (hidden * 3, dim), dtype=jnp.float32) * dim ** (-0.5)
        w_out = jax.random.normal(k3, (dim, hidden), dtype=jnp.float32) * hidden ** (-0.5)
        out_gamma = jnp.ones((dim,), dtype=jnp.float32)
        return {'x': x, 'norm_gamma': norm_gamma, 'w_qkv': w_qkv, 'w_out': w_out, 'out_gamma': out_gamma}
    _L1_attn_all = _L1_attn_setup()
    _L1_attn_in = {k: v for k, v in _L1_attn_all.items() if k in ('norm_gamma', 'w_qkv', 'w_out', 'out_gamma')}
    del _L1_attn_all

    def _L1_ffn_setup():
        import jax, jax.numpy as jnp
        import numpy as np
        NUM_EXPERTS = 8
        TOP_K = 2
        key = jax.random.key(seed)
        ks = jax.random.split(key, 6)
        B, S, D, F, E = (2, 512, 128, 384, NUM_EXPERTS)
        scale = 0.02
        return {'x': jax.random.normal(ks[0], (B, S, D), dtype=jnp.float32), 'Wg': jax.random.normal(ks[1], (D, E), dtype=jnp.float32) * scale, 'W1': jax.random.normal(ks[2], (E, D, F), dtype=jnp.float32) * scale, 'W2': jax.random.normal(ks[3], (E, F, D), dtype=jnp.float32) * scale, 'W3': jax.random.normal(ks[4], (E, D, F), dtype=jnp.float32) * scale, 'b3': jax.random.normal(ks[5], (E, F), dtype=jnp.float32) * scale}
    _L1_ffn_all = _L1_ffn_setup()
    _L1_ffn_in = {k: v for k, v in _L1_ffn_all.items() if k in ('Wg', 'W1', 'W2', 'W3', 'b3')}
    del _L1_ffn_all
    return {'x': x, 'L0_conv_W_in': _L0_conv_in['W_in'], 'L0_conv_conv_k': _L0_conv_in['conv_k'], 'L0_conv_W_xproj': _L0_conv_in['W_xproj'], 'L0_conv_W_dt': _L0_conv_in['W_dt'], 'L0_conv_b_dt': _L0_conv_in['b_dt'], 'L0_conv_A_log': _L0_conv_in['A_log'], 'L0_conv_Dskip': _L0_conv_in['Dskip'], 'L0_conv_W_dtN': _L0_conv_in['W_dtN'], 'L0_conv_b_dtN': _L0_conv_in['b_dtN'], 'L0_conv_ln_g': _L0_conv_in['ln_g'], 'L0_conv_ln_b': _L0_conv_in['ln_b'], 'L0_conv_W_out': _L0_conv_in['W_out'], 'L0_conv_b_out': _L0_conv_in['b_out'], 'L1_attn_norm_gamma': _L1_attn_in['norm_gamma'], 'L1_attn_w_qkv': _L1_attn_in['w_qkv'], 'L1_attn_w_out': _L1_attn_in['w_out'], 'L1_attn_out_gamma': _L1_attn_in['out_gamma'], 'L1_ffn_Wg': _L1_ffn_in['Wg'], 'L1_ffn_W1': _L1_ffn_in['W1'], 'L1_ffn_W2': _L1_ffn_in['W2'], 'L1_ffn_W3': _L1_ffn_in['W3'], 'L1_ffn_b3': _L1_ffn_in['b3']}

def reference(x, L0_conv_W_in, L0_conv_conv_k, L0_conv_W_xproj, L0_conv_W_dt, L0_conv_b_dt, L0_conv_A_log, L0_conv_Dskip, L0_conv_W_dtN, L0_conv_b_dtN, L0_conv_ln_g, L0_conv_ln_b, L0_conv_W_out, L0_conv_b_out, L1_attn_norm_gamma, L1_attn_w_qkv, L1_attn_w_out, L1_attn_out_gamma, L1_ffn_Wg, L1_ffn_W1, L1_ffn_W2, L1_ffn_W3, L1_ffn_b3):
    import jax
    import jax.numpy as jnp

    def _L0_conv_ref(x, W_in, conv_k, W_xproj, W_dt, b_dt, A_log, Dskip, W_dtN, b_dtN, ln_g, ln_b, W_out, b_out):
        import jax, jax.numpy as jnp
        import numpy as np
        D_MODEL = 128
        D_STATE = 16
        EXPAND = 2
        DT_RANK = 8
        D_INNER = EXPAND * D_MODEL
        LN_EPS = 1e-05

        def _ss2d(x, W_in, conv_k, W_xproj, W_dt, b_dt, A_log, Dskip, W_dtN, b_dtN, ln_g, ln_b, W_out, b_out):
            B, H, W_, _ = x.shape
            L = H * W_
            xz = x @ W_in
            xh, z = jnp.split(xz, 2, axis=-1)
            xc = jax.lax.conv_general_dilated(xh, conv_k, window_strides=(1, 1), padding='SAME', dimension_numbers=('NHWC', 'HWIO', 'NHWC'), feature_group_count=D_INNER)
            xp = xc @ W_xproj
            dt_r = xp[..., :DT_RANK]
            Bp = xp[..., DT_RANK:DT_RANK + D_STATE]
            Cp = xp[..., DT_RANK + D_STATE:]
            dt = dt_r @ W_dt + b_dt
            x_seq = xc.reshape(B, L, D_INNER)
            dt_seq = jax.nn.softplus(dt.reshape(B, L, D_INNER))
            B_seq = Bp.reshape(B, L, D_STATE)
            C_seq = Cp.reshape(B, L, D_STATE)
            A = -jnp.exp(A_log)
            dtN = dt_seq @ W_dtN + b_dtN

            def step(h, t):
                x_t, dt_t, dtN_t, B_t, C_t = t
                dA = jnp.exp(dt_t[:, :, None] * A)
                dB = dtN_t * B_t
                h = dA * h + dB[:, None, :] * x_t[:, :, None]
                y = jnp.einsum('bdn,bn->bd', h, C_t) + Dskip * x_t
                return (h, y)
            h0 = jnp.zeros((B, D_INNER, D_STATE), x.dtype)
            xs = (x_seq.transpose(1, 0, 2), dt_seq.transpose(1, 0, 2), dtN.transpose(1, 0, 2), B_seq.transpose(1, 0, 2), C_seq.transpose(1, 0, 2))
            _, ys = jax.lax.scan(step, h0, xs)
            y = ys.transpose(1, 0, 2).reshape(B, H, W_, D_INNER)
            mu = y.mean(-1, keepdims=True)
            var = ((y - mu) ** 2).mean(-1, keepdims=True)
            y = (y - mu) / jnp.sqrt(var + LN_EPS) * ln_g + ln_b
            y = y * jax.nn.silu(z)
            return y @ W_out + b_out
        return _ss2d(x, W_in, conv_k, W_xproj, W_dt, b_dt, A_log, Dskip, W_dtN, b_dtN, ln_g, ln_b, W_out, b_out)

    def _L1_attn_ref(x, norm_gamma, w_qkv, w_out, out_gamma):
        import jax, jax.numpy as jnp
        import numpy as np
        HEADS = 8
        DIM_HEAD = 16
        EPS = 1e-05

        def layer_norm(x, gamma):
            mu = jnp.mean(x, axis=-1, keepdims=True)
            var = jnp.var(x, axis=-1, keepdims=True)
            return (x - mu) * jax.lax.rsqrt(var + EPS) * gamma
        b, n, dim = x.shape
        h, d = (HEADS, DIM_HEAD)
        scale = d ** (-0.5)
        x = layer_norm(x, norm_gamma)
        qkv = jnp.einsum('bnc,fc->bnf', x, w_qkv)
        q, k, v = jnp.split(qkv, 3, axis=-1)
        to_bhnd = lambda t: t.reshape(b, n, h, d).transpose(0, 2, 1, 3)
        q, k, v = (to_bhnd(q), to_bhnd(k), to_bhnd(v))
        q = jax.nn.softmax(q, axis=-1) * scale
        k = jax.nn.softmax(k, axis=-2)
        context = jnp.einsum('bhnd,bhne->bhde', k, v)
        out = jnp.einsum('bhde,bhnd->bhne', context, q)
        out = out.transpose(0, 2, 1, 3).reshape(b, n, h * d)
        out = jnp.einsum('bnf,cf->bnc', out, w_out)
        return layer_norm(out, out_gamma)

    def _L1_ffn_ref(x, Wg, W1, W2, W3, b3):
        import jax, jax.numpy as jnp
        import numpy as np
        NUM_EXPERTS = 8
        TOP_K = 2
        logits = jnp.einsum('bsd,de->bse', x, Wg)
        top_logits, top_idx = jax.lax.top_k(logits, TOP_K)
        top_w = jax.nn.softmax(top_logits, axis=-1)
        onehot = jax.nn.one_hot(top_idx, NUM_EXPERTS, dtype=x.dtype)
        C = jnp.sum(onehot * top_w[..., None], axis=-2)
        h = jnp.einsum('bsd,edf->bsef', x, W1)
        g = jnp.einsum('bsd,edf->bsef', x, W3) + b3
        act = jax.nn.silu(h) * g
        out = jnp.einsum('bse,bsef,efd->bsd', C, act, W2)
        return out

    def _gn(v, G=32, eps=1e-05):
        B_, H_, W_, C_ = v.shape
        g = v.reshape(B_, H_, W_, G, C_ // G)
        m = jnp.mean(g, axis=(1, 2, 4), keepdims=True)
        s = jnp.var(g, axis=(1, 2, 4), keepdims=True)
        return ((g - m) / jnp.sqrt(s + eps)).reshape(v.shape)

    def _ln_c(v, eps=1e-06):
        m = jnp.mean(v, axis=-1, keepdims=True)
        s = jnp.var(v, axis=-1, keepdims=True)
        return (v - m) / jnp.sqrt(s + eps)

    def _ln_t(v, eps=1e-05):
        m = jnp.mean(v, axis=-1, keepdims=True)
        s = jnp.var(v, axis=-1, keepdims=True)
        return (v - m) / jnp.sqrt(s + eps)

    def _to_tokens(v):
        B_, H_, W_, C_ = v.shape
        return v.reshape(B_, H_ * W_, C_)

    def _from_tokens(t, like):
        return t.reshape(like.shape)
    x = x + _L0_conv_ref(_gn(x), L0_conv_W_in, L0_conv_conv_k, L0_conv_W_xproj, L0_conv_W_dt, L0_conv_b_dt, L0_conv_A_log, L0_conv_Dskip, L0_conv_W_dtN, L0_conv_b_dtN, L0_conv_ln_g, L0_conv_ln_b, L0_conv_W_out, L0_conv_b_out)
    t = _to_tokens(x)
    t = t + _L1_attn_ref(_ln_t(t), L1_attn_norm_gamma, L1_attn_w_qkv, L1_attn_w_out, L1_attn_out_gamma)
    t = t + _L1_ffn_ref(_ln_t(t), L1_ffn_Wg, L1_ffn_W1, L1_ffn_W2, L1_ffn_W3, L1_ffn_b3)
    x = _from_tokens(t, x)
    return x

_drawn_inputs = setup_inputs


def setup_inputs(seed=0):
    import zlib

    import numpy as np

    out = dict(_drawn_inputs(seed))
    spreads = {'L0_conv_b_dt': (0.10000000149011612, 0.6),
     'L0_conv_Dskip': (1.0, 0.6),
     'L0_conv_b_dtN': (0.0, 0.8),
     'L0_conv_ln_g': (1.0, 0.6),
     'L0_conv_ln_b': (0.0, 0.8),
     'L0_conv_b_out': (0.0, 0.1),
     'L1_attn_norm_gamma': (1.0, 0.2),
     'L1_attn_out_gamma': (1.0, 0.2)}
    factors = {'L0_conv_W_xproj': 8.0,
     'L0_conv_W_dt': 35.724,
     'L0_conv_A_log': 28.79,
     'L0_conv_W_dtN': 8.0,
     'L1_ffn_Wg': 8.0,
     'L1_ffn_W1': 8.0,
     'L1_ffn_W2': 8.0,
     'L1_ffn_W3': 8.0,
     'L1_ffn_b3': 8.0}
    for name, (base, spread) in spreads.items():
        noise = np.random.default_rng([zlib.crc32(name.encode()), seed]).standard_normal(out[name].shape)
        drawn = base * np.exp(spread * noise) if base else spread * noise
        out[name] = jnp.asarray(drawn.astype(out[name].dtype))
    for name, factor in factors.items():
        out[name] = (out[name] * factor).astype(out[name].dtype)
    return out
```

```python
from contextlib import ExitStack

import numpy as np

import concourse.bass as bass
from concourse import mybir

ALU = mybir.AluOpType
ACT = mybir.ActivationFunctionType
AX = mybir.AxisListType
F32 = mybir.dt.float32
BF16 = mybir.dt.bfloat16
U32 = mybir.dt.uint32

P = 128
B, H, W, D = 8, 48, 48, 128
L = H * W
DI, NS, RK = 256, 16, 8
HV = DI // P
T = 384
ROWS = T // W
NC = L // T
TT = T // P
NT = L // P
JB = P // NS
NB = DI // JB
QD = 4
NH, DH = 8, 16
NE, F = 8, 384
MF = F // P
PARTS = 3
N_CLEAR, N_SETUP = 3, 17
ACT_STEPS, DVE_STEPS = 29, 107
BESIDE = (("C", 1, 1), ("B", 2, 1), ("dtr", 3, 1), ("dt0", 5, 1), ("dt1", 6, 1), ("mean", 7, -1), ("z0", 8, 1),
          ("z1", 9, 1), ("var", 11, -1), ("dtN", 14, 1), ("out", 18, -1))
CONV_AT = (0, 11)
FOLD_LAG = 3
HS = 8


def constants():
    eye = np.eye(P, dtype=np.float32)
    idx = np.arange(P)
    group = (idx[:, None] // 4 == idx[None, :] // 4).astype(np.float32) / 4
    heads = (idx[:, None] // DH == idx[None, :] // DH).astype(np.float32)
    mean = np.full((P, P), 1.0 / DI, np.float32)
    r = np.arange(32 * PARTS) % 32
    copy = np.stack([(r[:, None] == JB * b + idx[None, :] % JB) for b in range(4)], 1)
    fold = np.stack([(JB * b + idx[:, None] % JB == np.arange(32)[None, :]) for b in range(4)], 1)
    iota = np.broadcast_to(np.arange(NE, dtype=np.float32), (P, NE))
    return {
        "eye": eye, "group": group, "heads": heads, "mean": mean, "iota": np.ascontiguousarray(iota),
        "copy": np.ascontiguousarray(copy.astype(np.float32)), "fold": np.ascontiguousarray(fold.astype(np.float32)),
    }


def build(nc, a):
    with ExitStack() as ctx:
        def sb(name, shape, dt=F32):
            return ctx.enter_context(nc.sbuf_tensor(name, shape, dt))

        def psum(name):
            return ctx.enter_context(nc.psum_tensor(name, [P, 512], F32))

        eye, group, heads, mean = (sb(n, [P, P]) for n in ("eye", "group", "heads", "mean"))
        iota = sb("iota", [P, NE])
        fold = sb("fold", [P, 4, 32])
        copy = sb("copy", [32 * PARTS, 4, P], BF16)
        w_conv = sb("w_conv", [P, 9, DI])
        w_z = sb("w_z", [P, DI])
        w_xp = sb("w_xp", [P, HV, RK + 2 * NS])
        w_b, w_c, w_n = (sb(n, [P, HV, P]) for n in ("w_b", "w_c", "w_n"))
        w_dtn = sb("w_dtn", [P, HV, NS])
        w_dt = sb("w_dt", [RK, DI])
        w_out = sb("w_out", [P, HV, D])
        b_out, ones = sb("b_out", [1, D]), sb("ones", [1, P])
        vecs = sb("vecs", [P, 16])
        w_qkv = sb("w_qkv", [P, 3 * D])
        w_proj = sb("w_proj", [P, D])
        out_gamma = sb("out_gamma", [P, D])
        w_gate = sb("w_gate", [P, NE])
        b3 = sb("b3", [P, NE, MF])
        w1, w3, w2 = (sb(n, [P, 2, F]) for n in ("w1", "w3", "w2"))
        b_dt, d_skip, ln_g, ln_b = (vecs[:, 2 * k:2 * k + 2] for k in range(4))
        b_dtn, decay_rate, eps_ln, norm_gamma = (vecs[:, k:k + 1] for k in (8, 9, 10, 11))
        x_tok = sb("x_tok", [P, NT, D])
        gx = sb("gx", [P, H + 2, W + 2])
        t1 = sb("t1", [P, NT, D])
        big_t = sb("big_t", [P, L])
        big_k = sb("big_k", [P, L])
        big_u = sb("big_u", [P, NT, D])
        qv = sb("qv", [P, 2, NT, D])
        xc = sb("xc", [P, 3, HV, T])
        zc = sb("zc", [P, HV, T])
        z_tmp = sb("z_tmp", [P, HV, T])
        sz = sb("sz", [P, 2, HV, T])
        dt = sb("dt", [P, HV, T])
        dt_tmp = z_tmp
        dt_r = sb("dt_r", [RK, T])
        parts = sb("parts", [P, PARTS, HV, T], BF16)
        rest = sb("rest", [P, HV, T])
        x_stack = sb("x_stack", [32 * PARTS, 2, HV * QD, T], BF16)
        dt_stack = sb("dt_stack", [32 * PARTS, 2, HV * QD, T], BF16)
        b_rep = sb("b_rep", [P, T])
        db_rep = sb("db_rep", [P, 2, T])
        c_rep = sb("c_rep", [P, 2, T])
        decay = sb("decay", [P, 2, T])
        inflow = sb("inflow", [P, 2, T])
        state = sb("state", [P, HS, T])
        carry = sb("carry", [P, NB])
        prod = sb("prod", [P, HS, T])
        y = sb("y", [P, HV, T])
        y_sq = sb("y_sq", [P, HV, T])
        y_rs = sb("y_rs", [P, T])
        gst = sb("gst", [P, NC, 6])
        gmv = sb("gmv", [P, 8])
        gdev = sb("gdev", [P, 2 * NC])
        st = sb("st", [P, NT, 6])
        mv = sb("mv", [P, NT, 2])
        r1, r2, nb = (sb(n, [P, NT]) for n in ("r1", "r2", "nb"))
        q_max, q_sum = sb("q_max", [P, NT * NH]), sb("q_sum", [P, NT * NH])
        k_col = sb("k_col", [P, 4])
        ctx_t, ctx_o = sb("ctx_t", [P, D]), sb("ctx_o", [P, D])
        logit, top, gate, pick = (sb(n, [P, NT, NE]) for n in ("logit", "top", "gate", "pick"))
        where = sb("where", [P, NT, NE], U32)
        place = sb("place", [P, NT, NE])
        gw = sb("gw", [P, 4, NT])

        ps_dt = [psum("ps_dt0"), psum("ps_dt1")]
        ps_x = [psum("ps_x0"), psum("ps_x1")]
        ps_y = psum("ps_y")
        ps_conv = psum("ps_conv")
        ps_aux = [psum("ps_aux0"), psum("ps_aux1")]

        class Sem:

            def __init__(self, name, per, unit=1, first=0):
                self.sem = ctx.enter_context(nc.semaphore(name))
                self.per, self.unit, self.first = per, unit, first

            def at(self, i, k):
                return i * (self.per * self.unit) + (self.first + k * self.unit)

        uses = [f"xT{g}" for g in range(NC)] + ["gm", "gv"]
        uses += [f"{name}0" for name, n, dc in BESIDE if dc == 1]
        for c in range(NC):
            uses += [f"{name}{c + dc}" for name, n, dc in BESIDE if 0 <= c + dc < NC]
        uses += [f"{name}{NC - 1}" for name, n, dc in BESIDE if dc == -1]
        uses += [f"xnT{g}" for g in range(NC)] + [f"kT{g}" for g in range(NC)] + [f"qv{g}" for g in range(NT // 2)]
        uses += [f"ek{g}" for g in range(NC)] + ["ctx", "ctx2"] + [f"qT{g}" for g in range(NC)]
        uses += [f"ao{g}" for g in range(NC)] + [f"uT{g}" for g in range(NC)] + ["logit"]
        uses += [f"moe{e}_{g}" for e in range(NE) for g in range(NC)]
        aux_of = {}
        for n, name in enumerate(uses):
            aux_of[name] = (n % 2, n // 2)
        aux_per = [(len(uses) + 1 - b) // 2 for b in range(2)]
        aux_full = [Sem(f"aux_full{b}", aux_per[b]) for b in range(2)]
        aux_free = [Sem(f"aux_free{b}", aux_per[b], first=1) for b in range(2)]

        def aux(name):
            return ps_aux[aux_of[name][0]]

        def free(i, name):
            b, k = aux_of[name]
            return aux_free[b].sem, aux_free[b].at(i, k)

        def full(i, name):
            b, k = aux_of[name]
            return aux_full[b].sem, aux_full[b].at(i, k + 1)

        def read(i, name):
            b, k = aux_of[name]
            return aux_free[b].sem, aux_free[b].at(i, k + 1)

        def fills(name):
            return aux_full[aux_of[name][0]].sem

        def frees(name):
            return aux_free[aux_of[name][0]].sem

        def other_bank(name, *inputs):
            there = [x for x in inputs if aux_of[x][0] != aux_of[name][0]]
            return [max(there, key=lambda x: aux_of[x][1])] if there else []

        SC = NB * NC
        MO = NE * NC * MF
        s_const = Sem("s_const", 0)
        s_clear, s_setup, s_rate = Sem("s_clear", 0), Sem("s_setup", 0), Sem("s_rate", 0)
        s_x = Sem("s_x", 1, 16 * NC)
        s_norm = Sem("s_norm", 1)
        s_z = Sem("s_z", NC)
        s_zmin = Sem("s_zmin", NC)
        s_zexp = Sem("s_zexp", NC)
        s_sz = Sem("s_sz", NC)
        s_dtl = Sem("s_dtl", NC)
        s_dt = Sem("s_dt", NC)
        s_hi, s_rest, s_mid, s_lo = (Sem(n, 2 * NC) for n in ("s_hi", "s_rest", "s_mid", "s_lo"))
        s_xstack = Sem("s_xstack", NC, 16 * PARTS * QD)
        s_dtstack = Sem("s_dtstack", NC, 16 * PARTS * QD)
        s_dtrep = Sem("s_dtrep", SC + MO)
        s_dtread = Sem("s_dtread", SC + MO, first=1)
        s_xrep = Sem("s_xrep", SC + MO)
        s_xread = Sem("s_xread", SC + MO, first=1)
        s_state = Sem("s_state", SC)
        s_prod = Sem("s_prod", SC)
        s_fold = Sem("s_fold", SC // QD)
        s_y = Sem("s_y", 2 * NC)
        s_ysq = Sem("s_ysq", NC)
        s_yrs = Sem("s_yrs", NC)
        s_yn = Sem("s_yn", NC)
        s_yaff = Sem("s_yaff", NC)
        s_yg = Sem("s_yg", NC)
        s_conv = Sem("s_conv", 2 * NC)
        s_xc = Sem("s_xc", 2 * NC, first=1)
        s_gn = Sem("s_gn", 2)
        s_var = Sem("s_var", 4)
        s_root = Sem("s_root", 5)
        s_coef = Sem("s_coef", 3)
        s_xn = Sem("s_xn", 3 * NC)
        s_qsub = Sem("s_qsub", 1)
        s_qexp = Sem("s_qexp", 1)
        s_q = Sem("s_q", 1)
        s_top, s_topexp = Sem("s_top", 1), Sem("s_topexp", 1)
        act_step, dve_step = Sem("act_step", ACT_STEPS), Sem("dve_step", DVE_STEPS)
        s_kmax = Sem("s_kmax", 1)
        s_kexp = Sem("s_kexp", 1)
        s_w = [Sem(f"s_w{b}", NE // 2, 48) for b in range(2)]
        s_out = Sem("s_out", 1, 16, first=16)

        hidden = prod
        silu = decay

        block = ctx.enter_context(nc.Block())
        n_const = 0

        @block.sync
        def _(sp):
            nonlocal n_const
            loads = [
                (eye[:, :], a["eye"]), (group[:, :], a["group"]), (heads[:, :], a["heads"]), (mean[:, :], a["mean"]),
                (iota[:, :], a["iota"]), (fold[:, :, :], a["fold"]),
                (prod[0:32 * PARTS, 0:2, 0:256].rearrange("p s t -> p s t"),
                 a["copy"].rearrange("p (s b) m -> p s (b m)", s=2)),
                (y[:, 0, 0:DI], a["w_in"][:, 0:DI]), (w_z[:, :], a["w_in"][:, DI:2 * DI]),
                (state[:, 0:6, :].rearrange("p s t -> p (s t)"), a["conv_k"].broadcast_to([P, 9 * DI])),
                (w_xp[:, :, :], a["w_xp"].rearrange("(h p) n -> p h n", p=P)),
                (w_dtn[:, :, :], a["w_dtn"].rearrange("(h p) n -> p h n", p=P)),
                (w_dt[:, :], a["w_dt"]),
                (w_out[:, :, :], a["w_out"].rearrange("(h p) n -> p h n", p=P)),
                (b_out[:, :], a["b_out"]), (vecs[:, 0:10], a["vecs"]), (vecs[:, 11:12], a["norm_gamma"]),
                (w_qkv[:, :], a["w_qkv"]), (w_proj[:, :], a["w_proj"]), (out_gamma[:, :], a["out_gamma"].broadcast_to([P, D])),
                (w_gate[:, :], a["w_gate"]), (b3[:, :, :], a["b3"]),
            ]
            for dst, src in loads:
                sp.dma_start(dst, src).then_inc(s_const.sem, 16)
            n_const = 16 * len(loads)

            with sp.Fori(0, B) as i:
                for c in range(NC):
                    par = c % 2
                    for s_full, stack, k in ((s_xstack, x_stack, 2 * c), (s_dtstack, dt_stack, 2 * c + 1)):
                        sp.wait_ge(s_lo.sem, s_lo.at(i, k + 1))
                        for part in range(PARTS):
                            for q in range(QD):
                                dst = stack[32 * part:32 * part + 32, par].rearrange("p (h q) t -> p h q t", q=QD)[:, :, q, :]
                                sp.dma_start(dst, parts[32 * q:32 * q + 32, part]).then_inc(s_full.sem, 16)
                for e in range(NE):
                    if e >= 2:
                        sp.wait_ge(*read(i, f"moe{e - 2}_{NC - 1}"))
                    for dst, src in ((w1, a["w1"]), (w3, a["w3"])):
                        sp.dma_start(dst[:, e % 2, :], src[e]).then_inc(s_w[e % 2].sem, 16)
                    sp.dma_start(w2[:, e % 2, :].rearrange("p (m d) -> p m d", m=MF),
                                 a["w2"][e].rearrange("(m p) d -> p m d", p=P)).then_inc(s_w[e % 2].sem, 16)

        @block.gpsimd
        def _(pool):
            pool.memset(gx[:, :, :], 0.0).then_inc(s_clear.sem, 1)
            pool.memset(ones[:, :], 1.0).then_inc(s_clear.sem, 1)
            pool.memset(eps_ln, 1e-5).then_inc(s_clear.sem, 1)
            pool.wait_ge(s_clear.sem, N_CLEAR)
            with pool.Fori(0, B) as i:
                for c in range(NC):
                    pool.wait_ge(*read(i, f"C{c}"))
                    for n in range(NB):
                        k = NB * c + n
                        pool.wait_ge(s_state.sem, s_state.at(i, k + 1))
                        if k >= HS:
                            pool.wait_ge(s_fold.sem, s_fold.at(i, (k - HS) // QD + 1))
                        pool.tensor_tensor(prod[:, n % HS, :], state[:, n % HS, :], c_rep[:, c % 2, :], ALU.mult).then_inc(s_prod.sem, 1)

        @block.tensor
        def _(pe):
            pe.wait_ge(s_const.sem, n_const)
            pe.wait_ge(s_clear.sem, N_CLEAR)
            pe.wait_ge(s_setup.sem, N_SETUP)

            def transposes(i, names, src):
                for g, name in enumerate(names):
                    pe.wait_ge(*free(i, name))
                    for k in range(TT):
                        ins = pe.transpose(aux(name)[:, P * k:P * k + P], src(TT * g + k), eye[:, :])
                    ins.then_inc(fills(name), 1)

            def group_norm(i):
                pe.wait_ge(s_x.sem, s_x.at(i, 1))
                transposes(i, [f"xT{g}" for g in range(NC)], lambda k: x_tok[:, k, :])
                for k, name in enumerate(("gm", "gv")):
                    pe.wait_ge(*free(i, name))
                    pe.wait_ge(s_gn.sem, s_gn.at(i, k + 1))
                    pe.matmul(aux(name)[:, 0:1], group[:, :], gmv[:, 2 * k:2 * k + 1], start=True, stop=True).then_inc(fills(name), 1)

            def halves(i, name, lhs, rhs, rows=P, inputs=()):
                pe.wait_ge(*free(i, name))
                for x in other_bank(name, *inputs):
                    pe.wait_ge(*read(i, x))
                for hf in range(HV):
                    ins = pe.matmul(aux(name)[0:rows, 0:T], lhs[:, hf, :], rhs[:, hf, :], start=hf == 0, stop=hf == HV - 1)
                ins.then_inc(fills(name), 1)

            def conv(i, c, hf, tap):
                if tap == 0:
                    pe.wait_ge(s_xc.sem, s_xc.at(i, 2 * c + hf))
                dy, dx = tap // 3, tap % 3
                ins = pe.matmul(ps_conv[:, 0:T], w_conv[:, tap, P * hf:P * hf + P],
                                gx[:, ROWS * c + dy:ROWS * c + dy + ROWS, dx:dx + W], start=tap == 0, stop=tap == 8)
                if tap == 8:
                    ins.then_inc(s_conv.sem, 1)

            def project(i, c, name):
                use = f"{name}{c}"
                hf = int(name[-1]) if name[-1] in "01" else 0
                pe.wait_ge(*free(i, use))
                if name == "C":
                    pe.wait_ge(s_xc.sem, s_xc.at(i, 2 * c + 2))
                if name[:2] == "dt" and name[-1] in "01":
                    for x in other_bank(use, f"dtr{c}"):
                        pe.wait_ge(*read(i, x))
                    ins = pe.matmul(aux(use)[:, 0:T], w_dt[:, P * hf:P * hf + P], dt_r[:, :], start=True, stop=True)
                elif name[0] == "z":
                    ins = pe.matmul(aux(use)[:, 0:T], w_z[:, P * hf:P * hf + P],
                                    gx[:, ROWS * c + 1:ROWS * c + 1 + ROWS, 1:1 + W], start=True, stop=True)
                else:
                    if name == "dtN":
                        pe.wait_ge(s_dt.sem, s_dt.at(i, c + 1))
                    lhs = {"B": w_b, "C": w_c, "dtr": w_xp[:, :, 0:RK], "dtN": w_n}[name]
                    rhs = dt if name == "dtN" else xc[:, c % 3]
                    rows = RK if name == "dtr" else P
                    for h in range(HV):
                        ins = pe.matmul(aux(use)[0:rows, 0:T], lhs[:, h, :], rhs[:, h, :], start=h == 0, stop=h == HV - 1)
                ins.then_inc(fills(use), 1)

            def fold_quad(i, c, m):
                hf, b = m // 4, m % 4
                if b == 0 and (c or hf):
                    pe.wait_ge(s_y.sem, s_y.at(i, 2 * c + hf))
                pe.wait_ge(s_prod.sem, s_prod.at(i, NB * c + QD * (m + 1)))
                for q in range(QD):
                    ins = pe.matmul(ps_y[32 * q:32 * q + 32, 0:T], fold[:, b, :], prod[:, (QD * m + q) % HS, :],
                                    start=b == 0, stop=b == 3)
                ins.then_inc(s_fold.sem, 1)

            def beside(i, c, n):
                if c + 2 < NC:
                    for hf in range(HV):
                        if CONV_AT[hf] <= n < CONV_AT[hf] + 9:
                            conv(i, c + 2, hf, n - CONV_AT[hf])
                for name, at, dc in BESIDE:
                    if at == n and 0 <= c + dc < NC:
                        if dc == 1:
                            project(i, c + 1, name)
                        else:
                            finish(i, c - 1, name)

            def scan(i, c):
                par = c % 2
                pe.wait_ge(s_dtstack.sem, s_dtstack.at(i, c + 1))
                pe.wait_ge(s_xstack.sem, s_xstack.at(i, c + 1))
                for n in range(NB):
                    k = NB * c + n
                    hf, b, q = n // 16, n % 16 // 4, n % 4
                    pe.wait_ge(s_dtread.sem, s_dtread.at(i, max(k - 1, 0)))
                    pe.matmul(ps_dt[n % 2][:, 0:T], copy[:, b, :], dt_stack[:, par, QD * hf + q, :],
                              start=True, stop=True).then_inc(s_dtrep.sem, 1)
                    pe.wait_ge(s_xread.sem, s_xread.at(i, max(k - 1, 0)))
                    pe.matmul(ps_x[n % 2][:, 0:T], copy[:, b, :], x_stack[:, par, QD * hf + q, :],
                              start=True, stop=True).then_inc(s_xrep.sem, 1)
                    if n % QD == FOLD_LAG and k >= QD:
                        fold_quad(i, (k - QD) // NB, (n // QD - 1) % (NB // QD))
                    beside(i, c, n)

            def finish(i, c, name):
                use = f"{name}{c}"
                pe.wait_ge(*free(i, use))
                if name == "mean":
                    pe.wait_ge(s_y.sem, s_y.at(i, 2 * c + 2))
                elif name == "var":
                    pe.wait_ge(s_ysq.sem, s_ysq.at(i, c + 1))
                else:
                    pe.wait_ge(s_yg.sem, s_yg.at(i, c + 1))
                if name != "out":
                    src = y if name == "mean" else y_sq
                    for hf in range(HV):
                        ins = pe.matmul(aux(use)[:, 0:T], mean[:, :], src[:, hf, :], start=hf == 0, stop=hf == 1)
                else:
                    for k in range(TT):
                        o = aux(use)[:, P * k:P * k + P]
                        for hf in range(HV):
                            pe.matmul(o, y[:, hf, P * k:P * k + P], w_out[:, hf, :], start=hf == 0, stop=False)
                        ins = pe.matmul(o, ones[0:1, :], b_out[0:1, :], start=False, stop=True)
                ins.then_inc(fills(use), 1)

            def attention(i):
                names = [f"xnT{g}" for g in range(NC)]
                for g, name in enumerate(names):
                    pe.wait_ge(s_xn.sem, s_xn.at(i, g + 1))
                    pe.wait_ge(*free(i, name))
                    for k in range(TT):
                        ins = pe.transpose(aux(name)[:, P * k:P * k + P], big_u[:, TT * g + k, :], eye[:, :])
                    ins.then_inc(fills(name), 1)
                for g in range(NC):
                    name = f"kT{g}"
                    pe.wait_ge(*free(i, name))
                    for x in other_bank(name, f"xnT{g}"):
                        pe.wait_ge(*read(i, x))
                    pe.matmul(aux(name)[:, 0:T], w_qkv[:, D:2 * D], big_t[:, T * g:T * g + T], start=True, stop=True).then_inc(fills(name), 1)
                for g in range(NT // 2):
                    name = f"qv{g}"
                    pe.wait_ge(*free(i, name))
                    for x in other_bank(name, *(f"xnT{h}" for h in range(2 * g // TT, (2 * g + 1) // TT + 1))):
                        pe.wait_ge(*read(i, x))
                    for k in range(2):
                        lhs = big_t[:, P * (2 * g + k):P * (2 * g + k + 1)]
                        for w in range(2):
                            ins = pe.matmul(aux(name)[:, D * (2 * k + w):D * (2 * k + w + 1)], lhs, w_qkv[:, 2 * w * D:(2 * w + 1) * D],
                                            start=True, stop=True)
                    ins.then_inc(fills(name), 1)
                pe.wait_ge(s_kexp.sem, s_kexp.at(i, 1))
                transposes(i, [f"ek{g}" for g in range(NC)], lambda k: big_k[:, P * k:P * k + P])
                pe.wait_ge(*free(i, "ctx"))
                for x in other_bank("ctx", *(f"ek{g}" for g in range(NC)), *(f"qv{g}" for g in range(NT // 2))):
                    pe.wait_ge(*read(i, x))
                for k in range(NT):
                    ins = pe.matmul(aux("ctx")[:, 0:D], qv[:, 1, k, :], big_u[:, k, :], start=k == 0, stop=k == NT - 1)
                ins.then_inc(fills("ctx"), 1)
                pe.wait_ge(*free(i, "ctx2"))
                for x in other_bank("ctx2", "ctx"):
                    pe.wait_ge(*read(i, x))
                pe.matmul(aux("ctx2")[:, 0:D], ctx_t[:, :], w_proj[:, :], start=True, stop=True).then_inc(fills("ctx2"), 1)
                pe.wait_ge(s_q.sem, s_q.at(i, 1))
                transposes(i, [f"qT{g}" for g in range(NC)], lambda k: qv[:, 0, k, :])
                for g in range(NC):
                    name = f"ao{g}"
                    pe.wait_ge(*free(i, name))
                    for x in other_bank(name, "ctx2", f"qT{g}"):
                        pe.wait_ge(*read(i, x))
                    for k in range(TT):
                        o = T * g + P * k
                        ins = pe.matmul(aux(name)[:, P * k:P * k + P], big_t[:, o:o + P], ctx_o[:, :], start=True, stop=True)
                    ins.then_inc(fills(name), 1)
                for g in range(NC):
                    name = f"uT{g}"
                    pe.wait_ge(s_xn.sem, s_xn.at(i, 2 * NC + g + 1))
                    pe.wait_ge(*free(i, name))
                    for k in range(TT):
                        ins = pe.transpose(aux(name)[:, P * k:P * k + P], big_u[:, TT * g + k, :], eye[:, :])
                    ins.then_inc(fills(name), 1)
                pe.wait_ge(*free(i, "logit"))
                for x in other_bank("logit", *(f"uT{g}" for g in range(NC))):
                    pe.wait_ge(*read(i, x))
                for k in range(NT):
                    ins = pe.matmul(aux("logit")[:, NE * k:NE * k + NE], big_t[:, P * k:P * k + P], w_gate[:, :], start=True, stop=True)
                ins.then_inc(fills("logit"), 1)

            def experts(i):
                u = 0

                def sums(e, g):
                    name = f"moe{e}_{g}"
                    pe.wait_ge(*free(i, name))
                    n = MF * (NC * e + g)
                    pe.wait_ge(s_xread.sem, s_xread.at(i, SC + n + MF))
                    for k in range(TT):
                        for m in range(MF):
                            ins = pe.matmul(aux(name)[:, P * k:P * k + P], hidden[:, (n + m) % 6, P * k:P * k + P],
                                            w2[:, e % 2, P * m:P * m + P], start=m == 0, stop=m == MF - 1)
                    ins.then_inc(fills(name), 1)

                last = None
                for e in range(NE):
                    pe.wait_ge(s_w[e % 2].sem, s_w[e % 2].at(i, e // 2 + 1))
                    for g in range(NC):
                        for m in range(MF):
                            rhs = big_t[:, T * g:T * g + T]
                            pe.wait_ge(s_dtread.sem, s_dtread.at(i, SC + u - 1))
                            pe.matmul(ps_dt[u % 2][:, 0:T], w1[:, e % 2, P * m:P * m + P], rhs, start=True, stop=True).then_inc(s_dtrep.sem, 1)
                            pe.wait_ge(s_xread.sem, s_xread.at(i, SC + u - 1))
                            pe.matmul(ps_x[u % 2][:, 0:T], w3[:, e % 2, P * m:P * m + P], rhs, start=True, stop=True).then_inc(s_xrep.sem, 1)
                            u += 1
                        if last:
                            sums(*last)
                        last = (e, g)
                sums(*last)

            with pe.Fori(0, B) as i:
                group_norm(i)
                pe.wait_ge(s_norm.sem, s_norm.at(i, 1))
                for c in range(2):
                    for hf in range(HV):
                        for tap in range(9):
                            conv(i, c, hf, tap)
                for name, at, dc in BESIDE:
                    if dc == 1:
                        project(i, 0, name)
                for c in range(NC):
                    scan(i, c)
                fold_quad(i, NC - 1, NB // QD - 1)
                for name, at, dc in BESIDE:
                    if dc == -1:
                        finish(i, NC - 1, name)
                attention(i)
                experts(i)

        @block.scalar
        def _(act):
            for s in (aux_free[0], aux_free[1], s_dtread, s_xread, s_xc, s_out):
                act.sem_inc(s.sem, s.first)
            act.wait_ge(s_const.sem, n_const)
            act.wait_ge(s_clear.sem, N_CLEAR)
            act.wait_ge(s_setup.sem, N_SETUP)
            act.activation(y_rs[:, 0:1], decay_rate, ACT.Exp).then_inc(s_rate.sem, 1)
            act.wait_ge(s_rate.sem, 1)
            act.activation(decay_rate, y_rs[:, 0:1], ACT.Copy, scale=-1.0).then_inc(s_rate.sem, 1)
            act.wait_ge(s_rate.sem, 2)
            count = [0]

            def link(i, ins):
                count[0] += 1
                ins.then_inc(act_step.sem, 1)
                act.wait_ge(act_step.sem, act_step.at(i, count[0]))

            def evacuate(i, name, dst, src, func=ACT.Copy, **kw):
                act.wait_ge(*full(i, name))
                act.activation(dst, src, func, **kw).then_inc(frees(name), 1)

            roots = [0]
            group_var = gmv[:, 5:6]

            def root(i, buf):
                if buf is group_var:
                    act.wait_ge(*read(i, "gv"))
                else:
                    roots[0] += 1
                    act.wait_ge(s_var.sem, s_var.at(i, roots[0]))
                link(i, act.activation(buf, buf, ACT.Ln))
                act.activation(buf, buf, ACT.Exp, scale=-0.5).then_inc(s_root.sem, 1)

            def load(i):
                act.preload_act_table_set("natural_log_exp_and_others")
                for b in range(2):
                    act.wait_ge(aux_free[b].sem, aux_free[b].at(i, 0))
                rows = a["x"][bass.ds(i, 1)].rearrange("o (k p) d -> p (o k) d", p=P)
                for c in range(NC):
                    act.dma_start(x_tok[:, TT * c:TT * c + TT, :], rows[:, TT * c:TT * c + TT, :]).then_inc(s_x.sem, 16)

            def store(i):
                for b in range(2):
                    act.wait_ge(aux_free[b].sem, aux_free[b].at(i, aux_per[b]))
                act.dma_start(a["out"][bass.ds(i, 1)].rearrange("o (k p) d -> p (o k) d", p=P), t1[:, :, :]).then_inc(s_out.sem, 16)

            def group_norm(i):
                load(i)
                for g in range(NC):
                    evacuate(i, f"xT{g}", gx[:, 1 + ROWS * g:1 + ROWS * g + ROWS, 1:1 + W],
                             aux(f"xT{g}")[:, 0:T].rearrange("p (r w) -> p r w", w=W))
                root(i, group_var)

            def copy_conv(i, c, hf):
                if c >= 3:
                    act.wait_ge(s_y.sem, s_y.at(i, 2 * (c - 3) + 2))
                act.wait_ge(s_conv.sem, s_conv.at(i, 2 * c + hf + 1))
                act.activation(xc[:, c % 3, hf, :], ps_conv[:, 0:T], ACT.Copy).then_inc(s_xc.sem, 1)

            def copy_C(i, c):
                if c >= 2:
                    act.wait_ge(s_prod.sem, s_prod.at(i, NB * (c - 1)))
                evacuate(i, f"C{c}", c_rep[:, c % 2, :], aux(f"C{c}")[:, 0:T])

            def copy_B(i, c):
                if c >= 1:
                    act.wait_ge(*read(i, f"dtN{c - 1}"))
                evacuate(i, f"B{c}", b_rep[:, :], aux(f"B{c}")[:, 0:T])

            def copy_dtr(i, c):
                evacuate(i, f"dtr{c}", dt_r[:, :], aux(f"dtr{c}")[0:RK, 0:T])

            def add_bias(i, c, hf):
                if c >= 1 and hf == 0:
                    act.wait_ge(s_rest.sem, s_rest.at(i, 2 * c))
                evacuate(i, f"dt{hf}{c}", dt[:, hf, :], aux(f"dt{hf}{c}")[:, 0:T], ACT.Identity, bias=b_dt[:, hf:hf + 1])

            def softplus(i, c, k):
                if k == 0:
                    if c >= 1:
                        act.wait_ge(s_sz.sem, s_sz.at(i, c))
                    for hf in range(HV):
                        act.wait_ge(*read(i, f"dt{hf}{c}"))
                    link(i, act.activation(dt_tmp[:, :, :], dt[:, :, :], ACT.Abs))
                elif k == 1:
                    link(i, act.activation(dt_tmp[:, :, :], dt_tmp[:, :, :], ACT.Exp, scale=-1.0))
                else:
                    act.activation(dt_tmp[:, :, :], dt_tmp[:, :, :], ACT.Ln, bias=1.0).then_inc(s_dtl.sem, 1)

            def copy_z(i, c, hf):
                if c >= 1 and hf == 0:
                    act.wait_ge(s_sz.sem, s_sz.at(i, c))
                evacuate(i, f"z{hf}{c}", zc[:, hf, :], aux(f"z{hf}{c}")[:, 0:T])

            def sigmoid(i, c, k):
                if k == 0:
                    act.wait_ge(s_dt.sem, s_dt.at(i, c + 1))
                    for hf in range(HV):
                        act.wait_ge(*read(i, f"z{hf}{c}"))
                    link(i, act.activation(z_tmp[:, :, :], zc[:, :, :], ACT.Abs))
                elif k == 1:
                    link(i, act.activation(z_tmp[:, :, :], z_tmp[:, :, :], ACT.Exp, scale=-1.0))
                elif k == 2:
                    act.activation(z_tmp[:, :, :], z_tmp[:, :, :], ACT.Ln, bias=1.0).then_inc(s_z.sem, 1)
                else:
                    act.wait_ge(s_zmin.sem, s_zmin.at(i, c + 1))
                    act.activation(z_tmp[:, :, :], z_tmp[:, :, :], ACT.Exp).then_inc(s_zexp.sem, 1)

            def first_part(i, c, k):
                if k:
                    act.wait_ge(s_dt.sem, s_dt.at(i, c + 1))
                    act.wait_ge(s_xstack.sem, s_xstack.at(i, c + 1))
                else:
                    act.wait_ge(s_xc.sem, s_xc.at(i, 2 * c + 2))
                    if c:
                        act.wait_ge(s_dtstack.sem, s_dtstack.at(i, c))
                src = dt if k else xc[:, c % 3]
                act.activation(parts[:, 0], src[:, :, :], ACT.Copy).then_inc(s_hi.sem, 1)

            def second_part(i, c, k):
                act.wait_ge(s_rest.sem, s_rest.at(i, 2 * c + k + 1))
                act.activation(parts[:, 1], rest[:, :, :], ACT.Copy).then_inc(s_mid.sem, 1)

            def square(i, c):
                act.wait_ge(*read(i, f"mean{c}"))
                act.activation(y_sq[:, :, :], y[:, :, :], ACT.Square).then_inc(s_ysq.sem, 1)

            def inverse_root(i, c, k):
                if k == 0:
                    evacuate(i, f"var{c}", y_rs[:, :], aux(f"var{c}")[:, 0:T], ACT.Ln, bias=eps_ln)
                else:
                    act.wait_ge(*read(i, f"var{c}"))
                    act.activation(y_rs[:, :], y_rs[:, :], ACT.Exp, scale=-0.5).then_inc(s_yrs.sem, 1)

            def affine(i, c):
                act.wait_ge(s_yn.sem, s_yn.at(i, c + 1))
                for hf in range(HV):
                    ins = act.activation(y[:, hf, :], y[:, hf, :], ACT.Identity, bias=ln_b[:, hf:hf + 1], scale=ln_g[:, hf:hf + 1])
                ins.then_inc(s_yaff.sem, 1)

            def project(i, c, n):
                if n == 2:
                    copy_C(i, c)
                if n == 3:
                    copy_B(i, c)
                if n == 4:
                    copy_dtr(i, c)
                if n == 5:
                    first_part(i, c, 0)
                if n in (6, 7):
                    add_bias(i, c, n - 6)
                if n == 8:
                    second_part(i, c, 0)
                if n in (8, 9, 10):
                    softplus(i, c, n - 8)
                if n in (9, 10):
                    copy_z(i, c, n - 9)
                if n == 13:
                    first_part(i, c, 1)
                if n in (13, 14, 15):
                    sigmoid(i, c, n - 13)
                if n == 16:
                    second_part(i, c, 1)
                if n == 18:
                    sigmoid(i, c, 3)

            def finish(i, c, n):
                if n == 9:
                    square(i, c)
                if n in (12, 13):
                    inverse_root(i, c, n - 12)
                if n == 16:
                    affine(i, c)

            def scan(i, c):
                for n in range(NB):
                    k = NB * c + n
                    act.wait_ge(s_dtrep.sem, s_dtrep.at(i, k + 1))
                    if k >= 2:
                        act.wait_ge(s_state.sem, s_state.at(i, k - 1))
                    act.activation(decay[:, n % 2, :], ps_dt[n % 2][:, 0:T], ACT.Exp, scale=decay_rate).then_inc(s_dtread.sem, 1)
                    if c + 1 < NC:
                        project(i, c + 1, n)
                    if c:
                        finish(i, c - 1, n)
                    if c + 2 < NC:
                        for hf in range(HV):
                            if n == CONV_AT[hf] + 9:
                                copy_conv(i, c + 2, hf)

            def normalise(i, k, src, dst):
                act.wait_ge(s_coef.sem, s_coef.at(i, k + 1))
                for g in range(NC):
                    for t in range(TT * g, TT * g + TT):
                        ins = act.activation(dst[:, t, :], src[:, t, :], ACT.Identity, bias=nb[:, t:t + 1], scale=r1[:, t:t + 1])
                    ins.then_inc(s_xn.sem, 1)

            def attention(i):
                root(i, r1[:, :])
                root(i, r2[:, :])
                normalise(i, 0, t1, big_u)
                for g in range(NC):
                    evacuate(i, f"xnT{g}", big_t[:, T * g:T * g + T], aux(f"xnT{g}")[:, 0:T])
                for g in range(NC):
                    evacuate(i, f"kT{g}", big_k[:, T * g:T * g + T], aux(f"kT{g}")[:, 0:T])
                for g in range(NT // 2):
                    evacuate(i, f"qv{g}", qv[:, :, 2 * g:2 * g + 2, :].rearrange("p w k d -> p k w d"),
                             aux(f"qv{g}")[:, :].rearrange("p (k w d) -> p k w d", k=2, w=2))
                for g in (NC - 2, NC - 1):
                    act.wait_ge(*read(i, f"kT{g}"))
                act.wait_ge(s_kmax.sem, s_kmax.at(i, 1))
                act.activation(big_k[:, :], big_k[:, :], ACT.Exp, bias=k_col[:, 0:1], accum_out=k_col[:, 1:2]).then_inc(s_kexp.sem, 1)
                act.wait_ge(s_qsub.sem, s_qsub.at(i, 1))
                act.activation(qv[:, 0], qv[:, 0], ACT.Exp).then_inc(s_qexp.sem, 1)
                for g in range(NC):
                    evacuate(i, f"ek{g}", big_u[:, TT * g:TT * g + TT, :].rearrange("p k d -> p (k d)"), aux(f"ek{g}")[:, 0:T])
                for g in range(NC):
                    evacuate(i, f"qT{g}", big_t[:, T * g:T * g + T], aux(f"qT{g}")[:, 0:T])
                for g in range(NC):
                    evacuate(i, f"ao{g}", big_k[:, T * g:T * g + T], aux(f"ao{g}")[:, 0:T])
                root(i, r1[:, :])
                ao = big_k[:, :].rearrange("p (k d) -> p k d", d=D)
                normalise(i, 1, ao, ao)
                root(i, r1[:, :])
                normalise(i, 2, t1, big_u)
                for g in range(NC):
                    evacuate(i, f"uT{g}", big_t[:, T * g:T * g + T], aux(f"uT{g}")[:, 0:T])
                act.wait_ge(s_top.sem, s_top.at(i, 1))
                act.activation(gw[:, 0, :], gw[:, 0, :], ACT.Exp).then_inc(s_topexp.sem, 1)

            def experts(i):
                for u in range(MO):
                    act.wait_ge(s_dtrep.sem, s_dtrep.at(i, SC + u + 1))
                    if u >= 2:
                        act.wait_ge(s_xread.sem, s_xread.at(i, SC + u - 1))
                    act.activation(silu[:, u % 2, :], ps_dt[u % 2][:, 0:T], ACT.Silu).then_inc(s_dtread.sem, 1)

            with act.Fori(0, B) as i:
                group_norm(i)
                for c in range(2):
                    for hf in range(HV):
                        copy_conv(i, c, hf)
                for n in range(NB):
                    project(i, 0, n)
                for c in range(NC):
                    scan(i, c)
                for n in range(NB):
                    finish(i, NC - 1, n)
                attention(i)
                experts(i)
                store(i)
            act.wait_ge(s_out.sem, 16 * (B + 1))
            assert count[0] == ACT_STEPS, count

        @block.vector
        def _(dve):
            dve.wait_ge(s_const.sem, n_const)
            for k, (dst, src) in enumerate(((w_b, w_xp[:, :, RK:RK + NS]), (w_c, w_xp[:, :, RK + NS:RK + 2 * NS]), (w_n, w_dtn[:, :, :]))):
                for hf in range(HV):
                    dve.tensor_copy(dst[:, hf, :].rearrange("p (n j) -> p n j", j=JB),
                                    src[:, hf, :].unsqueeze(2).broadcast_to([P, NS, JB])).then_inc(s_setup.sem, 1)
            taps = state[:, 0:6, :].rearrange("p s t -> p (s t)").rearrange("p (k d) -> p k d", d=DI)
            for tap in range(9):
                dve.tensor_tensor(w_conv[:, tap, :], y[:, 0, 0:DI], taps[:, tap, :], ALU.mult).then_inc(s_setup.sem, 1)
            dve.tensor_scalar(w_qkv[:, :], w_qkv[:, :], norm_gamma, None, ALU.mult).then_inc(s_setup.sem, 1)
            dve.tensor_copy(copy[:, :, :].rearrange("p (s b) m -> p s (b m)", s=2), prod[0:32 * PARTS, 0:2, 0:256]).then_inc(s_setup.sem, 1)
            dve.wait_ge(s_clear.sem, N_CLEAR)
            dve.wait_ge(s_setup.sem, N_SETUP)
            count = [0]

            def link(i, ins):
                count[0] += 1
                ins.then_inc(dve_step.sem, 1)
                dve.wait_ge(dve_step.sem, dve_step.at(i, count[0]))

            def group_norm(i):
                for g in range(NC):
                    dve.wait_ge(*read(i, f"xT{g}"))
                    ins = dve.bn_stats(gst[:, g, :], gx[:, 1 + ROWS * g:1 + ROWS * g + ROWS, 1:1 + W])
                    link(i, ins)
                part = gst[:, :, :].rearrange("p g (s k) -> p (g s) k", k=3)
                link(i, dve.tensor_reduce(gmv[:, 7:8], part[:, :, 1], AX.X, ALU.add))
                link(i, dve.tensor_scalar(gmv[:, 0:1], gmv[:, 7:8], 1.0 / (2 * NC), None, ALU.mult))
                link(i, dve.tensor_scalar(gdev[:, :], part[:, :, 1], gmv[:, 0:1], None, ALU.subtract))
                link(i, dve.tensor_tensor(gdev[:, :], gdev[:, :], gdev[:, :], ALU.mult))
                link(i, dve.tensor_scalar(gdev[:, :], gdev[:, :], L / (2.0 * NC), None, ALU.mult))
                link(i, dve.tensor_tensor(gdev[:, :], gdev[:, :], part[:, :, 2], ALU.add))
                link(i, dve.tensor_reduce(gmv[:, 7:8], gdev[:, :], AX.X, ALU.add))
                dve.tensor_scalar(gmv[:, 1:2], gmv[:, 7:8], 1.0 / L, None, ALU.mult).then_inc(s_gn.sem, 1)
                dve.wait_ge(s_gn.sem, s_gn.at(i, 1))
                dve.wait_ge(*full(i, "gm"))
                dve.tensor_copy(gmv[:, 4:5], aux("gm")[:, 0:1]).then_inc(frees("gm"), 1)
                dve.wait_ge(*read(i, "gm"))
                link(i, dve.tensor_tensor(gmv[:, 3:4], gmv[:, 0:1], gmv[:, 4:5], ALU.subtract))
                dve.scalar_tensor_tensor(out=gmv[:, 2:3], in0=gmv[:, 3:4], scalar=gmv[:, 3:4], in1=gmv[:, 1:2],
                                         op0=ALU.mult, op1=ALU.add).then_inc(s_gn.sem, 1)
                dve.wait_ge(*full(i, "gv"))
                dve.tensor_scalar(gmv[:, 5:6], aux("gv")[:, 0:1], 1e-5, None, ALU.add).then_inc(frees("gv"), 1)
                dve.wait_ge(s_root.sem, s_root.at(i, 1))
                link(i, dve.scalar_tensor_tensor(out=gmv[:, 6:7], in0=gmv[:, 4:5], scalar=-1.0, in1=gmv[:, 5:6],
                                                 op0=ALU.mult, op1=ALU.mult))
                inner = gx[:, 1:1 + H, 1:1 + W]
                dve.tensor_scalar(inner, inner, gmv[:, 5:6], gmv[:, 6:7], ALU.mult, ALU.add).then_inc(s_norm.sem, 1)

            def project(i, c, n):
                if n in (6, 14):
                    k = 0 if n == 6 else 1
                    src = dt if k else xc[:, c % 3]
                    dve.wait_ge(s_hi.sem, s_hi.at(i, 2 * c + k + 1))
                    dve.tensor_tensor(rest[:, :, :], src[:, :, :], parts[:, 0], ALU.subtract).then_inc(s_rest.sem, 1)
                if n in (10, 18):
                    k = 0 if n == 10 else 1
                    dve.wait_ge(s_mid.sem, s_mid.at(i, 2 * c + k + 1))
                    dve.tensor_tensor(parts[:, 2], rest[:, :, :], parts[:, 1], ALU.subtract).then_inc(s_lo.sem, 1)
                if n == 12:
                    dve.wait_ge(s_dtl.sem, s_dtl.at(i, c + 1))
                    dve.scalar_tensor_tensor(out=dt[:, :, :], in0=dt[:, :, :], scalar=0.0, in1=dt_tmp[:, :, :],
                                             op0=ALU.max, op1=ALU.add).then_inc(s_dt.sem, 1)
                if n == 15:
                    use = f"dtN{c}"
                    dve.wait_ge(*full(i, use))
                    for x in other_bank(use, f"B{c}"):
                        dve.wait_ge(*read(i, x))
                    dve.scalar_tensor_tensor(out=db_rep[:, c % 2, :], in0=aux(use)[:, 0:T], scalar=b_dtn, in1=b_rep[:, :],
                                             op0=ALU.add, op1=ALU.mult).then_inc(frees(use), 1)
                if n == 16:
                    dve.wait_ge(s_z.sem, s_z.at(i, c + 1))
                    dve.scalar_tensor_tensor(out=z_tmp[:, :, :], in0=zc[:, :, :], scalar=0.0, in1=z_tmp[:, :, :],
                                             op0=ALU.min, op1=ALU.subtract).then_inc(s_zmin.sem, 1)
                if n == 19:
                    dve.wait_ge(s_zexp.sem, s_zexp.at(i, c + 1))
                    dve.tensor_tensor(sz[:, c % 2], zc[:, :, :], z_tmp[:, :, :], ALU.mult).then_inc(s_sz.sem, 1)

            def skip(i, c, hf):
                dve.wait_ge(s_fold.sem, s_fold.at(i, NB // QD * c + 4 * (hf + 1)))
                dve.scalar_tensor_tensor(out=y[:, hf, :], in0=xc[:, c % 3, hf, :], scalar=d_skip[:, hf:hf + 1], in1=ps_y[:, 0:T],
                                         op0=ALU.mult, op1=ALU.add).then_inc(s_y.sem, 1)

            def finish(i, c, n):
                both = lambda v: v.unsqueeze(1).broadcast_to([P, HV, T])
                if n == 5:
                    skip(i, c, 1)
                if n == 8:
                    use = f"mean{c}"
                    dve.wait_ge(*full(i, use))
                    dve.wait_ge(s_y.sem, s_y.at(i, 2 * c + 2))
                    dve.tensor_tensor(y[:, :, :], y[:, :, :], both(aux(use)[:, 0:T]), ALU.subtract).then_inc(frees(use), 1)
                if n == 15:
                    dve.wait_ge(s_yrs.sem, s_yrs.at(i, c + 1))
                    dve.wait_ge(*read(i, f"mean{c}"))
                    dve.tensor_tensor(y[:, :, :], y[:, :, :], both(y_rs[:, :]), ALU.mult).then_inc(s_yn.sem, 1)
                if n == 17:
                    dve.wait_ge(s_yaff.sem, s_yaff.at(i, c + 1))
                    dve.tensor_tensor(y[:, :, :], y[:, :, :], sz[:, c % 2], ALU.mult).then_inc(s_yg.sem, 1)
                if n == 20:
                    use = f"out{c}"
                    dve.wait_ge(*full(i, use))
                    if c == 0:
                        dve.wait_ge(s_out.sem, s_out.at(i, 0))
                    tok = slice(TT * c, TT * c + TT)
                    dve.tensor_tensor(t1[:, tok, :].rearrange("p k d -> p (k d)"), aux(use)[:, 0:T],
                                      x_tok[:, tok, :].rearrange("p k d -> p (k d)"), ALU.add).then_inc(frees(use), 1)

            def inflows(i, c, n):
                k = NB * c + n
                dve.wait_ge(s_xrep.sem, s_xrep.at(i, k + 1))
                if k >= 2:
                    dve.wait_ge(s_state.sem, s_state.at(i, k - 1))
                dve.tensor_tensor(inflow[:, n % 2, :], ps_x[n % 2][:, 0:T], db_rep[:, c % 2, :], ALU.mult).then_inc(s_xread.sem, 1)

            def scan(i, c):
                if c == 0:
                    dve.wait_ge(*read(i, f"dtN{c}"))
                    inflows(i, c, 0)
                for n in range(NB):
                    k = NB * c + n
                    if n + 1 < NB:
                        inflows(i, c, n + 1)
                    elif c + 1 < NC:
                        dve.wait_ge(*read(i, f"dtN{c + 1}"))
                        inflows(i, c + 1, 0)
                    dve.wait_ge(s_xread.sem, s_xread.at(i, k + 1))
                    dve.wait_ge(s_dtread.sem, s_dtread.at(i, k + 1))
                    if k >= HS:
                        dve.wait_ge(s_prod.sem, s_prod.at(i, k - HS + 1))
                    init = carry[:, n:n + 1] if c else 0.0
                    dve.tensor_tensor_scan(state[:, n % HS, :], decay[:, n % 2, :], inflow[:, n % 2, :], init,
                                           ALU.mult, ALU.add).then_inc(s_state.sem, 1)
                    if n % QD == QD - 1:
                        dve.wait_ge(s_state.sem, s_state.at(i, k + 1))
                        s0 = n % HS - QD + 1
                        link(i, dve.tensor_copy(carry[:, n - QD + 1:n + 1], state[:, s0:s0 + QD, T - 1]))
                    if c + 1 < NC:
                        project(i, c + 1, n)
                    if c:
                        finish(i, c - 1, n)
                    if n == 22:
                        skip(i, c, 0)

            roots = [1]

            def attention_start(i):
                dve.wait_ge(*read(i, f"out{NC - 2}"))
                dve.wait_ge(*read(i, f"out{NC - 1}"))

            def stats(i, k, src, twice=False):
                for t in range(NT):
                    ins = dve.bn_stats(st[:, t, :], src[:, t, :])
                link(i, ins)
                link(i, dve.tensor_tensor(mv[:, :, 0], st[:, :, 1], st[:, :, 4], ALU.subtract))
                link(i, dve.tensor_tensor(mv[:, :, 0], mv[:, :, 0], mv[:, :, 0], ALU.mult))
                link(i, dve.tensor_tensor(mv[:, :, 1], st[:, :, 2], st[:, :, 5], ALU.add))
                link(i, dve.scalar_tensor_tensor(out=mv[:, :, 1], in0=mv[:, :, 0], scalar=D / 4.0, in1=mv[:, :, 1], op0=ALU.mult, op1=ALU.add))
                link(i, dve.tensor_scalar(mv[:, :, 1], mv[:, :, 1], 1.0 / D, None, ALU.mult))
                link(i, dve.tensor_tensor(mv[:, :, 0], st[:, :, 1], st[:, :, 4], ALU.add))
                link(i, dve.tensor_scalar(mv[:, :, 0], mv[:, :, 0], 0.5, None, ALU.mult))
                dve.tensor_scalar(r1[:, :], mv[:, :, 1], 1e-5, None, ALU.add).then_inc(s_var.sem, 1)
                roots[0] += 1
                dve.wait_ge(s_root.sem, s_root.at(i, roots[0]))
                if twice:
                    link(i, dve.tensor_tensor(r2[:, :], mv[:, :, 1], r1[:, :], ALU.mult))
                    link(i, dve.tensor_tensor(r2[:, :], r2[:, :], r1[:, :], ALU.mult))
                    dve.tensor_scalar(r2[:, :], r2[:, :], 1e-5, None, ALU.add).then_inc(s_var.sem, 1)
                    roots[0] += 1
                    dve.wait_ge(s_root.sem, s_root.at(i, roots[0]))
                    link(i, dve.tensor_tensor(r1[:, :], r1[:, :], r2[:, :], ALU.mult))
                dve.scalar_tensor_tensor(out=nb[:, :], in0=mv[:, :, 0], scalar=-1.0, in1=r1[:, :],
                                         op0=ALU.mult, op1=ALU.mult).then_inc(s_coef.sem, 1)

            def attention(i):
                attention_start(i)
                stats(i, 0, t1, twice=True)
                q = qv[:, 0].rearrange("p k (h d) -> p (k h) d", d=DH)
                for g in (NC - 2, NC - 1):
                    dve.wait_ge(*read(i, f"kT{g}"))
                link(i, dve.tensor_reduce(k_col[:, 2:3], big_k[:, :], AX.X, ALU.max))
                dve.tensor_scalar(k_col[:, 0:1], k_col[:, 2:3], -1.0, None, ALU.mult).then_inc(s_kmax.sem, 1)
                for g in (NT // 2 - 2, NT // 2 - 1):
                    dve.wait_ge(*read(i, f"qv{g}"))
                link(i, dve.tensor_reduce(q_max[:, :], q, AX.X, ALU.max))
                dve.tensor_tensor(q, q, q_max[:, :].unsqueeze(2).broadcast_to([P, NT * NH, DH]), ALU.subtract).then_inc(s_qsub.sem, 1)
                dve.wait_ge(s_kexp.sem, s_kexp.at(i, 1))
                link(i, dve.reciprocal(k_col[:, 3:4], k_col[:, 1:2]))
                dve.wait_ge(s_qexp.sem, s_qexp.at(i, 1))
                link(i, dve.tensor_reduce(q_sum[:, :], q, AX.X, ALU.add))
                link(i, dve.reciprocal(q_max[:, :], q_sum[:, :]))
                dve.tensor_tensor(q, q, q_max[:, :].unsqueeze(2).broadcast_to([P, NT * NH, DH]), ALU.mult).then_inc(s_q.sem, 1)
                dve.wait_ge(*full(i, "ctx"))
                dve.tensor_tensor(ctx_t[:, :], aux("ctx")[:, 0:D], heads[:, :], ALU.mult).then_inc(frees("ctx"), 1)
                dve.wait_ge(*full(i, "ctx2"))
                dve.tensor_scalar(ctx_o[:, :], aux("ctx2")[:, 0:D], k_col[:, 3:4], DH ** -0.5, ALU.mult, ALU.mult).then_inc(frees("ctx2"), 1)
                for g in (NC - 2, NC - 1):
                    dve.wait_ge(*read(i, f"ao{g}"))
                ao = big_k[:, :].rearrange("p (k d) -> p k d", d=D)
                stats(i, 1, ao)
                dve.wait_ge(s_xn.sem, s_xn.at(i, 2 * NC))
                link(i, dve.tensor_tensor(ao, ao, out_gamma[:, :].unsqueeze(1).broadcast_to([P, NT, D]), ALU.mult))
                link(i, dve.tensor_tensor(t1[:, :, :], t1[:, :, :], ao, ALU.add))
                stats(i, 2, t1)
                dve.wait_ge(*full(i, "logit"))
                dve.tensor_copy(logit[:, :, :].rearrange("p k e -> p (k e)"), aux("logit")[:, 0:NT * NE])
                for t in range(NT):
                    ins = dve.max(top[:, t, :], aux("logit")[:, NE * t:NE * t + NE])
                ins.then_inc(frees("logit"), 1)
                dve.wait_ge(*read(i, "logit"))
                dve.tensor_tensor(gw[:, 0, :], top[:, :, 1], top[:, :, 0], ALU.subtract).then_inc(s_top.sem, 1)
                for t in range(NT):
                    ins = dve.max_index(where[:, t, :], top[:, t, :], logit[:, t, :])
                link(i, ins)
                link(i, dve.tensor_copy(place[:, :, :], where[:, :, :]))
                dve.wait_ge(s_topexp.sem, s_topexp.at(i, 1))
                link(i, dve.tensor_scalar(gw[:, 1, :], gw[:, 0, :], 1.0, None, ALU.add))
                link(i, dve.reciprocal(gw[:, 2, :], gw[:, 1, :]))
                link(i, dve.tensor_tensor(gw[:, 3, :], gw[:, 2, :], gw[:, 0, :], ALU.mult))
                for k, dst in enumerate((gate, pick)):
                    link(i, dve.tensor_tensor(dst[:, :, :], place[:, :, k:k + 1].broadcast_to([P, NT, NE]),
                                              iota[:, :].unsqueeze(1).broadcast_to([P, NT, NE]), ALU.is_equal))
                    link(i, dve.tensor_tensor(dst[:, :, :], dst[:, :, :], gw[:, 2 + k, :].unsqueeze(2).broadcast_to([P, NT, NE]), ALU.mult))
                link(i, dve.tensor_tensor(gate[:, :, :], gate[:, :, :], pick[:, :, :], ALU.add))

            def experts(i):
                def add(e, g):
                    name = f"moe{e}_{g}"
                    dve.wait_ge(*full(i, name))
                    if e:
                        dve.wait_ge(*read(i, f"moe{e - 1}_{g}"))
                    for k in range(TT):
                        t = TT * g + k
                        ins = dve.scalar_tensor_tensor(out=t1[:, t, :], in0=aux(name)[:, P * k:P * k + P], scalar=gate[:, t, e:e + 1],
                                                       in1=t1[:, t, :], op0=ALU.mult, op1=ALU.add)
                    ins.then_inc(frees(name), 1)

                last = None
                u = 0
                for e in range(NE):
                    for g in range(NC):
                        for m in range(MF):
                            dve.wait_ge(s_xrep.sem, s_xrep.at(i, SC + u + 1))
                            dve.wait_ge(s_dtread.sem, s_dtread.at(i, SC + u + 1))
                            dve.scalar_tensor_tensor(out=hidden[:, u % 6, :], in0=ps_x[u % 2][:, 0:T], scalar=b3[:, e, m:m + 1],
                                                     in1=silu[:, u % 2, :], op0=ALU.add, op1=ALU.mult).then_inc(s_xread.sem, 1)
                            u += 1
                        if last:
                            add(*last)
                        last = (e, g)
                add(*last)

            with dve.Fori(0, B) as i:
                group_norm(i)
                for n in range(NB):
                    project(i, 0, n)
                for c in range(NC):
                    scan(i, c)
                for n in range(NB):
                    finish(i, NC - 1, n)
                attention(i)
                experts(i)
            assert count[0] == DVE_STEPS, count


_ORDER = ["x", "w_in", "conv_k", "w_xp", "w_dt", "w_dtn", "w_out", "b_out", "vecs", "norm_gamma", "w_qkv", "w_proj",
          "out_gamma", "w_gate", "w1", "w2", "w3", "b3", "eye", "group", "heads", "mean", "iota", "copy", "fold"]


def kernel(**v):
    import numpy as _np
    import concourse.bacc as _bacc
    from concourse import mybir as _mybir
    from concourse.bass_utils import run_bass_kernel_spmd as _run

    v = {k: _np.asarray(x) for k, x in v.items()}
    s, t, f = "L0_conv_", "L1_attn_", "L1_ffn_"
    halves = lambda x: x.reshape(HV, P).T
    states = lambda x: _np.repeat(x, JB).reshape(P, 1)
    arrays = {
        "x": v["x"].reshape(B, L, D), "w_in": v[s + "W_in"], "conv_k": v[s + "conv_k"].reshape(1, 9 * DI),
        "w_xp": v[s + "W_xproj"], "w_dt": v[s + "W_dt"], "w_dtn": v[s + "W_dtN"], "w_out": v[s + "W_out"],
        "b_out": v[s + "b_out"].reshape(1, D),
        "vecs": _np.concatenate([halves(v[s + "b_dt"]), halves(v[s + "Dskip"]), halves(v[s + "ln_g"]), halves(v[s + "ln_b"]),
                                 states(v[s + "b_dtN"]), states(v[s + "A_log"])], axis=1),
        "norm_gamma": v[t + "norm_gamma"].reshape(P, 1), "w_qkv": v[t + "w_qkv"].T, "w_proj": v[t + "w_out"].T,
        "out_gamma": v[t + "out_gamma"].reshape(1, D), "w_gate": v[f + "Wg"],
        "w1": v[f + "W1"], "w2": v[f + "W2"], "w3": v[f + "W3"],
        "b3": v[f + "b3"].reshape(NE, MF, P).transpose(2, 0, 1),
        **constants(),
    }
    nc = _bacc.Bacc("TRN2", target_bir_lowering=False, num_devices=1, dynamic_dma_scratch_size=4096)
    given, aps = {}, {}
    for name in _ORDER:
        x = _np.ascontiguousarray(arrays[name])
        given[f"in_{name}"] = x
        aps[name] = nc.dram_tensor(f"in_{name}", x.shape, _mybir.dt.from_np(x.dtype), kind="ExternalInput").ap()
    aps["out"] = nc.dram_tensor("out_0", (B, L, D), F32, kind="ExternalOutput").ap()
    build(nc, aps)
    r = _run(nc, [given], core_ids=[0])
    return r.results[0]["out_0"].reshape(B, H, W, D)
```

```python
from contextlib import ExitStack

import numpy as np

import concourse.bass as bass
from concourse import mybir

ALU = mybir.AluOpType
ACT = mybir.ActivationFunctionType
AX = mybir.AxisListType
F32 = mybir.dt.float32
BF16 = mybir.dt.bfloat16
U32 = mybir.dt.uint32

P = 128
B, H, W, D = 8, 48, 48, 128
L = H * W
DI, NS, RK = 256, 16, 8
HV = DI // P
T = 384
ROWS = T // W
NC = L // T
TT = T // P
NT = L // P
JB = P // NS
NB = DI // JB
QD = 4
NH, DH = 8, 16
NE, F = 8, 384
MF = F // P
PARTS = 3
N_CLEAR, N_SETUP = 3, 17
ACT_STEPS, DVE_STEPS = (13,4), (63,45)
BESIDE = (("dtr", 0, 1), ("dt0", 2, 1), ("dt1", 4, 1), ("mean", 7, -1), ("var", 10, -1), ("B", 12, 1), ("dtN", 14, 1),
          ("C", 16, 1), ("out", 18, -1), ("z0", 20, 1), ("z1", 24, 1))
CONV_AT = (1, 12)
FOLD_LAG = 3
GROUP = 4
HS = 8


def constants():
    eye = np.eye(P, dtype=np.float32)
    idx = np.arange(P)
    group = (idx[:, None] // 4 == idx[None, :] // 4).astype(np.float32) / 4
    heads = (idx[:, None] // DH == idx[None, :] // DH).astype(np.float32)
    mean = np.full((P, P), 1.0 / DI, np.float32)
    r = np.arange(32 * PARTS) % 32
    copy = np.stack([(r[:, None] == JB * b + idx[None, :] % JB) for b in range(4)], 1)
    fold = np.stack([(JB * b + idx[:, None] % JB == np.arange(32)[None, :]) for b in range(4)], 1)
    iota = np.broadcast_to(np.arange(NE, dtype=np.float32), (P, NE))
    return {
        "eye": eye, "group": group, "heads": heads, "mean": mean, "iota": np.ascontiguousarray(iota),
        "copy": np.ascontiguousarray(copy.astype(np.float32)), "fold": np.ascontiguousarray(fold.astype(np.float32)),
    }


def build(nc, a):
    with ExitStack() as ctx:
        def sb(name, shape, dt=F32):
            return ctx.enter_context(nc.sbuf_tensor(name, shape, dt))

        def psum(name):
            return ctx.enter_context(nc.psum_tensor(name, [P, 512], F32))

        eye, group, heads, mean = (sb(n, [P, P]) for n in ("eye", "group", "heads", "mean"))
        iota = sb("iota", [P, NE])
        fold = sb("fold", [P, 4, 32])
        copy = sb("copy", [32 * PARTS, 4, P], BF16)
        w_conv = sb("w_conv", [P, 9, DI])
        w_z = sb("w_z", [P, DI])
        w_xp = sb("w_xp", [P, HV, RK + 2 * NS])
        w_b, w_c, w_n = (sb(n, [P, HV, P]) for n in ("w_b", "w_c", "w_n"))
        w_dtn = sb("w_dtn", [P, HV, NS])
        w_dt = sb("w_dt", [RK, DI])
        w_out = sb("w_out", [P, HV, D])
        b_out, ones = sb("b_out", [1, D]), sb("ones", [1, P])
        vecs = sb("vecs", [P, 16])
        w_qkv = sb("w_qkv", [P, 3 * D])
        w_proj = sb("w_proj", [P, D])
        out_gamma = sb("out_gamma", [P, D])
        w_gate = sb("w_gate", [P, NE])
        b3 = sb("b3", [P, NE, MF])
        w1, w3, w2 = (sb(n, [P, 2, F]) for n in ("w1", "w3", "w2"))
        b_dt, d_skip, ln_g, ln_b = (vecs[:, 2 * k:2 * k + 2] for k in range(4))
        b_dtn, decay_rate, eps_ln, norm_gamma = (vecs[:, k:k + 1] for k in (8, 9, 10, 11))
        x_tok = sb("x_tok", [P, NT, D])
        gx = sb("gx", [P, H + 2, W + 2])
        t1 = sb("t1", [P, NT, D])
        big_t = sb("big_t", [P, L])
        big_k = sb("big_k", [P, L])
        big_u = sb("big_u", [P, NT, D])
        qv = sb("qv", [P, 2, NT, D])
        xc = sb("xc", [P, 3, HV, T])
        z_tmp = sb("z_tmp", [P, HV, T])
        sz = sb("sz", [P, 2, HV, T])
        dt = sb("dt", [P, HV, T])
        dt_tmp = sb("dt_tmp", [P, HV, T])
        dt_r = sb("dt_r", [RK, T])
        parts = sb("parts", [P, PARTS, HV, T], BF16)
        rest = sb("rest", [P, HV, T])
        x_stack = sb("x_stack", [32 * PARTS, 2, HV * QD, T], BF16)
        dt_stack = sb("dt_stack", [32 * PARTS, 2, HV * QD, T], BF16)
        b_rep = sb("b_rep", [P, T])
        db_rep = sb("db_rep", [P, 2, T])
        c_rep = sb("c_rep", [P, 2, T])
        decay = sb("decay", [P, 2, T])
        inflow = sb("inflow", [P, 2, T])
        state = sb("state", [P, HS, T])
        carry = sb("carry", [P, NB])
        prod = sb("prod", [P, HS, T])
        y = sb("y", [P, HV, T])
        y_sq = sb("y_sq", [P, HV, T])
        y_rs = sb("y_rs", [P, T])
        gst = sb("gst", [P, NC, 6])
        gmv = sb("gmv", [P, 8])
        gdev = sb("gdev", [P, 2 * NC])
        st = sb("st", [P, NT, 6])
        mv = sb("mv", [P, NT, 2])
        r1, r2, nb = (sb(n, [P, NT]) for n in ("r1", "r2", "nb"))
        q_max, q_sum = sb("q_max", [P, NT * NH]), sb("q_sum", [P, NT * NH])
        k_col = sb("k_col", [P, 4])
        ctx_t, ctx_o = sb("ctx_t", [P, D]), sb("ctx_o", [P, D])
        logit, top, gate, pick = (sb(n, [P, NT, NE]) for n in ("logit", "top", "gate", "pick"))
        where = sb("where", [P, NT, NE], U32)
        place = sb("place", [P, NT, NE])
        gw = sb("gw", [P, 4, NT])

        ps_dt, ps_x, ps_y, ps_conv = (psum(n) for n in ("ps_dt", "ps_x", "ps_y", "ps_conv"))
        ps_main, ps_h, ps_g, ps_sum = (psum(n) for n in ("ps_main", "ps_h", "ps_g", "ps_sum"))

        class Next:

            def __init__(self, j):
                self.j = j

        class Sem:

            def __init__(self, name, per, unit=1, first=0):
                self.sem = ctx.enter_context(nc.semaphore(name))
                self.per, self.unit, self.first = per, unit, first

            def at(self, i, k):
                if isinstance(i, Next):
                    return i.j * (self.per * self.unit) + (self.first + (self.per + k) * self.unit)
                return i * (self.per * self.unit) + (self.first + k * self.unit)

        banks = [ps_main, ps_h, ps_g, ps_sum]
        MAIN, HB, GB, SB = range(4)
        scan_uses = [f"xT{g}" for g in range(NC)] + ["gm", "gv"]
        scan_uses += [f"{name}0" for name, n, dc in BESIDE if dc == 1]
        for c in range(NC):
            scan_uses += [f"{name}{c + dc}" for name, n, dc in BESIDE if 0 <= c + dc < NC]
        scan_uses += [f"{name}{NC - 1}" for name, n, dc in BESIDE if dc == -1]
        attn_uses = [f"xnT{g}" for g in range(NC)] + [f"kT{g}" for g in range(NC)] + [f"qv{g}" for g in range(NT // 2)]
        attn_uses += [f"ek{g}" for g in range(NC)] + ["ctx", "ctx2"] + [f"qT{g}" for g in range(NC)]
        attn_uses += [f"ao{g}" for g in range(NC)] + [f"uT{g}" for g in range(NC)] + ["logit"]
        MO = NE * NC * MF
        placed = [(name, MAIN) for name in scan_uses]
        placed += [(name, (HB, GB, SB)[n % 3]) for n, name in enumerate(attn_uses)]
        for u in range(MO):
            placed += [(f"h{u}", HB), (f"g{u}", GB)]
        placed += [(f"moe{g}", SB) for g in range(NE * NC)]
        aux_of = {}
        aux_per = [0] * 4
        for name, b in placed:
            aux_of[name] = (b, aux_per[b])
            aux_per[b] += 1
        bank_names = ("main", "h", "g", "sum")
        aux_full = [Sem(f"{bank_names[b]}_full", aux_per[b]) for b in range(4)]
        aux_free = [Sem(f"{bank_names[b]}_free", aux_per[b], first=1) for b in range(4)]

        def aux(name):
            return banks[aux_of[name][0]]

        def free(i, name):
            b, k = aux_of[name]
            return aux_free[b].sem, aux_free[b].at(i, k)

        def full(i, name):
            b, k = aux_of[name]
            return aux_full[b].sem, aux_full[b].at(i, k + 1)

        def read(i, name):
            b, k = aux_of[name]
            return aux_free[b].sem, aux_free[b].at(i, k + 1)

        def fills(name):
            return aux_full[aux_of[name][0]].sem

        def frees(name):
            return aux_free[aux_of[name][0]].sem

        def other_bank(name, *inputs):
            last = {}
            for x in inputs:
                b, k = aux_of[x]
                if b != aux_of[name][0] and (b not in last or k > aux_of[last[b]][1]):
                    last[b] = x
            return list(last.values())

        SC = NB * NC
        s_const = Sem("s_const", 0)
        s_half = Sem("s_half", 0)
        s_clear, s_setup, s_rate = Sem("s_clear", 0), Sem("s_setup", 0), Sem("s_rate", 0)
        s_x = Sem("s_x", 1, 16 * NC)
        s_norm = Sem("s_norm", 1)
        s_tanh = Sem("s_tanh", 2 * NC)
        s_dtl = Sem("s_dtl", NC)
        s_dt = Sem("s_dt", NC)
        s_hi, s_rest, s_mid, s_lo = (Sem(n, 2 * NC) for n in ("s_hi", "s_rest", "s_mid", "s_lo"))
        s_xstack = Sem("s_xstack", NC, 16 * PARTS * QD)
        s_dtstack = Sem("s_dtstack", NC, 16 * PARTS * QD)
        s_dtrep = Sem("s_dtrep", SC)
        s_dtread = Sem("s_dtread", SC, first=1)
        s_xrep = Sem("s_xrep", SC)
        s_xread = Sem("s_xread", SC, first=1)
        s_state = Sem("s_state", SC)
        s_prod = Sem("s_prod", SC)
        s_fold = Sem("s_fold", SC // QD)
        s_y = Sem("s_y", 2 * NC)
        s_ysq = Sem("s_ysq", NC)
        s_yrs = Sem("s_yrs", NC)
        s_yn = Sem("s_yn", NC)
        s_yaff = Sem("s_yaff", NC)
        s_yg = Sem("s_yg", NC)
        s_conv = Sem("s_conv", 2 * NC)
        s_xc = Sem("s_xc", 2 * NC, first=1)
        s_gn = Sem("s_gn", 2)
        s_var = Sem("s_var", 4)
        s_root = Sem("s_root", 4)
        s_groot = Sem("s_groot", 1)
        s_htanh = Sem("s_htanh", MO)
        s_gated = Sem("s_gated", MO)
        s_coef = Sem("s_coef", 3)
        s_xn = Sem("s_xn", 3 * NC)
        s_qsub = Sem("s_qsub", 1)
        s_qexp = Sem("s_qexp", 1)
        s_q = Sem("s_q", 1)
        s_top, s_topexp = Sem("s_top", 1), Sem("s_topexp", 1)
        act_step, act_post = Sem("act_step", ACT_STEPS[0]), Sem("act_post", ACT_STEPS[1])
        dve_step, dve_post = Sem("dve_step", DVE_STEPS[0]), Sem("dve_post", DVE_STEPS[1])
        s_kmax = Sem("s_kmax", 1)
        s_kexp = Sem("s_kexp", 1)
        s_w = [Sem(f"s_w{b}", NE // 2, 48) for b in range(2)]
        s_out = Sem("s_out", 1, 16, first=16)

        acc = qv[:, 0]
        hidden = qv[:, 1].rearrange("p k d -> p (k d)").rearrange("p (s t) -> p s t", t=T)
        silu = big_k[:, :].rearrange("p (s t) -> p s t", t=T)
        HID = L // T

        SLOTS = SC + GROUP + 1
        assert GROUP * NE * NC == SC

        def unit_at(k):
            return MF * (k // GROUP) + k % GROUP if k < SC and k % GROUP < MF else None

        def sums_at(k):
            return k // GROUP - 1 if k % GROUP == GROUP - 1 and k >= GROUP else None

        def add_at(k):
            return k // GROUP - 2 if k % GROUP == 0 and k >= 2 * GROUP else None

        block = ctx.enter_context(nc.Block())
        n_const = 0

        @block.sync
        def _(sp):
            nonlocal n_const
            loads = [
                (eye[:, :], a["eye"]), (group[:, :], a["group"]), (heads[:, :], a["heads"]), (mean[:, :], a["mean"]),
                (iota[:, :], a["iota"]), (fold[:, :, :], a["fold"]),
                (prod[0:32 * PARTS, 0:2, 0:256].rearrange("p s t -> p s t"),
                 a["copy"].rearrange("p (s b) m -> p s (b m)", s=2)),
                (y[:, 0, 0:DI], a["w_in"][:, 0:DI]), (w_z[:, :], a["w_in"][:, DI:2 * DI]),
                (state[:, 0:6, :].rearrange("p s t -> p (s t)"), a["conv_k"].broadcast_to([P, 9 * DI])),
                (w_xp[:, :, :], a["w_xp"].rearrange("(h p) n -> p h n", p=P)),
                (w_dtn[:, :, :], a["w_dtn"].rearrange("(h p) n -> p h n", p=P)),
                (w_dt[:, :], a["w_dt"]),
                (w_out[:, :, :], a["w_out"].rearrange("(h p) n -> p h n", p=P)),
                (b_out[:, :], a["b_out"]), (vecs[:, 0:10], a["vecs"]), (vecs[:, 11:12], a["norm_gamma"]),
                (w_qkv[:, :], a["w_qkv"]), (w_proj[:, :], a["w_proj"]), (out_gamma[:, :], a["out_gamma"].broadcast_to([P, D])),
                (w_gate[:, :], a["w_gate"]), (b3[:, :, :], a["b3"]),
            ]
            for dst, src in loads:
                sp.dma_start(dst, src).then_inc(s_const.sem, 16)
            n_const = 16 * len(loads)

            def stack(i, c, k):
                s_full, dst_of = ((s_xstack, x_stack), (s_dtstack, dt_stack))[k]
                sp.wait_ge(s_lo.sem, s_lo.at(i, 2 * c + k + 1))
                for part in range(PARTS):
                    for q in range(QD):
                        dst = dst_of[32 * part:32 * part + 32, c % 2].rearrange("p (h q) t -> p h q t", q=QD)[:, :, q, :]
                        sp.dma_start(dst, parts[32 * q:32 * q + 32, part]).then_inc(s_full.sem, 16)

            def weights(j, e):
                if e < 2:
                    sp.wait_ge(aux_free[SB].sem, aux_free[SB].at(j, 0))
                else:
                    sp.wait_ge(*read(j, f"moe{NC * (e - 1) - 1}"))
                for dst, src in ((w1, a["w1"]), (w3, a["w3"])):
                    sp.dma_start(dst[:, e % 2, :], src[e]).then_inc(s_w[e % 2].sem, 16)
                sp.dma_start(w2[:, e % 2, :].rearrange("p (m d) -> p m d", m=MF),
                             a["w2"][e].rearrange("(m p) d -> p m d", p=P)).then_inc(s_w[e % 2].sem, 16)

            def image(i, j):
                for k in range(-NB, SC):
                    c, n = k // NB + 1, k % NB
                    if j is not None and k == -NB:
                        weights(j, 0)
                        weights(j, 1)
                    if i is not None and c < NC and n in (6, 17):
                        stack(i, c, 0 if n == 6 else 1)
                    if j is not None and k >= SC // NE and k % (SC // NE) == 6 and k // (SC // NE) + 1 < NE:
                        weights(j, k // (SC // NE) + 1)

            image(0, None)
            with sp.Fori(0, B - 1) as j:
                image(Next(j), j)
            image(None, B - 1)

        @block.gpsimd
        def _(pool):
            pool.memset(gx[:, :, :], 0.0).then_inc(s_clear.sem, 1)
            pool.memset(ones[:, :], 1.0).then_inc(s_clear.sem, 1)
            pool.memset(eps_ln, 1e-5).then_inc(s_clear.sem, 1)
            pool.wait_ge(s_clear.sem, N_CLEAR)
            def products(i):
                for c in range(NC):
                    pool.wait_ge(*read(i, f"C{c}"))
                    for n in range(NB):
                        k = NB * c + n
                        pool.wait_ge(s_state.sem, s_state.at(i, k + 1))
                        if k >= HS:
                            pool.wait_ge(s_fold.sem, s_fold.at(i, (k - HS) // QD + 1))
                        pool.tensor_tensor(prod[:, n % HS, :], state[:, n % HS, :], c_rep[:, c % 2, :], ALU.mult).then_inc(s_prod.sem, 1)

            products(0)
            with pool.Fori(0, B - 1) as j:
                products(Next(j))

        @block.tensor
        def _(pe):
            pe.wait_ge(s_const.sem, n_const)
            pe.wait_ge(s_clear.sem, N_CLEAR)
            pe.wait_ge(s_setup.sem, N_SETUP)

            def transposes(i, names, src):
                for g, name in enumerate(names):
                    pe.wait_ge(*free(i, name))
                    for k in range(TT):
                        ins = pe.transpose(aux(name)[:, P * k:P * k + P], src(TT * g + k), eye[:, :])
                    ins.then_inc(fills(name), 1)

            def turn(i):
                pe.wait_ge(s_x.sem, s_x.at(i, 1))
                transposes(i, [f"xT{g}" for g in range(NC)], lambda k: x_tok[:, k, :])

            def group_norm(i):
                for k, name in enumerate(("gm", "gv")):
                    pe.wait_ge(*free(i, name))
                    pe.wait_ge(s_gn.sem, s_gn.at(i, k + 1))
                    pe.matmul(aux(name)[:, 0:1], group[:, :], gmv[:, 2 * k:2 * k + 1], start=True, stop=True).then_inc(fills(name), 1)

            def halves(i, name, lhs, rhs, rows=P, inputs=()):
                pe.wait_ge(*free(i, name))
                for x in other_bank(name, *inputs):
                    pe.wait_ge(*read(i, x))
                for hf in range(HV):
                    ins = pe.matmul(aux(name)[0:rows, 0:T], lhs[:, hf, :], rhs[:, hf, :], start=hf == 0, stop=hf == HV - 1)
                ins.then_inc(fills(name), 1)

            def conv(i, c, hf, tap):
                if tap == 0:
                    pe.wait_ge(s_xc.sem, s_xc.at(i, 2 * c + hf))
                dy, dx = tap // 3, tap % 3
                ins = pe.matmul(ps_conv[:, 0:T], w_conv[:, tap, P * hf:P * hf + P],
                                gx[:, ROWS * c + dy:ROWS * c + dy + ROWS, dx:dx + W], start=tap == 0, stop=tap == 8)
                if tap == 8:
                    ins.then_inc(s_conv.sem, 1)

            def project(i, c, name):
                use = f"{name}{c}"
                hf = int(name[-1]) if name[-1] in "01" else 0
                pe.wait_ge(*free(i, use))
                if name == "dtr":
                    pe.wait_ge(s_xc.sem, s_xc.at(i, 2 * c + 2))
                if name[:2] == "dt" and name[-1] in "01":
                    for x in other_bank(use, f"dtr{c}"):
                        pe.wait_ge(*read(i, x))
                    ins = pe.matmul(aux(use)[:, 0:T], w_dt[:, P * hf:P * hf + P], dt_r[:, :], start=True, stop=True)
                elif name[0] == "z":
                    ins = pe.matmul(aux(use)[:, 0:T], w_z[:, P * hf:P * hf + P],
                                    gx[:, ROWS * c + 1:ROWS * c + 1 + ROWS, 1:1 + W], start=True, stop=True)
                else:
                    if name == "dtN":
                        pe.wait_ge(s_dt.sem, s_dt.at(i, c + 1))
                    lhs = {"B": w_b, "C": w_c, "dtr": w_xp[:, :, 0:RK], "dtN": w_n}[name]
                    rhs = dt if name == "dtN" else xc[:, c % 3]
                    rows = RK if name == "dtr" else P
                    for h in range(HV):
                        ins = pe.matmul(aux(use)[0:rows, 0:T], lhs[:, h, :], rhs[:, h, :], start=h == 0, stop=h == HV - 1)
                ins.then_inc(fills(use), 1)

            def fold_quad(i, c, m):
                hf, b = m // 4, m % 4
                if b == 0 and (c or hf):
                    pe.wait_ge(s_y.sem, s_y.at(i, 2 * c + hf))
                pe.wait_ge(s_prod.sem, s_prod.at(i, NB * c + QD * (m + 1)))
                for q in range(QD):
                    ins = pe.matmul(ps_y[32 * q:32 * q + 32, 0:T], fold[:, b, :], prod[:, (QD * m + q) % HS, :],
                                    start=b == 0, stop=b == 3)
                ins.then_inc(s_fold.sem, 1)

            def beside(i, c, n):
                if c + 2 < NC:
                    for hf in range(HV):
                        if CONV_AT[hf] <= n < CONV_AT[hf] + 9:
                            conv(i, c + 2, hf, n - CONV_AT[hf])
                for name, at, dc in BESIDE:
                    if at == n and 0 <= c + dc < NC:
                        if dc == 1:
                            project(i, c + 1, name)
                        else:
                            finish(i, c - 1, name)

            def scan(i, c, j):
                par = c % 2
                pe.wait_ge(s_dtstack.sem, s_dtstack.at(i, c + 1))
                pe.wait_ge(s_xstack.sem, s_xstack.at(i, c + 1))
                for n in range(NB):
                    k = NB * c + n
                    hf, b, q = n // 16, n % 16 // 4, n % 4
                    pe.wait_ge(s_dtread.sem, s_dtread.at(i, k))
                    pe.matmul(ps_dt[:, 0:T], copy[:, b, :], dt_stack[:, par, QD * hf + q, :],
                              start=True, stop=True).then_inc(s_dtrep.sem, 1)
                    pe.wait_ge(s_xread.sem, s_xread.at(i, k))
                    pe.matmul(ps_x[:, 0:T], copy[:, b, :], x_stack[:, par, QD * hf + q, :],
                              start=True, stop=True).then_inc(s_xrep.sem, 1)
                    if j is not None:
                        experts(j, k)
                    if n % QD == FOLD_LAG and k >= QD:
                        fold_quad(i, (k - QD) // NB, (n // QD - 1) % (NB // QD))
                    beside(i, c, n)

            def finish(i, c, name):
                use = f"{name}{c}"
                pe.wait_ge(*free(i, use))
                if name == "mean":
                    pe.wait_ge(s_y.sem, s_y.at(i, 2 * c + 2))
                elif name == "var":
                    pe.wait_ge(s_ysq.sem, s_ysq.at(i, c + 1))
                else:
                    pe.wait_ge(s_yg.sem, s_yg.at(i, c + 1))
                if name != "out":
                    src = y if name == "mean" else y_sq
                    for hf in range(HV):
                        ins = pe.matmul(aux(use)[:, 0:T], mean[:, :], src[:, hf, :], start=hf == 0, stop=hf == 1)
                else:
                    for k in range(TT):
                        o = aux(use)[:, P * k:P * k + P]
                        for hf in range(HV):
                            pe.matmul(o, y[:, hf, P * k:P * k + P], w_out[:, hf, :], start=hf == 0, stop=False)
                        ins = pe.matmul(o, ones[0:1, :], b_out[0:1, :], start=False, stop=True)
                ins.then_inc(fills(use), 1)

            def attend_project(i):
                names = [f"xnT{g}" for g in range(NC)]
                for g, name in enumerate(names):
                    pe.wait_ge(s_xn.sem, s_xn.at(i, g + 1))
                    pe.wait_ge(*free(i, name))
                    for k in range(TT):
                        ins = pe.transpose(aux(name)[:, P * k:P * k + P], big_u[:, TT * g + k, :], eye[:, :])
                    ins.then_inc(fills(name), 1)
                for g in range(NC):
                    name = f"kT{g}"
                    pe.wait_ge(*free(i, name))
                    for x in other_bank(name, f"xnT{g}"):
                        pe.wait_ge(*read(i, x))
                    pe.matmul(aux(name)[:, 0:T], w_qkv[:, D:2 * D], big_t[:, T * g:T * g + T], start=True, stop=True).then_inc(fills(name), 1)
                for g in range(NT // 2):
                    name = f"qv{g}"
                    pe.wait_ge(*free(i, name))
                    for x in other_bank(name, *(f"xnT{h}" for h in range(2 * g // TT, (2 * g + 1) // TT + 1))):
                        pe.wait_ge(*read(i, x))
                    for k in range(2):
                        lhs = big_t[:, P * (2 * g + k):P * (2 * g + k + 1)]
                        for w in range(2):
                            ins = pe.matmul(aux(name)[:, D * (2 * k + w):D * (2 * k + w + 1)], lhs, w_qkv[:, 2 * w * D:(2 * w + 1) * D],
                                            start=True, stop=True)
                    ins.then_inc(fills(name), 1)

            def attend_context(i):
                pe.wait_ge(s_kexp.sem, s_kexp.at(i, 1))
                transposes(i, [f"ek{g}" for g in range(NC)], lambda k: big_k[:, P * k:P * k + P])
                pe.wait_ge(*free(i, "ctx"))
                for x in other_bank("ctx", *(f"ek{g}" for g in range(NC)), *(f"qv{g}" for g in range(NT // 2))):
                    pe.wait_ge(*read(i, x))
                for k in range(NT):
                    ins = pe.matmul(aux("ctx")[:, 0:D], qv[:, 1, k, :], big_u[:, k, :], start=k == 0, stop=k == NT - 1)
                ins.then_inc(fills("ctx"), 1)
                pe.wait_ge(*free(i, "ctx2"))
                for x in other_bank("ctx2", "ctx"):
                    pe.wait_ge(*read(i, x))
                pe.matmul(aux("ctx2")[:, 0:D], ctx_t[:, :], w_proj[:, :], start=True, stop=True).then_inc(fills("ctx2"), 1)

            def attend_out(i):
                pe.wait_ge(s_q.sem, s_q.at(i, 1))
                transposes(i, [f"qT{g}" for g in range(NC)], lambda k: qv[:, 0, k, :])
                for g in range(NC):
                    name = f"ao{g}"
                    pe.wait_ge(*free(i, name))
                    for x in other_bank(name, "ctx2", f"qT{g}"):
                        pe.wait_ge(*read(i, x))
                    for k in range(TT):
                        o = T * g + P * k
                        ins = pe.matmul(aux(name)[:, P * k:P * k + P], big_t[:, o:o + P], ctx_o[:, :], start=True, stop=True)
                    ins.then_inc(fills(name), 1)

            def route(i):
                for g in range(NC):
                    name = f"uT{g}"
                    pe.wait_ge(s_xn.sem, s_xn.at(i, 2 * NC + g + 1))
                    pe.wait_ge(*free(i, name))
                    for k in range(TT):
                        ins = pe.transpose(aux(name)[:, P * k:P * k + P], big_u[:, TT * g + k, :], eye[:, :])
                    ins.then_inc(fills(name), 1)
                pe.wait_ge(*free(i, "logit"))
                for x in other_bank("logit", *(f"uT{g}" for g in range(NC))):
                    pe.wait_ge(*read(i, x))
                for k in range(NT):
                    ins = pe.matmul(aux("logit")[:, NE * k:NE * k + NE], big_t[:, P * k:P * k + P], w_gate[:, :], start=True, stop=True)
                ins.then_inc(fills("logit"), 1)

            def experts(j, k):
                u, s = unit_at(k), sums_at(k)
                if u is not None:
                    e, g, m = u // (NC * MF), u // MF % NC, u % MF
                    if u % (NC * MF) == 0:
                        pe.wait_ge(s_w[e % 2].sem, s_w[e % 2].at(j, e // 2 + 1))
                    for name, w in ((f"h{u}", w1), (f"g{u}", w3)):
                        pe.wait_ge(*free(j, name))
                        pe.matmul(aux(name)[:, 0:T], w[:, e % 2, P * m:P * m + P], big_t[:, T * g:T * g + T],
                                  start=True, stop=True).then_inc(fills(name), 1)
                if s is not None:
                    e, name = s // NC, f"moe{s}"
                    pe.wait_ge(*free(j, name))
                    pe.wait_ge(*read(j, f"g{MF * s + MF - 1}"))
                    for t in range(TT):
                        for m in range(MF):
                            ins = pe.matmul(aux(name)[:, P * t:P * t + P], hidden[:, (MF * s + m) % HID, P * t:P * t + P],
                                            w2[:, e % 2, P * m:P * m + P], start=m == 0, stop=m == MF - 1)
                    ins.then_inc(fills(name), 1)

            def convs(i, c):
                for hf in range(HV):
                    for tap in range(9):
                        conv(i, c, hf, tap)

            def first(i, lo, hi):
                for name, at, dc in BESIDE:
                    if dc == 1 and lo <= at < hi:
                        project(i, 0, name)

            def start(i):
                pe.wait_ge(s_norm.sem, s_norm.at(i, 1))
                convs(i, 0)

            def scans(i, j):
                for c in range(NC):
                    scan(i, c, j)
                fold_quad(i, NC - 1, NB // QD - 1)
                for name, at, dc in BESIDE:
                    if dc == -1:
                        finish(i, NC - 1, name)

            turn(0)
            group_norm(0)
            start(0)
            first(0, 0, 13)
            convs(0, 1)
            first(0, 13, NB)
            scans(0, None)
            with pe.Fori(0, B - 1) as j:
                i = Next(j)
                turn(i)
                group_norm(i)
                attend_project(j)
                start(i)
                attend_context(j)
                first(i, 0, 6)
                attend_out(j)
                convs(i, 1)
                first(i, 6, 13)
                route(j)
                first(i, 13, NB)
                scans(i, j)
                for k in range(SC, SLOTS):
                    experts(j, k)
            j = B - 1
            attend_project(j)
            attend_context(j)
            attend_out(j)
            route(j)
            for k in range(SLOTS):
                experts(j, k)

        @block.scalar
        def _(act):
            for s in (*aux_free, s_dtread, s_xread, s_xc, s_out):
                act.sem_inc(s.sem, s.first)
            act.wait_ge(s_const.sem, n_const)
            act.wait_ge(s_clear.sem, N_CLEAR)
            act.wait_ge(s_setup.sem, N_SETUP)
            act.wait_ge(s_half.sem, 1)
            act.activation(y_rs[:, 0:1], decay_rate, ACT.Exp).then_inc(s_rate.sem, 1)
            act.wait_ge(s_rate.sem, 1)
            act.activation(decay_rate, y_rs[:, 0:1], ACT.Copy, scale=-1.0).then_inc(s_rate.sem, 1)
            act.wait_ge(s_rate.sem, 2)
            count = [0, 0]

            def link(i, ins):
                count[0] += 1
                ins.then_inc(act_step.sem, 1)
                act.wait_ge(act_step.sem, act_step.at(i, count[0]))

            def tie(j, ins):
                count[1] += 1
                ins.then_inc(act_post.sem, 1)
                act.wait_ge(act_post.sem, act_post.at(j, count[1]))

            def logs():
                act.preload_act_table_set("natural_log_exp_and_others")

            def tanhs():
                act.preload_act_table_set("exp_and_others")

            def evacuate(i, name, dst, src, func=ACT.Copy, **kw):
                act.wait_ge(*full(i, name))
                act.activation(dst, src, func, **kw).then_inc(frees(name), 1)

            roots = [0]

            def root(j, buf):
                roots[0] += 1
                act.wait_ge(s_var.sem, s_var.at(j, roots[0]))
                tie(j, act.activation(buf, buf, ACT.Ln))
                act.activation(buf, buf, ACT.Exp, scale=-0.5).then_inc(s_root.sem, 1)

            def load(i):
                logs()
                act.wait_ge(aux_free[MAIN].sem, aux_free[MAIN].at(i, 0))
                image = i.j + 1 if isinstance(i, Next) else i
                rows = a["x"][bass.ds(image, 1)].rearrange("o (k p) d -> p (o k) d", p=P)
                for c in range(NC):
                    act.dma_start(x_tok[:, TT * c:TT * c + TT, :], rows[:, TT * c:TT * c + TT, :]).then_inc(s_x.sem, 16)

            def store(j):
                act.wait_ge(aux_free[SB].sem, aux_free[SB].at(j, aux_per[SB]))
                act.dma_start(a["out"][bass.ds(j, 1)].rearrange("o (k p) d -> p (o k) d", p=P), acc).then_inc(s_out.sem, 16)

            def turn(i):
                for g in range(NC):
                    evacuate(i, f"xT{g}", gx[:, 1 + ROWS * g:1 + ROWS * g + ROWS, 1:1 + W],
                             aux(f"xT{g}")[:, 0:T].rearrange("p (r w) -> p r w", w=W))

            def group_norm(i):
                group_var = gmv[:, 5:6]
                act.wait_ge(*read(i, "gv"))
                link(i, act.activation(group_var, group_var, ACT.Ln))
                act.activation(group_var, group_var, ACT.Exp, scale=-0.5).then_inc(s_groot.sem, 1)

            def copy_conv(i, c, hf):
                if c >= 3:
                    act.wait_ge(s_y.sem, s_y.at(i, 2 * (c - 3) + 2))
                act.wait_ge(s_conv.sem, s_conv.at(i, 2 * c + hf + 1))
                act.activation(xc[:, c % 3, hf, :], ps_conv[:, 0:T], ACT.Copy).then_inc(s_xc.sem, 1)

            def copy_C(i, c):
                if c >= 2:
                    act.wait_ge(s_prod.sem, s_prod.at(i, NB * (c - 1)))
                evacuate(i, f"C{c}", c_rep[:, c % 2, :], aux(f"C{c}")[:, 0:T])

            def copy_B(i, c):
                if c >= 1:
                    act.wait_ge(*read(i, f"dtN{c - 1}"))
                evacuate(i, f"B{c}", b_rep[:, :], aux(f"B{c}")[:, 0:T])

            def copy_dtr(i, c):
                evacuate(i, f"dtr{c}", dt_r[:, :], aux(f"dtr{c}")[0:RK, 0:T])

            def add_bias(i, c, hf):
                if c >= 1 and hf == 0:
                    act.wait_ge(s_rest.sem, s_rest.at(i, 2 * c))
                evacuate(i, f"dt{hf}{c}", dt[:, hf, :], aux(f"dt{hf}{c}")[:, 0:T], ACT.Identity, bias=b_dt[:, hf:hf + 1])

            def softplus(i, c, k):
                if k == 0:
                    act.wait_ge(*read(i, f"dt1{c}"))
                    link(i, act.activation(dt_tmp[:, :, :], dt[:, :, :], ACT.Abs))
                elif k == 1:
                    link(i, act.activation(dt_tmp[:, :, :], dt_tmp[:, :, :], ACT.Exp, scale=-1.0))
                else:
                    act.activation(dt_tmp[:, :, :], dt_tmp[:, :, :], ACT.Ln, bias=1.0).then_inc(s_dtl.sem, 1)

            def tanh_z(i, c, hf):
                if c >= 1 and hf == 0:
                    act.wait_ge(*read(i, f"z1{c - 1}"))
                act.wait_ge(*full(i, f"z{hf}{c}"))
                act.activation(z_tmp[:, hf, :], aux(f"z{hf}{c}")[:, 0:T], ACT.Tanh, scale=0.5).then_inc(s_tanh.sem, 1)

            def first_part(i, c, k):
                if k:
                    act.wait_ge(s_dt.sem, s_dt.at(i, c + 1))
                    act.wait_ge(s_xstack.sem, s_xstack.at(i, c + 1))
                else:
                    act.wait_ge(s_xc.sem, s_xc.at(i, 2 * c + 2))
                    if c:
                        act.wait_ge(s_dtstack.sem, s_dtstack.at(i, c))
                src = dt if k else xc[:, c % 3]
                act.activation(parts[:, 0], src[:, :, :], ACT.Copy).then_inc(s_hi.sem, 1)

            def second_part(i, c, k):
                act.wait_ge(s_rest.sem, s_rest.at(i, 2 * c + k + 1))
                act.activation(parts[:, 1], rest[:, :, :], ACT.Copy).then_inc(s_mid.sem, 1)

            def square(i, c):
                act.wait_ge(*read(i, f"mean{c}"))
                act.activation(y_sq[:, :, :], y[:, :, :], ACT.Square).then_inc(s_ysq.sem, 1)

            def inverse_root(i, c, k):
                if k == 0:
                    evacuate(i, f"var{c}", y_rs[:, :], aux(f"var{c}")[:, 0:T], ACT.Ln, bias=eps_ln)
                else:
                    act.wait_ge(*read(i, f"var{c}"))
                    act.activation(y_rs[:, :], y_rs[:, :], ACT.Exp, scale=-0.5).then_inc(s_yrs.sem, 1)

            def affine(i, c):
                act.wait_ge(s_yn.sem, s_yn.at(i, c + 1))
                for hf in range(HV):
                    ins = act.activation(y[:, hf, :], y[:, hf, :], ACT.Identity, bias=ln_b[:, hf:hf + 1], scale=ln_g[:, hf:hf + 1])
                ins.then_inc(s_yaff.sem, 1)

            def project(i, c, n):
                if n == 1:
                    first_part(i, c, 0)
                    copy_dtr(i, c)
                if n == 4:
                    second_part(i, c, 0)
                if n in (3, 5):
                    add_bias(i, c, (n - 3) // 2)
                if n in (6, 7):
                    softplus(i, c, n - 6)
                if n == 11:
                    softplus(i, c, 2)
                if n == 13:
                    copy_B(i, c)
                    first_part(i, c, 1)
                if n == 15:
                    second_part(i, c, 1)
                if n == 17:
                    copy_C(i, c)
                if n == 21:
                    tanh_z(i, c, 0)
                if n == 25:
                    tanh_z(i, c, 1)

            def finish(i, c, n):
                if n == 8:
                    square(i, c)
                if n in (11, 12):
                    inverse_root(i, c, n - 11)
                if n == 14:
                    affine(i, c)

            def experts(j, k):
                u = unit_at(k)
                if u is not None:
                    if u >= 2:
                        act.wait_ge(*read(j, f"g{u - 2}"))
                    act.wait_ge(*full(j, f"h{u}"))
                    act.activation(silu[:, u % 2, :], aux(f"h{u}")[:, 0:T], ACT.Tanh, scale=0.5).then_inc(s_htanh.sem, 1)

            def scan(i, c, j):
                for n in range(NB):
                    k = NB * c + n
                    act.wait_ge(s_dtrep.sem, s_dtrep.at(i, k + 1))
                    if k >= 2:
                        act.wait_ge(s_state.sem, s_state.at(i, k - 1))
                    act.activation(decay[:, n % 2, :], ps_dt[:, 0:T], ACT.Exp, scale=decay_rate).then_inc(s_dtread.sem, 1)
                    if n == 11:
                        logs()
                    if c + 1 < NC:
                        project(i, c + 1, n)
                    if c:
                        finish(i, c - 1, n)
                    if n == 11:
                        tanhs()
                    if j is not None:
                        experts(j, k)
                    if c + 2 < NC:
                        for hf in range(HV):
                            if n == CONV_AT[hf] + 9:
                                copy_conv(i, c + 2, hf)

            def normalise(i, k, src, dst):
                act.wait_ge(s_coef.sem, s_coef.at(i, k + 1))
                for g in range(NC):
                    for t in range(TT * g, TT * g + TT):
                        ins = act.activation(dst[:, t, :], src[:, t, :], ACT.Identity, bias=nb[:, t:t + 1], scale=r1[:, t:t + 1])
                    ins.then_inc(s_xn.sem, 1)

            def attend_start(i):
                root(i, r1[:, :])
                root(i, r2[:, :])
                normalise(i, 0, t1, big_u)

            def attend_project(i):
                for g in range(NC):
                    evacuate(i, f"xnT{g}", big_t[:, T * g:T * g + T], aux(f"xnT{g}")[:, 0:T])
                for g in range(NC):
                    evacuate(i, f"kT{g}", big_k[:, T * g:T * g + T], aux(f"kT{g}")[:, 0:T])
                act.wait_ge(s_out.sem, s_out.at(i, 0))
                for g in range(NT // 2):
                    evacuate(i, f"qv{g}", qv[:, :, 2 * g:2 * g + 2, :].rearrange("p w k d -> p k w d"),
                             aux(f"qv{g}")[:, :].rearrange("p (k w d) -> p k w d", k=2, w=2))

            def attend_context(i):
                for g in (NC - 3, NC - 2, NC - 1):
                    act.wait_ge(*read(i, f"kT{g}"))
                act.wait_ge(s_kmax.sem, s_kmax.at(i, 1))
                act.activation(big_k[:, :], big_k[:, :], ACT.Exp, bias=k_col[:, 0:1], accum_out=k_col[:, 1:2]).then_inc(s_kexp.sem, 1)
                act.wait_ge(s_qsub.sem, s_qsub.at(i, 1))
                act.activation(qv[:, 0], qv[:, 0], ACT.Exp).then_inc(s_qexp.sem, 1)
                for g in range(NC):
                    evacuate(i, f"ek{g}", big_u[:, TT * g:TT * g + TT, :].rearrange("p k d -> p (k d)"), aux(f"ek{g}")[:, 0:T])

            def attend_out(i):
                for g in range(NC):
                    evacuate(i, f"qT{g}", big_t[:, T * g:T * g + T], aux(f"qT{g}")[:, 0:T])
                for g in range(NC):
                    evacuate(i, f"ao{g}", big_k[:, T * g:T * g + T], aux(f"ao{g}")[:, 0:T])

            def attend_norm(i):
                root(i, r1[:, :])
                ao = big_k[:, :].rearrange("p (k d) -> p k d", d=D)
                normalise(i, 1, ao, ao)

            def route(i):
                root(i, r1[:, :])
                normalise(i, 2, acc, big_u)
                for g in range(NC):
                    evacuate(i, f"uT{g}", big_t[:, T * g:T * g + T], aux(f"uT{g}")[:, 0:T])
                act.wait_ge(s_top.sem, s_top.at(i, 1))
                act.activation(gw[:, 0, :], gw[:, 0, :], ACT.Exp).then_inc(s_topexp.sem, 1)

            def convs(i, c):
                for hf in range(HV):
                    copy_conv(i, c, hf)

            def first(i, lo, hi):
                for n in range(lo, hi):
                    project(i, 0, n)

            def scans(i, j):
                tanhs()
                for c in range(NC):
                    scan(i, c, j)
                logs()
                for n in range(NB):
                    finish(i, NC - 1, n)

            load(0)
            turn(0)
            group_norm(0)
            convs(0, 0)
            first(0, 0, 13)
            convs(0, 1)
            tanhs()
            first(0, 13, NB)
            scans(0, None)
            assert count[0] == ACT_STEPS[0], count
            with act.Fori(0, B - 1) as j:
                i = Next(j)
                count[:], roots[0] = (0, 0), 0
                load(i)
                attend_start(j)
                turn(i)
                group_norm(i)
                attend_project(j)
                convs(i, 0)
                attend_context(j)
                first(i, 0, 6)
                attend_out(j)
                convs(i, 1)
                attend_norm(j)
                first(i, 6, 13)
                route(j)
                tanhs()
                first(i, 13, NB)
                scans(i, j)
                for k in range(SC, SLOTS):
                    experts(j, k)
                store(j)
            assert count == [ACT_STEPS[0], ACT_STEPS[1]], count
            j = B - 1
            count[:], roots[0] = (0, 0), 0
            logs()
            attend_start(j)
            attend_project(j)
            attend_context(j)
            attend_out(j)
            attend_norm(j)
            route(j)
            tanhs()
            for k in range(SLOTS):
                experts(j, k)
            store(j)
            act.wait_ge(s_out.sem, 16 * (B + 1))

        @block.vector
        def _(dve):
            dve.wait_ge(s_const.sem, n_const)
            for k, (dst, src) in enumerate(((w_b, w_xp[:, :, RK:RK + NS]), (w_c, w_xp[:, :, RK + NS:RK + 2 * NS]), (w_n, w_dtn[:, :, :]))):
                for hf in range(HV):
                    dve.tensor_copy(dst[:, hf, :].rearrange("p (n j) -> p n j", j=JB),
                                    src[:, hf, :].unsqueeze(2).broadcast_to([P, NS, JB])).then_inc(s_setup.sem, 1)
            taps = state[:, 0:6, :].rearrange("p s t -> p (s t)").rearrange("p (k d) -> p k d", d=DI)
            for tap in range(9):
                dve.tensor_tensor(w_conv[:, tap, :], y[:, 0, 0:DI], taps[:, tap, :], ALU.mult).then_inc(s_setup.sem, 1)
            dve.tensor_scalar(w_qkv[:, :], w_qkv[:, :], norm_gamma, None, ALU.mult).then_inc(s_setup.sem, 1)
            dve.tensor_copy(copy[:, :, :].rearrange("p (s b) m -> p s (b m)", s=2), prod[0:32 * PARTS, 0:2, 0:256]).then_inc(s_setup.sem, 1)
            dve.wait_ge(s_clear.sem, N_CLEAR)
            dve.wait_ge(s_setup.sem, N_SETUP)
            dve.tensor_scalar(vecs[:, 4:8], vecs[:, 4:8], 0.5, None, ALU.mult).then_inc(s_half.sem, 1)
            count = [0, 0]

            def link(i, ins):
                count[0] += 1
                ins.then_inc(dve_step.sem, 1)
                dve.wait_ge(dve_step.sem, dve_step.at(i, count[0]))

            def tie(j, ins):
                count[1] += 1
                ins.then_inc(dve_post.sem, 1)
                dve.wait_ge(dve_post.sem, dve_post.at(j, count[1]))

            def turn(i):
                for g in range(NC):
                    dve.wait_ge(*read(i, f"xT{g}"))
                    ins = dve.bn_stats(gst[:, g, :], gx[:, 1 + ROWS * g:1 + ROWS * g + ROWS, 1:1 + W])
                    link(i, ins)

            def group_norm(i):
                part = gst[:, :, :].rearrange("p g (s k) -> p (g s) k", k=3)
                link(i, dve.tensor_reduce(gmv[:, 7:8], part[:, :, 1], AX.X, ALU.add))
                link(i, dve.tensor_scalar(gmv[:, 0:1], gmv[:, 7:8], 1.0 / (2 * NC), None, ALU.mult))
                link(i, dve.tensor_scalar(gdev[:, :], part[:, :, 1], gmv[:, 0:1], None, ALU.subtract))
                link(i, dve.tensor_tensor(gdev[:, :], gdev[:, :], gdev[:, :], ALU.mult))
                link(i, dve.tensor_scalar(gdev[:, :], gdev[:, :], L / (2.0 * NC), None, ALU.mult))
                link(i, dve.tensor_tensor(gdev[:, :], gdev[:, :], part[:, :, 2], ALU.add))
                link(i, dve.tensor_reduce(gmv[:, 7:8], gdev[:, :], AX.X, ALU.add))
                dve.tensor_scalar(gmv[:, 1:2], gmv[:, 7:8], 1.0 / L, None, ALU.mult).then_inc(s_gn.sem, 1)
                dve.wait_ge(s_gn.sem, s_gn.at(i, 1))
                dve.wait_ge(*full(i, "gm"))
                dve.tensor_copy(gmv[:, 4:5], aux("gm")[:, 0:1]).then_inc(frees("gm"), 1)
                dve.wait_ge(*read(i, "gm"))
                link(i, dve.tensor_tensor(gmv[:, 3:4], gmv[:, 0:1], gmv[:, 4:5], ALU.subtract))
                dve.scalar_tensor_tensor(out=gmv[:, 2:3], in0=gmv[:, 3:4], scalar=gmv[:, 3:4], in1=gmv[:, 1:2],
                                         op0=ALU.mult, op1=ALU.add).then_inc(s_gn.sem, 1)
                dve.wait_ge(*full(i, "gv"))
                dve.tensor_scalar(gmv[:, 5:6], aux("gv")[:, 0:1], 1e-5, None, ALU.add).then_inc(frees("gv"), 1)
                dve.wait_ge(s_groot.sem, s_groot.at(i, 1))
                link(i, dve.scalar_tensor_tensor(out=gmv[:, 6:7], in0=gmv[:, 4:5], scalar=-1.0, in1=gmv[:, 5:6],
                                                 op0=ALU.mult, op1=ALU.mult))
                inner = gx[:, 1:1 + H, 1:1 + W]
                dve.tensor_scalar(inner, inner, gmv[:, 5:6], gmv[:, 6:7], ALU.mult, ALU.add).then_inc(s_norm.sem, 1)

            def project(i, c, n):
                if n in (2, 14):
                    k = 0 if n == 2 else 1
                    src = dt if k else xc[:, c % 3]
                    dve.wait_ge(s_hi.sem, s_hi.at(i, 2 * c + k + 1))
                    dve.tensor_tensor(rest[:, :, :], src[:, :, :], parts[:, 0], ALU.subtract).then_inc(s_rest.sem, 1)
                if n in (5, 16):
                    k = 0 if n == 5 else 1
                    dve.wait_ge(s_mid.sem, s_mid.at(i, 2 * c + k + 1))
                    dve.tensor_tensor(parts[:, 2], rest[:, :, :], parts[:, 1], ALU.subtract).then_inc(s_lo.sem, 1)
                if n == 12:
                    dve.wait_ge(s_dtl.sem, s_dtl.at(i, c + 1))
                    dve.scalar_tensor_tensor(out=dt[:, :, :], in0=dt[:, :, :], scalar=0.0, in1=dt_tmp[:, :, :],
                                             op0=ALU.max, op1=ALU.add).then_inc(s_dt.sem, 1)
                if n == 15:
                    use = f"dtN{c}"
                    dve.wait_ge(*full(i, use))
                    dve.scalar_tensor_tensor(out=db_rep[:, c % 2, :], in0=aux(use)[:, 0:T], scalar=b_dtn, in1=b_rep[:, :],
                                             op0=ALU.add, op1=ALU.mult).then_inc(frees(use), 1)
                if n in (22, 26):
                    hf = 0 if n == 22 else 1
                    use = f"z{hf}{c}"
                    dve.wait_ge(s_tanh.sem, s_tanh.at(i, 2 * c + hf + 1))
                    dve.scalar_tensor_tensor(out=sz[:, c % 2, hf, :], in0=z_tmp[:, hf, :], scalar=1.0, in1=aux(use)[:, 0:T],
                                             op0=ALU.add, op1=ALU.mult).then_inc(frees(use), 1)

            def skip(i, c, hf):
                dve.wait_ge(s_fold.sem, s_fold.at(i, NB // QD * c + 4 * (hf + 1)))
                dve.scalar_tensor_tensor(out=y[:, hf, :], in0=xc[:, c % 3, hf, :], scalar=d_skip[:, hf:hf + 1], in1=ps_y[:, 0:T],
                                         op0=ALU.mult, op1=ALU.add).then_inc(s_y.sem, 1)

            def finish(i, c, n):
                both = lambda v: v.unsqueeze(1).broadcast_to([P, HV, T])
                if n == 5:
                    skip(i, c, 1)
                if n == 7:
                    use = f"mean{c}"
                    dve.wait_ge(*full(i, use))
                    dve.wait_ge(s_y.sem, s_y.at(i, 2 * c + 2))
                    dve.tensor_tensor(y[:, :, :], y[:, :, :], both(aux(use)[:, 0:T]), ALU.subtract).then_inc(frees(use), 1)
                if n == 13:
                    dve.wait_ge(s_yrs.sem, s_yrs.at(i, c + 1))
                    dve.wait_ge(*read(i, f"mean{c}"))
                    dve.tensor_tensor(y[:, :, :], y[:, :, :], both(y_rs[:, :]), ALU.mult).then_inc(s_yn.sem, 1)
                if n == 15:
                    dve.wait_ge(s_yaff.sem, s_yaff.at(i, c + 1))
                    dve.tensor_tensor(y[:, :, :], y[:, :, :], sz[:, c % 2], ALU.mult).then_inc(s_yg.sem, 1)
                if n == 19:
                    use = f"out{c}"
                    dve.wait_ge(*full(i, use))
                    tok = slice(TT * c, TT * c + TT)
                    dve.tensor_tensor(t1[:, tok, :].rearrange("p k d -> p (k d)"), aux(use)[:, 0:T],
                                      x_tok[:, tok, :].rearrange("p k d -> p (k d)"), ALU.add).then_inc(frees(use), 1)

            def inflows(i, c, n):
                k = NB * c + n
                dve.wait_ge(s_xrep.sem, s_xrep.at(i, k + 1))
                if k >= 2:
                    dve.wait_ge(s_state.sem, s_state.at(i, k - 1))
                dve.tensor_tensor(inflow[:, n % 2, :], ps_x[:, 0:T], db_rep[:, c % 2, :], ALU.mult).then_inc(s_xread.sem, 1)

            def scan(i, c, j):
                if c == 0:
                    dve.wait_ge(*read(i, f"dtN{c}"))
                    inflows(i, c, 0)
                for n in range(NB):
                    k = NB * c + n
                    if j is not None:
                        experts(j, k)
                    if n + 1 < NB:
                        inflows(i, c, n + 1)
                    elif c + 1 < NC:
                        dve.wait_ge(*read(i, f"dtN{c + 1}"))
                        inflows(i, c + 1, 0)
                    dve.wait_ge(s_xread.sem, s_xread.at(i, k + 1))
                    dve.wait_ge(s_dtread.sem, s_dtread.at(i, k + 1))
                    if k >= HS:
                        dve.wait_ge(s_prod.sem, s_prod.at(i, k - HS + 1))
                    init = carry[:, n:n + 1] if c else 0.0
                    dve.tensor_tensor_scan(state[:, n % HS, :], decay[:, n % 2, :], inflow[:, n % 2, :], init,
                                           ALU.mult, ALU.add).then_inc(s_state.sem, 1)
                    if n % QD == QD - 1:
                        dve.wait_ge(s_state.sem, s_state.at(i, k + 1))
                        s0 = n % HS - QD + 1
                        link(i, dve.tensor_copy(carry[:, n - QD + 1:n + 1], state[:, s0:s0 + QD, T - 1]))
                    if c + 1 < NC:
                        project(i, c + 1, n)
                    if c:
                        finish(i, c - 1, n)
                    if n == 22:
                        skip(i, c, 0)

            roots = [0]


            def stats(i, k, src, twice=False):
                for t in range(NT):
                    ins = dve.bn_stats(st[:, t, :], src[:, t, :])
                tie(i, ins)
                tie(i, dve.tensor_tensor(mv[:, :, 0], st[:, :, 1], st[:, :, 4], ALU.subtract))
                tie(i, dve.tensor_tensor(mv[:, :, 0], mv[:, :, 0], mv[:, :, 0], ALU.mult))
                tie(i, dve.tensor_tensor(mv[:, :, 1], st[:, :, 2], st[:, :, 5], ALU.add))
                tie(i, dve.scalar_tensor_tensor(out=mv[:, :, 1], in0=mv[:, :, 0], scalar=D / 4.0, in1=mv[:, :, 1], op0=ALU.mult, op1=ALU.add))
                tie(i, dve.tensor_scalar(mv[:, :, 1], mv[:, :, 1], 1.0 / D, None, ALU.mult))
                tie(i, dve.tensor_tensor(mv[:, :, 0], st[:, :, 1], st[:, :, 4], ALU.add))
                tie(i, dve.tensor_scalar(mv[:, :, 0], mv[:, :, 0], 0.5, None, ALU.mult))
                dve.tensor_scalar(r1[:, :], mv[:, :, 1], 1e-5, None, ALU.add).then_inc(s_var.sem, 1)
                roots[0] += 1
                dve.wait_ge(s_root.sem, s_root.at(i, roots[0]))
                if twice:
                    tie(i, dve.tensor_tensor(r2[:, :], mv[:, :, 1], r1[:, :], ALU.mult))
                    tie(i, dve.tensor_tensor(r2[:, :], r2[:, :], r1[:, :], ALU.mult))
                    dve.tensor_scalar(r2[:, :], r2[:, :], 1e-5, None, ALU.add).then_inc(s_var.sem, 1)
                    roots[0] += 1
                    dve.wait_ge(s_root.sem, s_root.at(i, roots[0]))
                    tie(i, dve.tensor_tensor(r1[:, :], r1[:, :], r2[:, :], ALU.mult))
                dve.scalar_tensor_tensor(out=nb[:, :], in0=mv[:, :, 0], scalar=-1.0, in1=r1[:, :],
                                         op0=ALU.mult, op1=ALU.mult).then_inc(s_coef.sem, 1)

            def attend_start(i):
                dve.wait_ge(*read(i, f"out{NC - 1}"))
                stats(i, 0, t1, twice=True)

            def attend_context(i):
                q = qv[:, 0].rearrange("p k (h d) -> p (k h) d", d=DH)
                for g in (NC - 3, NC - 2, NC - 1):
                    dve.wait_ge(*read(i, f"kT{g}"))
                tie(i, dve.tensor_reduce(k_col[:, 2:3], big_k[:, :], AX.X, ALU.max))
                dve.tensor_scalar(k_col[:, 0:1], k_col[:, 2:3], -1.0, None, ALU.mult).then_inc(s_kmax.sem, 1)
                for g in (NT // 2 - 3, NT // 2 - 2, NT // 2 - 1):
                    dve.wait_ge(*read(i, f"qv{g}"))
                tie(i, dve.tensor_reduce(q_max[:, :], q, AX.X, ALU.max))
                dve.tensor_tensor(q, q, q_max[:, :].unsqueeze(2).broadcast_to([P, NT * NH, DH]), ALU.subtract).then_inc(s_qsub.sem, 1)
                dve.wait_ge(s_kexp.sem, s_kexp.at(i, 1))
                tie(i, dve.reciprocal(k_col[:, 3:4], k_col[:, 1:2]))
                dve.wait_ge(s_qexp.sem, s_qexp.at(i, 1))
                tie(i, dve.tensor_reduce(q_sum[:, :], q, AX.X, ALU.add))
                tie(i, dve.reciprocal(q_max[:, :], q_sum[:, :]))
                dve.tensor_tensor(q, q, q_max[:, :].unsqueeze(2).broadcast_to([P, NT * NH, DH]), ALU.mult).then_inc(s_q.sem, 1)
                dve.wait_ge(*full(i, "ctx"))
                dve.tensor_tensor(ctx_t[:, :], aux("ctx")[:, 0:D], heads[:, :], ALU.mult).then_inc(frees("ctx"), 1)
                dve.wait_ge(*full(i, "ctx2"))
                dve.tensor_scalar(ctx_o[:, :], aux("ctx2")[:, 0:D], k_col[:, 3:4], DH ** -0.5, ALU.mult, ALU.mult).then_inc(frees("ctx2"), 1)

            def attend_norm(i):
                for g in (NC - 3, NC - 2, NC - 1):
                    dve.wait_ge(*read(i, f"ao{g}"))
                ao = big_k[:, :].rearrange("p (k d) -> p k d", d=D)
                stats(i, 1, ao)
                dve.wait_ge(s_xn.sem, s_xn.at(i, 2 * NC))
                tie(i, dve.tensor_tensor(ao, ao, out_gamma[:, :].unsqueeze(1).broadcast_to([P, NT, D]), ALU.mult))
                tie(i, dve.tensor_tensor(acc, t1[:, :, :], ao, ALU.add))

            def route(i):
                stats(i, 2, acc)
                dve.wait_ge(*full(i, "logit"))
                dve.tensor_copy(logit[:, :, :].rearrange("p k e -> p (k e)"), aux("logit")[:, 0:NT * NE])
                for t in range(NT):
                    ins = dve.max(top[:, t, :], aux("logit")[:, NE * t:NE * t + NE])
                ins.then_inc(frees("logit"), 1)
                dve.wait_ge(*read(i, "logit"))
                dve.tensor_tensor(gw[:, 0, :], top[:, :, 1], top[:, :, 0], ALU.subtract).then_inc(s_top.sem, 1)
                for t in range(NT):
                    ins = dve.max_index(where[:, t, :], top[:, t, :], logit[:, t, :])
                tie(i, ins)
                tie(i, dve.tensor_copy(place[:, :, :], where[:, :, :]))
                dve.wait_ge(s_topexp.sem, s_topexp.at(i, 1))
                tie(i, dve.tensor_scalar(gw[:, 1, :], gw[:, 0, :], 1.0, None, ALU.add))
                tie(i, dve.reciprocal(gw[:, 2, :], gw[:, 1, :]))
                tie(i, dve.tensor_scalar(gw[:, 2, :], gw[:, 2, :], 0.5, None, ALU.mult))
                tie(i, dve.tensor_tensor(gw[:, 3, :], gw[:, 2, :], gw[:, 0, :], ALU.mult))
                for k, dst in enumerate((gate, pick)):
                    tie(i, dve.tensor_tensor(dst[:, :, :], place[:, :, k:k + 1].broadcast_to([P, NT, NE]),
                                              iota[:, :].unsqueeze(1).broadcast_to([P, NT, NE]), ALU.is_equal))
                    tie(i, dve.tensor_tensor(dst[:, :, :], dst[:, :, :], gw[:, 2 + k, :].unsqueeze(2).broadcast_to([P, NT, NE]), ALU.mult))
                tie(i, dve.tensor_tensor(gate[:, :, :], gate[:, :, :], pick[:, :, :], ALU.add))

            def experts(j, k):
                u, s = unit_at(k), add_at(k)
                if u is not None:
                    e, m = u // (NC * MF), u % MF
                    dve.wait_ge(s_htanh.sem, s_htanh.at(j, u + 1))
                    dve.scalar_tensor_tensor(out=silu[:, u % 2, :], in0=silu[:, u % 2, :], scalar=1.0, in1=aux(f"h{u}")[:, 0:T],
                                             op0=ALU.add, op1=ALU.mult).then_inc(frees(f"h{u}"), 1)
                    dve.wait_ge(*full(j, f"g{u}"))
                    dve.wait_ge(*read(j, f"h{u}"))
                    if u >= HID:
                        dve.wait_ge(*full(j, f"moe{u // MF - HID // MF}"))
                    dve.scalar_tensor_tensor(out=hidden[:, u % HID, :], in0=aux(f"g{u}")[:, 0:T], scalar=b3[:, e, m:m + 1],
                                             in1=silu[:, u % 2, :], op0=ALU.add, op1=ALU.mult).then_inc(frees(f"g{u}"), 1)
                if s is not None:
                    e, g, name = s // NC, s % NC, f"moe{s}"
                    dve.wait_ge(*full(j, name))
                    for n in range(TT):
                        t = TT * g + n
                        ins = dve.scalar_tensor_tensor(out=acc[:, t, :], in0=aux(name)[:, P * n:P * n + P], scalar=gate[:, t, e:e + 1],
                                                       in1=acc[:, t, :], op0=ALU.mult, op1=ALU.add)
                    ins.then_inc(frees(name), 1)

            def first(i, lo, hi):
                for n in range(lo, hi):
                    project(i, 0, n)

            def scans(i, j):
                for c in range(NC):
                    scan(i, c, j)
                for n in range(NB):
                    finish(i, NC - 1, n)

            turn(0)
            group_norm(0)
            first(0, 0, NB)
            scans(0, None)
            assert count[0] == DVE_STEPS[0], count
            with dve.Fori(0, B - 1) as j:
                i = Next(j)
                count[:], roots[0] = (0, 0), 0
                attend_start(j)
                turn(i)
                group_norm(i)
                attend_context(j)
                first(i, 0, 6)
                attend_norm(j)
                first(i, 6, 13)
                route(j)
                first(i, 13, NB)
                scans(i, j)
                for k in range(SC, SLOTS):
                    experts(j, k)
            assert count == [DVE_STEPS[0], DVE_STEPS[1]], count
            j = B - 1
            count[:], roots[0] = (0, 0), 0
            attend_start(j)
            attend_context(j)
            attend_norm(j)
            route(j)
            for k in range(SLOTS):
                experts(j, k)


_ORDER = ["x", "w_in", "conv_k", "w_xp", "w_dt", "w_dtn", "w_out", "b_out", "vecs", "norm_gamma", "w_qkv", "w_proj",
          "out_gamma", "w_gate", "w1", "w2", "w3", "b3", "eye", "group", "heads", "mean", "iota", "copy", "fold"]


def kernel(**v):
    import numpy as _np
    import concourse.bacc as _bacc
    from concourse import mybir as _mybir
    from concourse.bass_utils import run_bass_kernel_spmd as _run

    v = {k: _np.asarray(x) for k, x in v.items()}
    s, t, f = "L0_conv_", "L1_attn_", "L1_ffn_"
    halves = lambda x: x.reshape(HV, P).T
    states = lambda x: _np.repeat(x, JB).reshape(P, 1)
    arrays = {
        "x": v["x"].reshape(B, L, D), "w_in": v[s + "W_in"], "conv_k": v[s + "conv_k"].reshape(1, 9 * DI),
        "w_xp": v[s + "W_xproj"], "w_dt": v[s + "W_dt"], "w_dtn": v[s + "W_dtN"], "w_out": v[s + "W_out"],
        "b_out": v[s + "b_out"].reshape(1, D),
        "vecs": _np.concatenate([halves(v[s + "b_dt"]), halves(v[s + "Dskip"]), halves(v[s + "ln_g"]), halves(v[s + "ln_b"]),
                                 states(v[s + "b_dtN"]), states(v[s + "A_log"])], axis=1),
        "norm_gamma": v[t + "norm_gamma"].reshape(P, 1), "w_qkv": v[t + "w_qkv"].T, "w_proj": v[t + "w_out"].T,
        "out_gamma": v[t + "out_gamma"].reshape(1, D), "w_gate": v[f + "Wg"],
        "w1": v[f + "W1"], "w2": v[f + "W2"], "w3": v[f + "W3"],
        "b3": v[f + "b3"].reshape(NE, MF, P).transpose(2, 0, 1),
        **constants(),
    }
    nc = _bacc.Bacc("TRN2", target_bir_lowering=False, num_devices=1, dynamic_dma_scratch_size=4096)
    given, aps = {}, {}
    for name in _ORDER:
        x = _np.ascontiguousarray(arrays[name])
        given[f"in_{name}"] = x
        aps[name] = nc.dram_tensor(f"in_{name}", x.shape, _mybir.dt.from_np(x.dtype), kind="ExternalInput").ap()
    aps["out"] = nc.dram_tensor("out_0", (B, L, D), F32, kind="ExternalOutput").ap()
    build(nc, aps)
    r = _run(nc, [given], core_ids=[0])
    return r.results[0]["out_0"].reshape(B, H, W, D)
```

```python
from contextlib import ExitStack

import numpy as np

import concourse.bass as bass
from concourse import mybir

ALU = mybir.AluOpType
ACT = mybir.ActivationFunctionType
AX = mybir.AxisListType
F32 = mybir.dt.float32
BF16 = mybir.dt.bfloat16
U32 = mybir.dt.uint32
I32 = mybir.dt.int32

P = 128
B, H, W, D = 8, 48, 48, 128
L = H * W
DI, NS, RK = 256, 16, 8
HV = DI // P
T = 384
ROWS = T // W
NC = L // T
TT = T // P
NT = L // P
JB = P // NS
NB = DI // JB
QD = 4
NH, DH = 8, 16
NE, F = 8, 384
MF = F // P
PARTS = 3
N_CLEAR, N_SETUP = 4, 17
ACT_STEPS, DVE_STEPS = (13, 4), (63, 58)
BESIDE = (("dtr", 0, 1), ("dt0", 2, 1), ("dt1", 4, 1), ("C", 6, 1), ("mean", 8, -1), ("var", 12, -1), ("B", 15, 1),
          ("dtN", 17, 1), ("out", 21, -1), ("z0", 24, 1), ("z1", 28, 1))
CONV_AT = ((1, 2, 4, 5, 9, 10, 13, 14, 18), (20, 22, 24, 25, 26, 28, 29, 30, 31))
FOLD_LAG = 3
TOP = 2
NU = (TOP * L + NE * (P - 1)) // P
NSC = TOP * NT
TILE0, TILE_STEP, GATHER0 = NSC + 9, 3, 179
GB_ROWS = 6
UIN = 4
WS = 3
LOAD_LEAD = 8
LAG = 3
HS = 8


def constants():
    eye = np.eye(P, dtype=np.float32)
    idx = np.arange(P)
    group = (idx[:, None] // 4 == idx[None, :] // 4).astype(np.float32) / 4
    heads = (idx[:, None] // DH == idx[None, :] // DH).astype(np.float32)
    mean = np.full((P, P), 1.0 / DI, np.float32)
    r = np.arange(32 * PARTS) % 32
    copy = np.stack([(r[:, None] == JB * b + idx[None, :] % JB) for b in range(4)], 1)
    fold = np.stack([(JB * b + idx[:, None] % JB == np.arange(32)[None, :]) for b in range(4)], 1)
    iota = np.broadcast_to(np.arange(NU, dtype=np.float32), (P, NU))
    before = (idx[:, None] < idx[None, :]).astype(np.float32)
    running = np.broadcast_to(np.tile((np.arange(NT) > 0).astype(np.float32), NE), (P, NE * NT))
    return {
        "eye": eye, "group": group, "heads": heads, "mean": mean, "iota": np.ascontiguousarray(iota), "before": before,
        "full": np.ones((P, P), np.float32), "running": np.ascontiguousarray(running),
        "copy": np.ascontiguousarray(copy.astype(np.float32)), "fold": np.ascontiguousarray(fold.astype(np.float32)),
    }


def build(nc, a):
    with ExitStack() as ctx:
        def sb(name, shape, dt=F32):
            return ctx.enter_context(nc.sbuf_tensor(name, shape, dt))

        def psum(name):
            return ctx.enter_context(nc.psum_tensor(name, [P, 512], F32))

        eye, group, heads, mean = (sb(n, [P, P]) for n in ("eye", "group", "heads", "mean"))
        before, full_ones = sb("before", [P, P]), sb("full_ones", [P, P])
        iota, running = sb("iota", [P, NU]), sb("running", [P, NE, NT])
        fold = sb("fold", [P, 4, 32])
        copy = sb("copy", [32 * PARTS, 4, P], BF16)
        w_conv = sb("w_conv", [P, 9, DI])
        w_z = sb("w_z", [P, DI])
        w_xp = sb("w_xp", [P, HV, RK + 2 * NS])
        w_b, w_c, w_n = (sb(n, [P, HV, P]) for n in ("w_b", "w_c", "w_n"))
        w_dtn = sb("w_dtn", [P, HV, NS])
        w_dt = sb("w_dt", [RK, DI])
        w_out = sb("w_out", [P, HV, D])
        b_out, ones = sb("b_out", [1, D]), sb("ones", [1, P])
        vecs = sb("vecs", [P, 16])
        w_qkv = sb("w_qkv", [P, 3 * D])
        w_proj = sb("w_proj", [P, D])
        out_gamma = sb("out_gamma", [P, D])
        w_gate = sb("w_gate", [P, NE])
        w_exp = sb("w_exp", [P, WS, 3 * F + MF])
        b_dt, d_skip, ln_g, ln_b = (vecs[:, 2 * k:2 * k + 2] for k in range(4))
        b_dtn, decay_rate, eps_ln, norm_gamma = (vecs[:, k:k + 1] for k in (8, 9, 10, 11))
        x_tok = sb("x_tok", [P, NT, D])
        gx = sb("gx", [P, H + 2, W + 2])
        t1 = sb("t1", [P, NT, D])
        big_t = sb("big_t", [P, L])
        big_k = sb("big_k", [P, L])
        big_u = sb("big_u", [P, NT, D])
        qv = sb("qv", [P, 2, NT, D])
        xc = sb("xc", [P, 3, HV, T])
        z_tmp = sb("z_tmp", [P, HV, T])
        sz = sb("sz", [P, 2, HV, T])
        dt = sb("dt", [P, HV, T])
        dt_tmp = sb("dt_tmp", [P, HV, T])
        dt_r = sb("dt_r", [RK, T])
        parts = sb("parts", [P, PARTS, HV, T], BF16)
        rest = sb("rest", [P, HV, T])
        x_stack = sb("x_stack", [32 * PARTS, 2, HV * QD, T], BF16)
        dt_stack = sb("dt_stack", [32 * PARTS, 2, HV * QD, T], BF16)
        b_rep = sb("b_rep", [P, T])
        db_rep = sb("db_rep", [P, 2, T])
        c_rep = sb("c_rep", [P, 2, T])
        decay = sb("decay", [P, 2, T])
        inflow = sb("inflow", [P, 2, T])
        state = sb("state", [P, HS, T])
        carry = sb("carry", [P, NB])
        prod = sb("prod", [P, HS, T])
        y = sb("y", [P, HV, T])
        y_sq = sb("y_sq", [P, HV, T])
        y_rs = sb("y_rs", [P, T])
        gst = sb("gst", [P, NC, 6])
        gmv = sb("gmv", [P, 8])
        gdev = sb("gdev", [P, 2 * NC])
        st = sb("st", [P, NT, 6])
        mv = sb("mv", [P, NT, 2])
        r1, r2, nb = (sb(n, [P, NT]) for n in ("r1", "r2", "nb"))
        q_max, q_sum = sb("q_max", [P, NT * NH]), sb("q_sum", [P, NT * NH])
        k_col = sb("k_col", [P, 4])
        ctx_t, ctx_o = sb("ctx_t", [P, D]), sb("ctx_o", [P, D])
        logit, top = (sb(n, [P, NT, NE]) for n in ("logit", "top"))
        each = [big_k[:, NE * NT * k:NE * NT * (k + 1)].rearrange("p (e t) -> p e t", e=NE) for k in range(7)]
        chosen, (both_of, upto, earlier, rank, picked) = each[0:TOP], each[TOP:]
        tally = sb("tally", [P, 4, NE])
        owner = big_k[:, NE * NT * 7:NE * NT * 7 + NU * NE].rearrange("p (u e) -> p u e", e=NE)
        tile_expert, expert_of = sb("tile_expert", [P, NU]), sb("expert_of", [P, NU], I32)
        pos, row_of = sb("pos", [P, TOP, NT]), sb("row_of", [P, NSC], I32)
        where = sb("where", [P, NT, NE], U32)
        place = sb("place", [P, NT, NE])
        gw = sb("gw", [P, 4, NT])

        ps_dt, ps_x, ps_y, ps_conv = (psum(n) for n in ("ps_dt", "ps_x", "ps_y", "ps_conv"))
        ps_main, ps_h, ps_g, ps_sum = (psum(n) for n in ("ps_main", "ps_h", "ps_g", "ps_sum"))

        class Next:

            def __init__(self, j, ahead=1):
                self.j, self.ahead = j, ahead

        class Sem:

            def __init__(self, name, per, unit=1, first=0):
                self.sem = ctx.enter_context(nc.semaphore(name))
                self.per, self.unit, self.first = per, unit, first

            def at(self, i, k):
                if isinstance(i, Next):
                    return i.j * (self.per * self.unit) + (self.first + (i.ahead * self.per + k) * self.unit)
                return i * (self.per * self.unit) + (self.first + k * self.unit)

        banks = [ps_main, ps_h, ps_g, ps_sum]
        MAIN, HB, GB, SB = range(4)
        scan_uses = [f"xT{g}" for g in range(NC)] + ["gm", "gv"]
        scan_uses += [f"{name}0" for name, n, dc in BESIDE if dc == 1]
        for c in range(NC):
            scan_uses += [f"{name}{c + dc}" for name, n, dc in BESIDE if 0 <= c + dc < NC]
        scan_uses += [f"{name}{NC - 1}" for name, n, dc in BESIDE if dc == -1]
        attn_uses = [f"xnT{g}" for g in range(NC)] + [f"kT{g}" for g in range(NC)] + [f"qv{g}" for g in range(NT // 2)]
        attn_uses += [f"ek{g}" for g in range(NC)] + ["ctx", "ctx2"] + [f"qT{g}" for g in range(NC)]
        attn_uses += [f"ao{g}" for g in range(NC)] + [f"uT{g}" for g in range(NC)] + ["logit", "rank"]
        placed = [(name, MAIN) for name in scan_uses]
        placed += [(name, (HB, GB, SB)[n % 3]) for n, name in enumerate(attn_uses)]
        NPAIR = NU + LAG
        placed += [(f"pair{v}", SB) for v in range(NPAIR)]
        for u in range(NU):
            placed += [(f"h{u}", HB), (f"g{u}", GB)]
        aux_of = {}
        aux_per = [0] * 4
        for name, b in placed:
            aux_of[name] = (b, aux_per[b])
            aux_per[b] += 1
        bank_names = ("main", "h", "g", "sum")
        aux_full = [Sem(f"{bank_names[b]}_full", aux_per[b]) for b in range(4)]
        aux_free = [Sem(f"{bank_names[b]}_free", aux_per[b], first=1) for b in range(4)]

        def aux(name):
            return banks[aux_of[name][0]]

        def free(i, name):
            b, k = aux_of[name]
            return aux_free[b].sem, aux_free[b].at(i, k)

        def full(i, name):
            b, k = aux_of[name]
            return aux_full[b].sem, aux_full[b].at(i, k + 1)

        def read(i, name):
            b, k = aux_of[name]
            return aux_free[b].sem, aux_free[b].at(i, k + 1)

        def fills(name):
            return aux_full[aux_of[name][0]].sem

        def frees(name):
            return aux_free[aux_of[name][0]].sem

        def other_bank(name, *inputs):
            last = {}
            for x in inputs:
                b, k = aux_of[x]
                if b != aux_of[name][0] and (b not in last or k > aux_of[last[b]][1]):
                    last[b] = x
            return list(last.values())

        SC = NB * NC
        s_const = Sem("s_const", 0)
        s_half = Sem("s_half", 0)
        s_clear, s_setup, s_rate = Sem("s_clear", 0), Sem("s_setup", 0), Sem("s_rate", 0)
        s_x, s_xlast = Sem("s_x", 1, 16 * (NC - 1)), Sem("s_xlast", 1, 16)
        s_norm = Sem("s_norm", 1)
        s_tanh = Sem("s_tanh", 2 * NC)
        s_dtl = Sem("s_dtl", NC)
        s_dt = Sem("s_dt", NC)
        s_hi, s_rest, s_mid, s_lo = (Sem(n, 2 * NC) for n in ("s_hi", "s_rest", "s_mid", "s_lo"))
        s_xstack = Sem("s_xstack", NC, 16 * PARTS * QD)
        s_dtstack = Sem("s_dtstack", NC, 16 * PARTS * QD)
        s_dtrep = Sem("s_dtrep", SC)
        s_dtread = Sem("s_dtread", SC, first=1)
        s_xrep = Sem("s_xrep", SC)
        s_xread = Sem("s_xread", SC, first=1)
        s_state = Sem("s_state", SC)
        s_prod = Sem("s_prod", SC)
        s_fold = Sem("s_fold", SC // QD)
        s_y = Sem("s_y", 2 * NC)
        s_ysq = Sem("s_ysq", NC)
        s_yrs = Sem("s_yrs", NC)
        s_yn = Sem("s_yn", NC)
        s_yaff = Sem("s_yaff", NC)
        s_yg = Sem("s_yg", NC)
        s_conv = Sem("s_conv", 2 * NC)
        s_xc = Sem("s_xc", 2 * NC, first=1)
        s_gn = Sem("s_gn", 2)
        s_var = Sem("s_var", 4)
        s_root = Sem("s_root", 4)
        s_groot = Sem("s_groot", 1)
        s_htanh = Sem("s_htanh", NU)
        s_sorted = Sem("s_sorted", 2)
        s_init = Sem("s_init", 0)
        s_scatter = Sem("s_scatter", NSC, 16)
        in_slot = [(NU + UIN - 1 - b) // UIN for b in range(UIN)]
        s_uload = [Sem(f"s_uload{b}", in_slot[b], 16) for b in range(UIN)]
        s_ostore = [Sem(f"s_ostore{b}", in_slot[b], 16) for b in range(UIN)]
        s_gather = [Sem(f"s_gather{b}", GB_ROWS, 16) for b in range(NSC // GB_ROWS)]
        s_added = Sem("s_added", TOP, first=1)
        s_coef = Sem("s_coef", 3)
        s_xn = Sem("s_xn", 3 * NC)
        s_qsub = Sem("s_qsub", 1)
        s_qexp = Sem("s_qexp", 1)
        s_q = Sem("s_q", 1)
        s_top, s_topexp = Sem("s_top", 1), Sem("s_topexp", 1)
        act_step, act_post = Sem("act_step", ACT_STEPS[0]), Sem("act_post", ACT_STEPS[1])
        dve_step, dve_post = Sem("dve_step", DVE_STEPS[0]), Sem("dve_post", DVE_STEPS[1])
        s_kmax = Sem("s_kmax", 1)
        s_kexp = Sem("s_kexp", 1)
        s_w = [Sem(f"s_w{b}", (NU + WS - 1 - b) // WS, 16) for b in range(WS)]
        s_out = Sem("s_out", 1, 16, first=16)

        acc = qv[:, 0]
        qv_rest = qv[:, 1].rearrange("p k d -> p (k d)").rearrange("p (s t) -> p s t", t=F)
        HID = 4
        hidden, silu = qv_rest[:, 0:HID], qv_rest[:, HID:HID + 2]
        tiles = big_t[:, :].rearrange("p (s d) -> p s d", d=D)
        u_in, u_t, u_out = tiles[:, 0:UIN], tiles[:, UIN:UIN + 3], tiles[:, UIN + 3:2 * UIN + 3]
        gathered = (big_u[:, :, :], big_k[:, :].rearrange("p (k d) -> p k d", d=D))
        rows_in = nc.dram_tensor("rows_in", [NU * P, D], F32, kind="Internal").ap()
        rows_out = nc.dram_tensor("rows_out", [NU * P, D], F32, kind="Internal").ap()

        def tile_at(k, shift, n=NU):
            u, r = divmod(k - TILE0 - shift, TILE_STEP)
            return u if r == 0 and 0 <= u < n else None

        PAIR = -4
        assert TILE0 + TILE_STEP * (NPAIR - 1) + PAIR + 2 < GATHER0 <= SC

        block = ctx.enter_context(nc.Block())
        n_const = 0
        N_INIT = 16 * -(-NU // NT)

        @block.sync
        def _(sp):
            nonlocal n_const
            loads = [
                (eye[:, :], a["eye"]), (group[:, :], a["group"]), (heads[:, :], a["heads"]), (mean[:, :], a["mean"]),
                (iota[:, :], a["iota"]), (before[:, :], a["before"]), (full_ones[:, :], a["full"]),
                (running[:, :, :], a["running"].rearrange("p (e t) -> p e t", e=NE)), (fold[:, :, :], a["fold"]),
                (prod[0:32 * PARTS, 0:2, 0:256].rearrange("p s t -> p s t"),
                 a["copy"].rearrange("p (s b) m -> p s (b m)", s=2)),
                (y[:, 0, 0:DI], a["w_in"][:, 0:DI]), (w_z[:, :], a["w_in"][:, DI:2 * DI]),
                (state[:, 0:6, :].rearrange("p s t -> p (s t)"), a["conv_k"].broadcast_to([P, 9 * DI])),
                (w_xp[:, :, :], a["w_xp"].rearrange("(h p) n -> p h n", p=P)),
                (w_dtn[:, :, :], a["w_dtn"].rearrange("(h p) n -> p h n", p=P)),
                (w_dt[:, :], a["w_dt"]),
                (w_out[:, :, :], a["w_out"].rearrange("(h p) n -> p h n", p=P)),
                (b_out[:, :], a["b_out"]), (vecs[:, 0:10], a["vecs"]), (vecs[:, 11:12], a["norm_gamma"]),
                (w_qkv[:, :], a["w_qkv"]), (w_proj[:, :], a["w_proj"]), (out_gamma[:, :], a["out_gamma"].broadcast_to([P, D])),
                (w_gate[:, :], a["w_gate"]),
            ]
            for dst, src in loads:
                sp.dma_start(dst, src).then_inc(s_const.sem, 16)
            n_const = 16 * len(loads)

            def stack(i, c, k):
                s_full, dst_of = ((s_xstack, x_stack), (s_dtstack, dt_stack))[k]
                sp.wait_ge(s_lo.sem, s_lo.at(i, 2 * c + k + 1))
                for part in range(PARTS):
                    for q in range(QD):
                        dst = dst_of[32 * part:32 * part + 32, c % 2].rearrange("p (h q) t -> p h q t", q=QD)[:, :, q, :]
                        sp.dma_start(dst, parts[32 * q:32 * q + 32, part]).then_inc(s_full.sem, 16)

            def load_tile(j, u):
                if u == 0:
                    sp.wait_ge(s_scatter.sem, s_scatter.at(j, NSC))
                if u == 1:
                    sp.wait_ge(s_added.sem, s_added.at(j, 0))
                if u >= UIN:
                    sp.wait_ge(*full(j, f"pair{u - UIN}"))
                sp.dma_start(u_in[:, u % UIN, :], rows_in[P * u:P * u + P, :]).then_inc(s_uload[u % UIN].sem, 16)

            def store_tile(j, u):
                sp.wait_ge(*read(j, f"pair{u + LAG}"))
                sp.dma_start(rows_out[P * u:P * u + P, :], u_out[:, u % UIN, :]).then_inc(s_ostore[u % UIN].sem, 16)

            def image(i, j):
                for k in range(-NB, SC):
                    c, n = k // NB + 1, k % NB
                    if i is not None and c < NC and n in (7, 20):
                        stack(i, c, 0 if n == 7 else 1)
                    if j is not None:
                        for u in range(NU):
                            if k == max(TILE0 + TILE_STEP * u + PAIR - LOAD_LEAD, NSC):
                                load_tile(j, u)
                        if tile_at(k, TILE_STEP * LAG + PAIR + 2) is not None:
                            store_tile(j, tile_at(k, TILE_STEP * LAG + PAIR + 2))

            sp.wait_ge(s_clear.sem, N_CLEAR)
            zeros = rows_in.rearrange("(k p) d -> p k d", p=P)
            for k in range(0, NU, NT):
                n = min(NT, NU - k)
                sp.dma_start(zeros[:, k:k + n, :], big_u[:, 0:n, :]).then_inc(s_init.sem, 16)
            sp.wait_ge(s_init.sem, N_INIT)
            image(0, None)
            with sp.Fori(0, B - 1) as j:
                image(Next(j), j)
            image(None, B - 1)

        @block.gpsimd
        def _(pool):
            pool.memset(gx[:, :, :], 0.0).then_inc(s_clear.sem, 1)
            pool.memset(ones[:, :], 1.0).then_inc(s_clear.sem, 1)
            pool.memset(eps_ln, 1e-5).then_inc(s_clear.sem, 1)
            pool.memset(big_u[:, :, :], 0.0).then_inc(s_clear.sem, 1)
            pool.wait_ge(s_clear.sem, N_CLEAR)
            pool.wait_ge(s_init.sem, N_INIT)

            def sources(j, k):
                if k == 0:
                    pool.wait_ge(s_xn.sem, s_xn.at(j, 3 * NC))
                    pool.wait_ge(s_sorted.sem, s_sorted.at(j, 2))
                if k == GATHER0:
                    for b in range(UIN):
                        pool.wait_ge(s_ostore[b].sem, s_ostore[b].at(j, in_slot[b]))

            def experts(j, k):
                if k < NSC:
                    pool.indirect_dma_start(rows_in, bass.IndirectOffsetOnAxis(ap=row_of[:, k:k + 1], axis=0),
                                            big_u[:, k % NT, :], None).then_inc(s_scatter.sem, 16)
                g = k - GATHER0
                if 0 <= g < NSC:
                    pool.indirect_dma_start(gathered[g // NT][:, g % NT, :], None, rows_out,
                                            bass.IndirectOffsetOnAxis(ap=row_of[:, g:g + 1], axis=0)).then_inc(s_gather[g // GB_ROWS].sem, 16)

            def products(i, j):
                for c in range(NC):
                    pool.wait_ge(*read(i, f"C{c}"))
                    for n in range(NB):
                        k = NB * c + n
                        if j is not None:
                            sources(j, k)
                        pool.wait_ge(s_state.sem, s_state.at(i, k + 1))
                        if k >= HS:
                            pool.wait_ge(s_fold.sem, s_fold.at(i, (k - HS) // QD + 1))
                        pool.tensor_tensor(prod[:, n % HS, :], state[:, n % HS, :], c_rep[:, c % 2, :], ALU.mult).then_inc(s_prod.sem, 1)
                        if j is not None:
                            experts(j, k)

            products(0, None)
            with pool.Fori(0, B - 1) as j:
                products(Next(j), j)
                for k in range(SC, GATHER0 + NSC):
                    experts(j, k)
            for k in range(GATHER0 + NSC):
                sources(B - 1, k)
                experts(B - 1, k)

        @block.tensor
        def _(pe):
            pe.wait_ge(s_const.sem, n_const)
            pe.wait_ge(s_clear.sem, N_CLEAR)
            pe.wait_ge(s_setup.sem, N_SETUP)

            def transposes(i, names, src):
                for g, name in enumerate(names):
                    pe.wait_ge(*free(i, name))
                    for k in range(TT):
                        ins = pe.transpose(aux(name)[:, P * k:P * k + P], src(TT * g + k), eye[:, :])
                    ins.then_inc(fills(name), 1)

            def turn(i):
                pe.wait_ge(s_x.sem, s_x.at(i, 1))
                transposes(i, [f"xT{g}" for g in range(NC - 1)], lambda k: x_tok[:, k, :])
                pe.wait_ge(s_xlast.sem, s_xlast.at(i, 1))
                transposes(i, [f"xT{NC - 1}"], lambda k: x_tok[:, k + TT * (NC - 1), :])

            def group_norm(i):
                for k, name in enumerate(("gm", "gv")):
                    pe.wait_ge(*free(i, name))
                    pe.wait_ge(s_gn.sem, s_gn.at(i, k + 1))
                    pe.matmul(aux(name)[:, 0:1], group[:, :], gmv[:, 2 * k:2 * k + 1], start=True, stop=True).then_inc(fills(name), 1)

            def halves(i, name, lhs, rhs, rows=P, inputs=()):
                pe.wait_ge(*free(i, name))
                for x in other_bank(name, *inputs):
                    pe.wait_ge(*read(i, x))
                for hf in range(HV):
                    ins = pe.matmul(aux(name)[0:rows, 0:T], lhs[:, hf, :], rhs[:, hf, :], start=hf == 0, stop=hf == HV - 1)
                ins.then_inc(fills(name), 1)

            def conv(i, c, hf, tap):
                if tap == 0:
                    pe.wait_ge(s_xc.sem, s_xc.at(i, 2 * c + hf))
                dy, dx = tap // 3, tap % 3
                ins = pe.matmul(ps_conv[:, 0:T], w_conv[:, tap, P * hf:P * hf + P],
                                gx[:, ROWS * c + dy:ROWS * c + dy + ROWS, dx:dx + W], start=tap == 0, stop=tap == 8)
                if tap == 8:
                    ins.then_inc(s_conv.sem, 1)

            def project(i, c, name):
                use = f"{name}{c}"
                hf = int(name[-1]) if name[-1] in "01" else 0
                pe.wait_ge(*free(i, use))
                if name == "dtr":
                    pe.wait_ge(s_xc.sem, s_xc.at(i, 2 * c + 2))
                if name[:2] == "dt" and name[-1] in "01":
                    for x in other_bank(use, f"dtr{c}"):
                        pe.wait_ge(*read(i, x))
                    ins = pe.matmul(aux(use)[:, 0:T], w_dt[:, P * hf:P * hf + P], dt_r[:, :], start=True, stop=True)
                elif name[0] == "z":
                    ins = pe.matmul(aux(use)[:, 0:T], w_z[:, P * hf:P * hf + P],
                                    gx[:, ROWS * c + 1:ROWS * c + 1 + ROWS, 1:1 + W], start=True, stop=True)
                else:
                    if name == "dtN":
                        pe.wait_ge(s_dt.sem, s_dt.at(i, c + 1))
                    lhs = {"B": w_b, "C": w_c, "dtr": w_xp[:, :, 0:RK], "dtN": w_n}[name]
                    rhs = dt if name == "dtN" else xc[:, c % 3]
                    rows = RK if name == "dtr" else P
                    for h in range(HV):
                        ins = pe.matmul(aux(use)[0:rows, 0:T], lhs[:, h, :], rhs[:, h, :], start=h == 0, stop=h == HV - 1)
                ins.then_inc(fills(use), 1)

            def fold_quad(i, c, m):
                hf, b = m // 4, m % 4
                if b == 0 and (c or hf):
                    pe.wait_ge(s_y.sem, s_y.at(i, 2 * c + hf))
                pe.wait_ge(s_prod.sem, s_prod.at(i, NB * c + QD * (m + 1)))
                for q in range(QD):
                    ins = pe.matmul(ps_y[32 * q:32 * q + 32, 0:T], fold[:, b, :], prod[:, (QD * m + q) % HS, :],
                                    start=b == 0, stop=b == 3)
                ins.then_inc(s_fold.sem, 1)

            def beside(i, c, n):
                if c + 2 < NC:
                    for hf in range(HV):
                        if n in CONV_AT[hf]:
                            conv(i, c + 2, hf, CONV_AT[hf].index(n))
                for name, at, dc in BESIDE:
                    if at == n and 0 <= c + dc < NC:
                        if dc == 1:
                            project(i, c + 1, name)
                        else:
                            finish(i, c - 1, name)

            def scan(i, c, j):
                par = c % 2
                pe.wait_ge(s_dtstack.sem, s_dtstack.at(i, c + 1))
                pe.wait_ge(s_xstack.sem, s_xstack.at(i, c + 1))
                for n in range(NB):
                    k = NB * c + n
                    hf, b, q = n // 16, n % 16 // 4, n % 4
                    pe.wait_ge(s_dtread.sem, s_dtread.at(i, k))
                    pe.matmul(ps_dt[:, 0:T], copy[:, b, :], dt_stack[:, par, QD * hf + q, :],
                              start=True, stop=True).then_inc(s_dtrep.sem, 1)
                    pe.wait_ge(s_xread.sem, s_xread.at(i, k))
                    pe.matmul(ps_x[:, 0:T], copy[:, b, :], x_stack[:, par, QD * hf + q, :],
                              start=True, stop=True).then_inc(s_xrep.sem, 1)
                    if j is not None:
                        experts(j, k)
                    if n % QD == FOLD_LAG and k >= QD:
                        fold_quad(i, (k - QD) // NB, (n // QD - 1) % (NB // QD))
                    beside(i, c, n)

            def finish(i, c, name):
                use = f"{name}{c}"
                pe.wait_ge(*free(i, use))
                if name == "mean":
                    pe.wait_ge(s_y.sem, s_y.at(i, 2 * c + 2))
                elif name == "var":
                    pe.wait_ge(s_ysq.sem, s_ysq.at(i, c + 1))
                else:
                    pe.wait_ge(s_yg.sem, s_yg.at(i, c + 1))
                if name != "out":
                    src = y if name == "mean" else y_sq
                    for hf in range(HV):
                        ins = pe.matmul(aux(use)[:, 0:T], mean[:, :], src[:, hf, :], start=hf == 0, stop=hf == 1)
                else:
                    for k in range(TT):
                        o = aux(use)[:, P * k:P * k + P]
                        for hf in range(HV):
                            pe.matmul(o, y[:, hf, P * k:P * k + P], w_out[:, hf, :], start=hf == 0, stop=False)
                        ins = pe.matmul(o, ones[0:1, :], b_out[0:1, :], start=False, stop=True)
                ins.then_inc(fills(use), 1)

            def attend_project(i):
                names = [f"xnT{g}" for g in range(NC)]
                for g, name in enumerate(names):
                    pe.wait_ge(s_xn.sem, s_xn.at(i, g + 1))
                    pe.wait_ge(*free(i, name))
                    for k in range(TT):
                        ins = pe.transpose(aux(name)[:, P * k:P * k + P], big_u[:, TT * g + k, :], eye[:, :])
                    ins.then_inc(fills(name), 1)
                for g in range(NC):
                    name = f"kT{g}"
                    pe.wait_ge(*free(i, name))
                    for x in other_bank(name, f"xnT{g}"):
                        pe.wait_ge(*read(i, x))
                    pe.matmul(aux(name)[:, 0:T], w_qkv[:, D:2 * D], big_t[:, T * g:T * g + T], start=True, stop=True).then_inc(fills(name), 1)
                for g in range(NT // 2):
                    name = f"qv{g}"
                    pe.wait_ge(*free(i, name))
                    for x in other_bank(name, *(f"xnT{h}" for h in range(2 * g // TT, (2 * g + 1) // TT + 1))):
                        pe.wait_ge(*read(i, x))
                    for k in range(2):
                        lhs = big_t[:, P * (2 * g + k):P * (2 * g + k + 1)]
                        for w in range(2):
                            ins = pe.matmul(aux(name)[:, D * (2 * k + w):D * (2 * k + w + 1)], lhs, w_qkv[:, 2 * w * D:(2 * w + 1) * D],
                                            start=True, stop=True)
                    ins.then_inc(fills(name), 1)

            def attend_context(i):
                pe.wait_ge(s_kexp.sem, s_kexp.at(i, 1))
                transposes(i, [f"ek{g}" for g in range(NC)], lambda k: big_k[:, P * k:P * k + P])
                pe.wait_ge(*free(i, "ctx"))
                for x in other_bank("ctx", *(f"ek{g}" for g in range(NC)), *(f"qv{g}" for g in range(NT // 2))):
                    pe.wait_ge(*read(i, x))
                for k in range(NT):
                    ins = pe.matmul(aux("ctx")[:, 0:D], qv[:, 1, k, :], big_u[:, k, :], start=k == 0, stop=k == NT - 1)
                ins.then_inc(fills("ctx"), 1)
                pe.wait_ge(*free(i, "ctx2"))
                for x in other_bank("ctx2", "ctx"):
                    pe.wait_ge(*read(i, x))
                pe.matmul(aux("ctx2")[:, 0:D], ctx_t[:, :], w_proj[:, :], start=True, stop=True).then_inc(fills("ctx2"), 1)

            def attend_out(i):
                pe.wait_ge(s_q.sem, s_q.at(i, 1))
                transposes(i, [f"qT{g}" for g in range(NC)], lambda k: qv[:, 0, k, :])
                for g in range(NC):
                    name = f"ao{g}"
                    pe.wait_ge(*free(i, name))
                    for x in other_bank(name, "ctx2", f"qT{g}"):
                        pe.wait_ge(*read(i, x))
                    for k in range(TT):
                        o = T * g + P * k
                        ins = pe.matmul(aux(name)[:, P * k:P * k + P], big_t[:, o:o + P], ctx_o[:, :], start=True, stop=True)
                    ins.then_inc(fills(name), 1)

            def route(i):
                for g in range(NC):
                    name = f"uT{g}"
                    pe.wait_ge(s_xn.sem, s_xn.at(i, 2 * NC + g + 1))
                    pe.wait_ge(*free(i, name))
                    for k in range(TT):
                        ins = pe.transpose(aux(name)[:, P * k:P * k + P], big_u[:, TT * g + k, :], eye[:, :])
                    ins.then_inc(fills(name), 1)
                pe.wait_ge(*free(i, "logit"))
                for x in other_bank("logit", *(f"uT{g}" for g in range(NC))):
                    pe.wait_ge(*read(i, x))
                for k in range(NT):
                    ins = pe.matmul(aux("logit")[:, NE * k:NE * k + NE], big_t[:, P * k:P * k + P], w_gate[:, :], start=True, stop=True)
                ins.then_inc(fills("logit"), 1)

            def sort(i):
                pe.wait_ge(s_sorted.sem, s_sorted.at(i, 1))
                pe.wait_ge(*free(i, "rank"))
                o = aux("rank")[:, 0:NE * NT]
                pe.matmul(o, before[:, :], both_of[:, :, :], start=True, stop=False)
                pe.matmul(o, full_ones[:, :], earlier[:, :, :], start=False, stop=True)
                pe.matmul(aux("rank")[:, NE * NT:NE * NT + NE], full_ones[:, :], upto[:, :, NT - 1],
                          start=True, stop=True).then_inc(fills("rank"), 1)

            def experts(j, k):
                for o, bank in enumerate("hg"):
                    u = tile_at(k, o)
                    if u is not None:
                        name = f"{bank}{u}"
                        if bank == "h":
                            pe.wait_ge(*read(j, f"pair{u}"))
                            pe.wait_ge(s_w[u % WS].sem, s_w[u % WS].at(j, u // WS + 1))
                        pe.wait_ge(*free(j, name))
                        for m in range(MF):
                            ins = pe.matmul(aux(name)[:, P * m:P * m + P], w_exp[:, u % WS, F * o + P * m:F * o + P * m + P],
                                            u_t[:, u % 3, :], start=True, stop=True)
                        ins.then_inc(fills(name), 1)
                v = tile_at(k, PAIR, NPAIR)
                if v is not None:
                    name, u = f"pair{v}", v - LAG
                    pe.wait_ge(*free(j, name))
                    if v < NU:
                        pe.wait_ge(s_uload[v % UIN].sem, s_uload[v % UIN].at(j, v // UIN + 1))
                        ins = pe.transpose(aux(name)[:, 0:P], u_in[:, v % UIN, :], eye[:, :])
                    if u >= 0:
                        pe.wait_ge(*read(j, f"g{u}"))
                        for m in range(MF):
                            ins = pe.matmul(aux(name)[:, P:2 * P], hidden[:, u % HID, P * m:P * m + P],
                                            w_exp[:, u % WS, 2 * F + P * m:2 * F + P * m + P], start=m == 0, stop=m == MF - 1)
                    ins.then_inc(fills(name), 1)

            def convs(i, c):
                for hf in range(HV):
                    for tap in range(9):
                        conv(i, c, hf, tap)

            def first(i, lo, hi):
                for name, at, dc in BESIDE:
                    if dc == 1 and lo <= at < hi:
                        project(i, 0, name)

            def start(i):
                pe.wait_ge(s_norm.sem, s_norm.at(i, 1))
                convs(i, 0)

            def scans(i, j):
                for c in range(NC):
                    scan(i, c, j)
                fold_quad(i, NC - 1, NB // QD - 1)
                for name, at, dc in BESIDE:
                    if dc == -1:
                        finish(i, NC - 1, name)

            turn(0)
            group_norm(0)
            start(0)
            first(0, 0, 15)
            convs(0, 1)
            first(0, 15, NB)
            scans(0, None)
            with pe.Fori(0, B - 1) as j:
                i = Next(j)
                turn(i)
                attend_project(j)
                group_norm(i)
                start(i)
                attend_context(j)
                attend_out(j)
                first(i, 0, 6)
                first(i, 6, 15)
                convs(i, 1)
                route(j)
                first(i, 15, NB)
                sort(j)
                scans(i, j)
            j = B - 1
            attend_project(j)
            attend_context(j)
            attend_out(j)
            route(j)
            sort(j)
            for k in range(SC):
                experts(j, k)

        @block.scalar
        def _(act):
            for s in (s_added, *aux_free, s_dtread, s_xread, s_xc, s_out):
                act.sem_inc(s.sem, s.first)
            act.wait_ge(s_const.sem, n_const)
            act.wait_ge(s_clear.sem, N_CLEAR)
            act.wait_ge(s_setup.sem, N_SETUP)
            act.wait_ge(s_half.sem, 1)
            act.wait_ge(s_init.sem, N_INIT)
            act.activation(y_rs[:, 0:1], decay_rate, ACT.Exp).then_inc(s_rate.sem, 1)
            act.wait_ge(s_rate.sem, 1)
            act.activation(decay_rate, y_rs[:, 0:1], ACT.Copy, scale=-1.0).then_inc(s_rate.sem, 1)
            act.wait_ge(s_rate.sem, 2)
            count = [0, 0]

            def link(i, ins):
                count[0] += 1
                ins.then_inc(act_step.sem, 1)
                act.wait_ge(act_step.sem, act_step.at(i, count[0]))

            def tie(j, ins):
                count[1] += 1
                ins.then_inc(act_post.sem, 1)
                act.wait_ge(act_post.sem, act_post.at(j, count[1]))

            def logs():
                act.preload_act_table_set("natural_log_exp_and_others")

            def tanhs():
                act.preload_act_table_set("exp_and_others")

            def evacuate(i, name, dst, src, func=ACT.Copy, **kw):
                act.wait_ge(*full(i, name))
                act.activation(dst, src, func, **kw).then_inc(frees(name), 1)

            roots = [0]

            def root(j, buf):
                roots[0] += 1
                act.wait_ge(s_var.sem, s_var.at(j, roots[0]))
                tie(j, act.activation(buf, buf, ACT.Ln))
                act.activation(buf, buf, ACT.Exp, scale=-0.5).then_inc(s_root.sem, 1)

            def load(i, chunks):
                image = i.j + i.ahead if isinstance(i, Next) else i
                rows = a["x"][bass.ds(image, 1)].rearrange("o (k p) d -> p (o k) d", p=P)
                for c in chunks:
                    act.dma_start(x_tok[:, TT * c:TT * c + TT, :], rows[:, TT * c:TT * c + TT, :]).then_inc((s_xlast if c == NC - 1 else s_x).sem, 16)

            def load_last(i, before):
                act.wait_ge(*read(before, f"out{NC - 1}"))
                load(i, [NC - 1])

            def store(j):
                act.wait_ge(s_added.sem, s_added.at(j, TOP))
                act.dma_start(a["out"][bass.ds(j, 1)].rearrange("o (k p) d -> p (o k) d", p=P), acc).then_inc(s_out.sem, 16)

            def turn(i):
                for g in range(NC):
                    evacuate(i, f"xT{g}", gx[:, 1 + ROWS * g:1 + ROWS * g + ROWS, 1:1 + W],
                             aux(f"xT{g}")[:, 0:T].rearrange("p (r w) -> p r w", w=W))

            def group_norm(i):
                group_var = gmv[:, 5:6]
                act.wait_ge(*read(i, "gv"))
                link(i, act.activation(group_var, group_var, ACT.Ln))
                act.activation(group_var, group_var, ACT.Exp, scale=-0.5).then_inc(s_groot.sem, 1)

            def copy_conv(i, c, hf):
                if c >= 3:
                    act.wait_ge(s_y.sem, s_y.at(i, 2 * (c - 3) + 2))
                act.wait_ge(s_conv.sem, s_conv.at(i, 2 * c + hf + 1))
                act.activation(xc[:, c % 3, hf, :], ps_conv[:, 0:T], ACT.Copy).then_inc(s_xc.sem, 1)

            def copy_C(i, c):
                if c >= 2:
                    act.wait_ge(s_prod.sem, s_prod.at(i, NB * (c - 1)))
                evacuate(i, f"C{c}", c_rep[:, c % 2, :], aux(f"C{c}")[:, 0:T])

            def copy_B(i, c):
                if c >= 1:
                    act.wait_ge(*read(i, f"dtN{c - 1}"))
                evacuate(i, f"B{c}", b_rep[:, :], aux(f"B{c}")[:, 0:T])

            def copy_dtr(i, c):
                evacuate(i, f"dtr{c}", dt_r[:, :], aux(f"dtr{c}")[0:RK, 0:T])

            def add_bias(i, c, hf):
                if c >= 1 and hf == 0:
                    act.wait_ge(s_rest.sem, s_rest.at(i, 2 * c))
                evacuate(i, f"dt{hf}{c}", dt[:, hf, :], aux(f"dt{hf}{c}")[:, 0:T], ACT.Identity, bias=b_dt[:, hf:hf + 1])

            def softplus(i, c, k):
                if k == 0:
                    act.wait_ge(*read(i, f"dt1{c}"))
                    link(i, act.activation(dt_tmp[:, :, :], dt[:, :, :], ACT.Abs))
                elif k == 1:
                    link(i, act.activation(dt_tmp[:, :, :], dt_tmp[:, :, :], ACT.Exp, scale=-1.0))
                else:
                    act.activation(dt_tmp[:, :, :], dt_tmp[:, :, :], ACT.Ln, bias=1.0).then_inc(s_dtl.sem, 1)

            def tanh_z(i, c, hf):
                if c >= 1 and hf == 0:
                    act.wait_ge(*read(i, f"z1{c - 1}"))
                act.wait_ge(*full(i, f"z{hf}{c}"))
                act.activation(z_tmp[:, hf, :], aux(f"z{hf}{c}")[:, 0:T], ACT.Tanh, scale=0.5).then_inc(s_tanh.sem, 1)

            def first_part(i, c, k):
                if k:
                    act.wait_ge(s_dt.sem, s_dt.at(i, c + 1))
                    act.wait_ge(s_xstack.sem, s_xstack.at(i, c + 1))
                else:
                    act.wait_ge(s_xc.sem, s_xc.at(i, 2 * c + 2))
                    if c:
                        act.wait_ge(s_dtstack.sem, s_dtstack.at(i, c))
                src = dt if k else xc[:, c % 3]
                act.activation(parts[:, 0], src[:, :, :], ACT.Copy).then_inc(s_hi.sem, 1)

            def second_part(i, c, k):
                act.wait_ge(s_rest.sem, s_rest.at(i, 2 * c + k + 1))
                act.activation(parts[:, 1], rest[:, :, :], ACT.Copy).then_inc(s_mid.sem, 1)

            def square(i, c):
                act.wait_ge(*read(i, f"mean{c}"))
                act.activation(y_sq[:, :, :], y[:, :, :], ACT.Square).then_inc(s_ysq.sem, 1)

            def inverse_root(i, c, k):
                if k == 0:
                    evacuate(i, f"var{c}", y_rs[:, :], aux(f"var{c}")[:, 0:T], ACT.Ln, bias=eps_ln)
                else:
                    act.wait_ge(*read(i, f"var{c}"))
                    act.activation(y_rs[:, :], y_rs[:, :], ACT.Exp, scale=-0.5).then_inc(s_yrs.sem, 1)

            def affine(i, c):
                act.wait_ge(s_yn.sem, s_yn.at(i, c + 1))
                for hf in range(HV):
                    ins = act.activation(y[:, hf, :], y[:, hf, :], ACT.Identity, bias=ln_b[:, hf:hf + 1], scale=ln_g[:, hf:hf + 1])
                ins.then_inc(s_yaff.sem, 1)

            def project(i, c, n):
                if n == 1:
                    first_part(i, c, 0)
                    copy_dtr(i, c)
                if n == 4:
                    second_part(i, c, 0)
                if n in (3, 5):
                    add_bias(i, c, (n - 3) // 2)
                if n in (6, 7):
                    softplus(i, c, n - 6)
                if n == 13:
                    softplus(i, c, 2)
                if n == 16:
                    copy_B(i, c)
                if n == 15:
                    first_part(i, c, 1)
                if n == 18:
                    second_part(i, c, 1)
                if n == 7:
                    copy_C(i, c)
                if n == 25:
                    tanh_z(i, c, 0)
                if n == 29:
                    tanh_z(i, c, 1)

            def finish(i, c, n):
                if n == 10:
                    square(i, c)
                if n in (13, 14):
                    inverse_root(i, c, n - 13)
                if n == 17:
                    affine(i, c)

            def weights(j, k):
                u = tile_at(k, -3)
                if u is not None:
                    e = act.value_load(expert_of[0:1, u:u + 1], min_val=0, max_val=NE - 1)
                    if u < WS:
                        act.wait_ge(aux_free[SB].sem, aux_free[SB].at(j, 0))
                    else:
                        act.wait_ge(*full(j, f"pair{u - WS + LAG}"))
                    act.dma_start(w_exp[:, u % WS, :], a["w_exp"][bass.ds(e, 1)].rearrange("o p f -> p (o f)")).then_inc(s_w[u % WS].sem, 16)

            def experts(j, k):
                u = tile_at(k, 0)
                if u is not None:
                    act.wait_ge(*full(j, f"h{u}"))
                    if u >= 2:
                        act.wait_ge(*read(j, f"g{u - 2}"))
                    act.activation(silu[:, u % 2, :], aux(f"h{u}")[:, 0:F], ACT.Tanh, scale=0.5).then_inc(s_htanh.sem, 1)
                v = tile_at(k, PAIR + 1, NPAIR)
                if v is not None:
                    name, u = f"pair{v}", v - LAG
                    if u >= UIN:
                        act.wait_ge(s_ostore[u % UIN].sem, s_ostore[u % UIN].at(j, u // UIN))
                    act.wait_ge(*full(j, name))
                    if v < NU:
                        ins = act.activation(u_t[:, v % 3, :], aux(name)[:, 0:P], ACT.Copy)
                    if u >= 0:
                        ins = act.activation(u_out[:, u % UIN, :], aux(name)[:, P:2 * P], ACT.Copy)
                    ins.then_inc(frees(name), 1)

            def scan(i, c, j, following):
                for n in range(NB):
                    k = NB * c + n
                    if j is not None and k == 0:
                        sort(j)
                    act.wait_ge(s_dtrep.sem, s_dtrep.at(i, k + 1))
                    if k >= 2:
                        act.wait_ge(s_state.sem, s_state.at(i, k - 1))
                    act.activation(decay[:, n % 2, :], ps_dt[:, 0:T], ACT.Exp, scale=decay_rate).then_inc(s_dtread.sem, 1)
                    if j is not None:
                        weights(j, k)
                    if c == NC - 1 and n == 24 and following is not None:
                        act.wait_ge(*read(i, f"out{NC - 2}"))
                        load(following, range(NC - 1))
                    if n == 13:
                        logs()
                    if c + 1 < NC:
                        project(i, c + 1, n)
                    if c:
                        finish(i, c - 1, n)
                    if n == 13:
                        tanhs()
                    if j is not None:
                        experts(j, k)
                    if c + 2 < NC:
                        for hf in range(HV):
                            if n == min(CONV_AT[hf][-1] + 1, NB - 1):
                                copy_conv(i, c + 2, hf)

            def attend_start(i):
                root(i, r1[:, :])
                root(i, r2[:, :])

            def attend_project(i):
                for g in range(NC):
                    evacuate(i, f"xnT{g}", big_t[:, T * g:T * g + T], aux(f"xnT{g}")[:, 0:T])
                for g in range(NC):
                    evacuate(i, f"kT{g}", big_k[:, T * g:T * g + T], aux(f"kT{g}")[:, 0:T])
                act.wait_ge(s_out.sem, s_out.at(i, 0))
                for g in range(NT // 2):
                    evacuate(i, f"qv{g}", qv[:, :, 2 * g:2 * g + 2, :].rearrange("p w k d -> p k w d"),
                             aux(f"qv{g}")[:, :].rearrange("p (k w d) -> p k w d", k=2, w=2))

            def attend_context(i):
                for g in (NC - 3, NC - 2, NC - 1):
                    act.wait_ge(*read(i, f"kT{g}"))
                act.wait_ge(s_kmax.sem, s_kmax.at(i, 1))
                act.activation(big_k[:, :], big_k[:, :], ACT.Exp, bias=k_col[:, 0:1], accum_out=k_col[:, 1:2]).then_inc(s_kexp.sem, 1)
                act.wait_ge(s_qsub.sem, s_qsub.at(i, 1))
                act.activation(qv[:, 0], qv[:, 0], ACT.Exp).then_inc(s_qexp.sem, 1)
                for g in range(NC):
                    evacuate(i, f"ek{g}", big_u[:, TT * g:TT * g + TT, :].rearrange("p k d -> p (k d)"), aux(f"ek{g}")[:, 0:T])

            def attend_out(i):
                for g in range(NC):
                    evacuate(i, f"qT{g}", big_t[:, T * g:T * g + T], aux(f"qT{g}")[:, 0:T])
                for g in range(NC):
                    evacuate(i, f"ao{g}", big_k[:, T * g:T * g + T], aux(f"ao{g}")[:, 0:T])

            def attend_norm(i):
                root(i, r1[:, :])

            def route(i):
                root(i, r1[:, :])
                for g in range(NC):
                    evacuate(i, f"uT{g}", big_t[:, T * g:T * g + T], aux(f"uT{g}")[:, 0:T])
                act.wait_ge(s_top.sem, s_top.at(i, 1))
                act.activation(gw[:, 0, :], gw[:, 0, :], ACT.Exp).then_inc(s_topexp.sem, 1)

            def sort(i):
                act.wait_ge(s_sorted.sem, s_sorted.at(i, 2))

            def convs(i, c):
                for hf in range(HV):
                    copy_conv(i, c, hf)

            def first(i, lo, hi):
                for n in range(lo, hi):
                    project(i, 0, n)

            def scans(i, j, following):
                tanhs()
                for c in range(NC):
                    scan(i, c, j, following)
                logs()
                for n in range(NB):
                    finish(i, NC - 1, n)

            logs()
            load(0, range(NC))
            turn(0)
            group_norm(0)
            convs(0, 0)
            first(0, 0, 15)
            convs(0, 1)
            tanhs()
            first(0, 15, NB)
            scans(0, None, 1)
            assert count[0] == ACT_STEPS[0], count
            load_last(1, 0)
            turn(1)

            def both(i, j, following):
                count[:], roots[0] = (0, 0), 0
                attend_start(j)
                attend_project(j)
                group_norm(i)
                convs(i, 0)
                attend_context(j)
                attend_out(j)
                first(i, 0, 6)
                attend_norm(j)
                first(i, 6, 15)
                convs(i, 1)
                route(j)
                tanhs()
                first(i, 15, NB)
                scans(i, j, following)
                if following is not None:
                    load_last(following, i)
                    turn(following)
                store(j)

            with act.Fori(0, B - 2) as j:
                both(Next(j), j, Next(j, 2))
            both(B - 1, B - 2, None)
            assert count == [ACT_STEPS[0], ACT_STEPS[1]], count
            j = B - 1
            count[:], roots[0] = (0, 0), 0
            logs()
            attend_start(j)
            attend_project(j)
            attend_context(j)
            attend_out(j)
            attend_norm(j)
            route(j)
            sort(j)
            tanhs()
            for k in range(SC):
                weights(j, k)
                experts(j, k)
            store(j)
            act.wait_ge(s_out.sem, 16 * (B + 1))

        @block.vector
        def _(dve):
            dve.wait_ge(s_const.sem, n_const)
            for k, (dst, src) in enumerate(((w_b, w_xp[:, :, RK:RK + NS]), (w_c, w_xp[:, :, RK + NS:RK + 2 * NS]), (w_n, w_dtn[:, :, :]))):
                for hf in range(HV):
                    dve.tensor_copy(dst[:, hf, :].rearrange("p (n j) -> p n j", j=JB),
                                    src[:, hf, :].unsqueeze(2).broadcast_to([P, NS, JB])).then_inc(s_setup.sem, 1)
            taps = state[:, 0:6, :].rearrange("p s t -> p (s t)").rearrange("p (k d) -> p k d", d=DI)
            for tap in range(9):
                dve.tensor_tensor(w_conv[:, tap, :], y[:, 0, 0:DI], taps[:, tap, :], ALU.mult).then_inc(s_setup.sem, 1)
            dve.tensor_scalar(w_qkv[:, :], w_qkv[:, :], norm_gamma, None, ALU.mult).then_inc(s_setup.sem, 1)
            dve.tensor_copy(copy[:, :, :].rearrange("p (s b) m -> p s (b m)", s=2), prod[0:32 * PARTS, 0:2, 0:256]).then_inc(s_setup.sem, 1)
            dve.wait_ge(s_clear.sem, N_CLEAR)
            dve.wait_ge(s_setup.sem, N_SETUP)
            dve.tensor_scalar(vecs[:, 4:8], vecs[:, 4:8], 0.5, None, ALU.mult).then_inc(s_half.sem, 1)
            count = [0, 0]

            def link(i, ins):
                count[0] += 1
                ins.then_inc(dve_step.sem, 1)
                dve.wait_ge(dve_step.sem, dve_step.at(i, count[0]))

            def tie(j, ins):
                count[1] += 1
                ins.then_inc(dve_post.sem, 1)
                dve.wait_ge(dve_post.sem, dve_post.at(j, count[1]))

            def turn(i):
                for g in range(NC):
                    dve.wait_ge(*read(i, f"xT{g}"))
                    ins = dve.bn_stats(gst[:, g, :], gx[:, 1 + ROWS * g:1 + ROWS * g + ROWS, 1:1 + W])
                    link(i, ins)

            def group_norm(i):
                part = gst[:, :, :].rearrange("p g (s k) -> p (g s) k", k=3)
                link(i, dve.tensor_reduce(gmv[:, 7:8], part[:, :, 1], AX.X, ALU.add))
                link(i, dve.tensor_scalar(gmv[:, 0:1], gmv[:, 7:8], 1.0 / (2 * NC), None, ALU.mult))
                link(i, dve.tensor_scalar(gdev[:, :], part[:, :, 1], gmv[:, 0:1], None, ALU.subtract))
                link(i, dve.tensor_tensor(gdev[:, :], gdev[:, :], gdev[:, :], ALU.mult))
                link(i, dve.tensor_scalar(gdev[:, :], gdev[:, :], L / (2.0 * NC), None, ALU.mult))
                link(i, dve.tensor_tensor(gdev[:, :], gdev[:, :], part[:, :, 2], ALU.add))
                link(i, dve.tensor_reduce(gmv[:, 7:8], gdev[:, :], AX.X, ALU.add))
                dve.tensor_scalar(gmv[:, 1:2], gmv[:, 7:8], 1.0 / L, None, ALU.mult).then_inc(s_gn.sem, 1)
                dve.wait_ge(s_gn.sem, s_gn.at(i, 1))
                dve.wait_ge(*full(i, "gm"))
                dve.tensor_copy(gmv[:, 4:5], aux("gm")[:, 0:1]).then_inc(frees("gm"), 1)
                dve.wait_ge(*read(i, "gm"))
                link(i, dve.tensor_tensor(gmv[:, 3:4], gmv[:, 0:1], gmv[:, 4:5], ALU.subtract))
                dve.scalar_tensor_tensor(out=gmv[:, 2:3], in0=gmv[:, 3:4], scalar=gmv[:, 3:4], in1=gmv[:, 1:2],
                                         op0=ALU.mult, op1=ALU.add).then_inc(s_gn.sem, 1)
                dve.wait_ge(*full(i, "gv"))
                dve.tensor_scalar(gmv[:, 5:6], aux("gv")[:, 0:1], 1e-5, None, ALU.add).then_inc(frees("gv"), 1)
                dve.wait_ge(s_groot.sem, s_groot.at(i, 1))
                link(i, dve.scalar_tensor_tensor(out=gmv[:, 6:7], in0=gmv[:, 4:5], scalar=-1.0, in1=gmv[:, 5:6],
                                                 op0=ALU.mult, op1=ALU.mult))
                inner = gx[:, 1:1 + H, 1:1 + W]
                dve.tensor_scalar(inner, inner, gmv[:, 5:6], gmv[:, 6:7], ALU.mult, ALU.add).then_inc(s_norm.sem, 1)

            def project(i, c, n):
                if n in (2, 16):
                    k = 0 if n == 2 else 1
                    src = dt if k else xc[:, c % 3]
                    dve.wait_ge(s_hi.sem, s_hi.at(i, 2 * c + k + 1))
                    dve.tensor_tensor(rest[:, :, :], src[:, :, :], parts[:, 0], ALU.subtract).then_inc(s_rest.sem, 1)
                if n in (6, 19):
                    k = 0 if n == 6 else 1
                    dve.wait_ge(s_mid.sem, s_mid.at(i, 2 * c + k + 1))
                    dve.tensor_tensor(parts[:, 2], rest[:, :, :], parts[:, 1], ALU.subtract).then_inc(s_lo.sem, 1)
                if n == 14:
                    dve.wait_ge(s_dtl.sem, s_dtl.at(i, c + 1))
                    dve.scalar_tensor_tensor(out=dt[:, :, :], in0=dt[:, :, :], scalar=0.0, in1=dt_tmp[:, :, :],
                                             op0=ALU.max, op1=ALU.add).then_inc(s_dt.sem, 1)
                if n == 18:
                    use = f"dtN{c}"
                    dve.wait_ge(*full(i, use))
                    dve.scalar_tensor_tensor(out=db_rep[:, c % 2, :], in0=aux(use)[:, 0:T], scalar=b_dtn, in1=b_rep[:, :],
                                             op0=ALU.add, op1=ALU.mult).then_inc(frees(use), 1)
                if n in (26, 30):
                    hf = 0 if n == 26 else 1
                    use = f"z{hf}{c}"
                    dve.wait_ge(s_tanh.sem, s_tanh.at(i, 2 * c + hf + 1))
                    dve.scalar_tensor_tensor(out=sz[:, c % 2, hf, :], in0=z_tmp[:, hf, :], scalar=1.0, in1=aux(use)[:, 0:T],
                                             op0=ALU.add, op1=ALU.mult).then_inc(frees(use), 1)

            def skip(i, c, hf):
                dve.wait_ge(s_fold.sem, s_fold.at(i, NB // QD * c + 4 * (hf + 1)))
                dve.scalar_tensor_tensor(out=y[:, hf, :], in0=xc[:, c % 3, hf, :], scalar=d_skip[:, hf:hf + 1], in1=ps_y[:, 0:T],
                                         op0=ALU.mult, op1=ALU.add).then_inc(s_y.sem, 1)

            def finish(i, c, n):
                both = lambda v: v.unsqueeze(1).broadcast_to([P, HV, T])
                if n == 5:
                    skip(i, c, 1)
                if n == 8:
                    use = f"mean{c}"
                    dve.wait_ge(*full(i, use))
                    dve.wait_ge(s_y.sem, s_y.at(i, 2 * c + 2))
                    dve.tensor_tensor(y[:, :, :], y[:, :, :], both(aux(use)[:, 0:T]), ALU.subtract).then_inc(frees(use), 1)
                if n == 15:
                    dve.wait_ge(s_yrs.sem, s_yrs.at(i, c + 1))
                    dve.wait_ge(*read(i, f"mean{c}"))
                    dve.tensor_tensor(y[:, :, :], y[:, :, :], both(y_rs[:, :]), ALU.mult).then_inc(s_yn.sem, 1)
                if n == 18:
                    dve.wait_ge(s_yaff.sem, s_yaff.at(i, c + 1))
                    dve.tensor_tensor(y[:, :, :], y[:, :, :], sz[:, c % 2], ALU.mult).then_inc(s_yg.sem, 1)
                if n == 22:
                    use = f"out{c}"
                    dve.wait_ge(*full(i, use))
                    tok = slice(TT * c, TT * c + TT)
                    dve.tensor_tensor(t1[:, tok, :].rearrange("p k d -> p (k d)"), aux(use)[:, 0:T],
                                      x_tok[:, tok, :].rearrange("p k d -> p (k d)"), ALU.add).then_inc(frees(use), 1)

            def inflows(i, c, n):
                k = NB * c + n
                dve.wait_ge(s_xrep.sem, s_xrep.at(i, k + 1))
                if k >= 2:
                    dve.wait_ge(s_state.sem, s_state.at(i, k - 1))
                dve.tensor_tensor(inflow[:, n % 2, :], ps_x[:, 0:T], db_rep[:, c % 2, :], ALU.mult).then_inc(s_xread.sem, 1)

            def scan(i, c, j):
                if c == 0:
                    dve.wait_ge(*read(i, f"dtN{c}"))
                    inflows(i, c, 0)
                for n in range(NB):
                    k = NB * c + n
                    if j is not None:
                        experts(j, k)
                    if n + 1 < NB:
                        inflows(i, c, n + 1)
                    elif c + 1 < NC:
                        dve.wait_ge(*read(i, f"dtN{c + 1}"))
                        inflows(i, c + 1, 0)
                    dve.wait_ge(s_xread.sem, s_xread.at(i, k + 1))
                    dve.wait_ge(s_dtread.sem, s_dtread.at(i, k + 1))
                    if k >= HS:
                        dve.wait_ge(s_prod.sem, s_prod.at(i, k - HS + 1))
                    init = carry[:, n:n + 1] if c else 0.0
                    dve.tensor_tensor_scan(state[:, n % HS, :], decay[:, n % 2, :], inflow[:, n % 2, :], init,
                                           ALU.mult, ALU.add).then_inc(s_state.sem, 1)
                    if n % QD == QD - 1:
                        dve.wait_ge(s_state.sem, s_state.at(i, k + 1))
                        s0 = n % HS - QD + 1
                        link(i, dve.tensor_copy(carry[:, n - QD + 1:n + 1], state[:, s0:s0 + QD, T - 1]))
                    if c + 1 < NC:
                        project(i, c + 1, n)
                    if c:
                        finish(i, c - 1, n)
                    if n == 22:
                        skip(i, c, 0)

            roots = [0]


            def stats(i, k, src, twice=False):
                for t in range(NT):
                    ins = dve.bn_stats(st[:, t, :], src[:, t, :])
                tie(i, ins)
                tie(i, dve.tensor_tensor(mv[:, :, 0], st[:, :, 1], st[:, :, 4], ALU.subtract))
                tie(i, dve.tensor_tensor(mv[:, :, 0], mv[:, :, 0], mv[:, :, 0], ALU.mult))
                tie(i, dve.tensor_tensor(mv[:, :, 1], st[:, :, 2], st[:, :, 5], ALU.add))
                tie(i, dve.scalar_tensor_tensor(out=mv[:, :, 1], in0=mv[:, :, 0], scalar=D / 4.0, in1=mv[:, :, 1], op0=ALU.mult, op1=ALU.add))
                tie(i, dve.tensor_scalar(mv[:, :, 1], mv[:, :, 1], 1.0 / D, None, ALU.mult))
                tie(i, dve.tensor_tensor(mv[:, :, 0], st[:, :, 1], st[:, :, 4], ALU.add))
                tie(i, dve.tensor_scalar(mv[:, :, 0], mv[:, :, 0], 0.5, None, ALU.mult))
                dve.tensor_scalar(r1[:, :], mv[:, :, 1], 1e-5, None, ALU.add).then_inc(s_var.sem, 1)
                roots[0] += 1
                dve.wait_ge(s_root.sem, s_root.at(i, roots[0]))
                if twice:
                    tie(i, dve.tensor_tensor(r2[:, :], mv[:, :, 1], r1[:, :], ALU.mult))
                    tie(i, dve.tensor_tensor(r2[:, :], r2[:, :], r1[:, :], ALU.mult))
                    dve.tensor_scalar(r2[:, :], r2[:, :], 1e-5, None, ALU.add).then_inc(s_var.sem, 1)
                    roots[0] += 1
                    dve.wait_ge(s_root.sem, s_root.at(i, roots[0]))
                    tie(i, dve.tensor_tensor(r1[:, :], r1[:, :], r2[:, :], ALU.mult))
                dve.scalar_tensor_tensor(out=nb[:, :], in0=mv[:, :, 0], scalar=-1.0, in1=r1[:, :],
                                         op0=ALU.mult, op1=ALU.mult).then_inc(s_coef.sem, 1)

            def normalise(i, k, src, dst):
                dve.wait_ge(s_coef.sem, s_coef.at(i, k + 1))
                for g in range(NC):
                    for t in range(TT * g, TT * g + TT):
                        ins = dve.tensor_scalar(dst[:, t, :], src[:, t, :], r1[:, t:t + 1], nb[:, t:t + 1], ALU.mult, ALU.add)
                    ins.then_inc(s_xn.sem, 1)

            def attend_start(i):
                dve.wait_ge(*read(i, f"out{NC - 1}"))
                stats(i, 0, t1, twice=True)
                normalise(i, 0, t1, big_u)

            def attend_context(i):
                q = qv[:, 0].rearrange("p k (h d) -> p (k h) d", d=DH)
                for g in (NC - 3, NC - 2, NC - 1):
                    dve.wait_ge(*read(i, f"kT{g}"))
                tie(i, dve.tensor_reduce(k_col[:, 2:3], big_k[:, :], AX.X, ALU.max))
                dve.tensor_scalar(k_col[:, 0:1], k_col[:, 2:3], -1.0, None, ALU.mult).then_inc(s_kmax.sem, 1)
                for g in (NT // 2 - 3, NT // 2 - 2, NT // 2 - 1):
                    dve.wait_ge(*read(i, f"qv{g}"))
                tie(i, dve.tensor_reduce(q_max[:, :], q, AX.X, ALU.max))
                dve.tensor_tensor(q, q, q_max[:, :].unsqueeze(2).broadcast_to([P, NT * NH, DH]), ALU.subtract).then_inc(s_qsub.sem, 1)
                dve.wait_ge(s_kexp.sem, s_kexp.at(i, 1))
                tie(i, dve.reciprocal(k_col[:, 3:4], k_col[:, 1:2]))
                dve.wait_ge(s_qexp.sem, s_qexp.at(i, 1))
                tie(i, dve.tensor_reduce(q_sum[:, :], q, AX.X, ALU.add))
                tie(i, dve.reciprocal(q_max[:, :], q_sum[:, :]))
                dve.tensor_tensor(q, q, q_max[:, :].unsqueeze(2).broadcast_to([P, NT * NH, DH]), ALU.mult).then_inc(s_q.sem, 1)
                dve.wait_ge(*full(i, "ctx"))
                dve.tensor_tensor(ctx_t[:, :], aux("ctx")[:, 0:D], heads[:, :], ALU.mult).then_inc(frees("ctx"), 1)
                dve.wait_ge(*full(i, "ctx2"))
                dve.tensor_scalar(ctx_o[:, :], aux("ctx2")[:, 0:D], k_col[:, 3:4], DH ** -0.5, ALU.mult, ALU.mult).then_inc(frees("ctx2"), 1)

            def attend_norm(i):
                for g in (NC - 3, NC - 2, NC - 1):
                    dve.wait_ge(*read(i, f"ao{g}"))
                ao = big_k[:, :].rearrange("p (k d) -> p k d", d=D)
                stats(i, 1, ao)
                normalise(i, 1, ao, ao)
                dve.wait_ge(s_xn.sem, s_xn.at(i, 2 * NC))
                tie(i, dve.tensor_tensor(ao, ao, out_gamma[:, :].unsqueeze(1).broadcast_to([P, NT, D]), ALU.mult))
                tie(i, dve.tensor_tensor(acc, t1[:, :, :], ao, ALU.add))

            def route(i):
                stats(i, 2, acc)
                normalise(i, 2, acc, big_u)
                dve.wait_ge(*full(i, "logit"))
                dve.tensor_copy(logit[:, :, :].rearrange("p k e -> p (k e)"), aux("logit")[:, 0:NT * NE])
                for t in range(NT):
                    ins = dve.max(top[:, t, :], aux("logit")[:, NE * t:NE * t + NE])
                ins.then_inc(frees("logit"), 1)
                dve.wait_ge(*read(i, "logit"))
                dve.tensor_tensor(gw[:, 0, :], top[:, :, 1], top[:, :, 0], ALU.subtract).then_inc(s_top.sem, 1)
                for t in range(NT):
                    ins = dve.max_index(where[:, t, :], top[:, t, :], logit[:, t, :])
                tie(i, ins)
                tie(i, dve.tensor_copy(place[:, :, :], where[:, :, :]))
                dve.wait_ge(s_topexp.sem, s_topexp.at(i, 1))
                tie(i, dve.tensor_scalar(gw[:, 1, :], gw[:, 0, :], 1.0, None, ALU.add))
                tie(i, dve.reciprocal(gw[:, 2, :], gw[:, 1, :]))
                tie(i, dve.tensor_scalar(gw[:, 2, :], gw[:, 2, :], 0.5, None, ALU.mult))
                tie(i, dve.tensor_tensor(gw[:, 3, :], gw[:, 2, :], gw[:, 0, :], ALU.mult))
                for k in range(TOP):
                    ins = dve.tensor_tensor(chosen[k], place[:, :, k].unsqueeze(1).broadcast_to([P, NE, NT]),
                                            iota[:, 0:NE].unsqueeze(2).broadcast_to([P, NE, NT]), ALU.is_equal)
                    tie(i, ins)
                tie(i, dve.tensor_tensor(both_of[:, :, :], chosen[0], chosen[1], ALU.add))
                flat = lambda v: v[:, :, :].rearrange("p e t -> p (e t)")
                tie(i, dve.tensor_tensor_scan(flat(upto), flat(running), flat(both_of), 0.0, ALU.mult, ALU.add))
                dve.tensor_tensor(earlier[:, :, :], upto[:, :, :], both_of[:, :, :], ALU.subtract).then_inc(s_sorted.sem, 1)

            def sort(i):
                dve.wait_ge(*full(i, "rank"))
                tie(i, dve.tensor_copy(tally[:, 0, :], aux("rank")[:, NE * NT:NE * NT + NE]))
                tie(i, dve.tensor_scalar(tally[:, 3, :], tally[:, 0, :], 1.0 / P, None, ALU.mult))
                tie(i, dve.tensor_tensor(picked[:, :, :], tally[:, 3, :].unsqueeze(2).broadcast_to([P, NE, NT]),
                                         iota[:, 0:NT].unsqueeze(1).broadcast_to([P, NE, NT]), ALU.is_gt))
                tie(i, dve.tensor_reduce(tally[:, 1, :], picked[:, :, :], AX.X, ALU.add))
                tie(i, dve.tensor_tensor_scan(tally[:, 2, :], full_ones[:, 0:NE], tally[:, 1, :], 0.0, ALU.mult, ALU.add))
                tie(i, dve.tensor_tensor(tally[:, 3, :], tally[:, 2, :], tally[:, 1, :], ALU.subtract))
                tie(i, dve.tensor_scalar(tally[:, 3, :], tally[:, 3, :], float(P), None, ALU.mult))
                dve.tensor_tensor(rank[:, :, :], aux("rank")[:, 0:NE * NT].rearrange("p (e t) -> p e t", e=NE),
                                  tally[:, 3, :].unsqueeze(2).broadcast_to([P, NE, NT]), ALU.add).then_inc(frees("rank"), 1)
                dve.wait_ge(*read(i, "rank"))
                for k in range(TOP):
                    tie(i, dve.tensor_tensor(picked[:, :, :], chosen[k], rank[:, :, :], ALU.mult))
                    tie(i, dve.tensor_reduce(pos[:, k, :], picked[:, :, :].rearrange("p e t -> p t e"), AX.X, ALU.add))
                tie(i, dve.tensor_copy(row_of[:, :], pos[:, :, :].rearrange("p k t -> p (k t)")))
                tie(i, dve.tensor_tensor(owner[:, :, :], iota[:, :].unsqueeze(2).broadcast_to([P, NU, NE]),
                                         tally[:, 2, :].unsqueeze(1).broadcast_to([P, NU, NE]), ALU.is_ge))
                tie(i, dve.tensor_reduce(tile_expert[:, :], owner[:, :, :], AX.X, ALU.add))
                dve.tensor_scalar(expert_of[:, :], tile_expert[:, :], float(NE - 1), None, ALU.min).then_inc(s_sorted.sem, 1)

            def experts(j, k):
                u = tile_at(k, 1)
                if u is not None:
                    dve.wait_ge(s_htanh.sem, s_htanh.at(j, u + 1))
                    dve.scalar_tensor_tensor(out=silu[:, u % 2, :], in0=silu[:, u % 2, :], scalar=1.0, in1=aux(f"h{u}")[:, 0:F],
                                             op0=ALU.add, op1=ALU.mult).then_inc(frees(f"h{u}"), 1)
                u = tile_at(k, 2)
                if u is not None:
                    dve.wait_ge(*full(j, f"g{u}"))
                    dve.wait_ge(*read(j, f"h{u}"))
                    if u >= HID:
                        dve.wait_ge(*full(j, f"pair{u - HID + LAG}"))
                    for m in range(MF):
                        o = slice(P * m, P * m + P)
                        ins = dve.scalar_tensor_tensor(out=hidden[:, u % HID, o], in0=aux(f"g{u}")[:, o],
                                                       scalar=w_exp[:, u % WS, 3 * F + m:3 * F + m + 1],
                                                       in1=silu[:, u % 2, o], op0=ALU.add, op1=ALU.mult)
                    ins.then_inc(frees(f"g{u}"), 1)
                g = k - GATHER0 - GB_ROWS - 1
                if 0 <= g < NSC:
                    n, t = g // NT, g % NT
                    if g == NT:
                        dve.wait_ge(s_added.sem, s_added.at(j, 1))
                    if g % GB_ROWS == 0:
                        dve.wait_ge(s_gather[g // GB_ROWS].sem, s_gather[g // GB_ROWS].at(j, GB_ROWS))
                    ins = dve.scalar_tensor_tensor(out=acc[:, t, :], in0=gathered[n][:, t, :], scalar=gw[:, 2 + n, t:t + 1],
                                                   in1=acc[:, t, :], op0=ALU.mult, op1=ALU.add)
                    if t == NT - 1:
                        ins.then_inc(s_added.sem, 1)

            def first(i, lo, hi):
                for n in range(lo, hi):
                    project(i, 0, n)

            def scans(i, j):
                for c in range(NC):
                    scan(i, c, j)
                for n in range(NB):
                    finish(i, NC - 1, n)

            turn(0)
            group_norm(0)
            first(0, 0, NB)
            scans(0, None)
            assert count[0] == DVE_STEPS[0], count
            with dve.Fori(0, B - 1) as j:
                i = Next(j)
                count[:], roots[0] = (0, 0), 0
                attend_start(j)
                turn(i)
                group_norm(i)
                attend_context(j)
                first(i, 0, 6)
                attend_norm(j)
                first(i, 6, 15)
                route(j)
                first(i, 15, NB)
                sort(j)
                scans(i, j)
                for k in range(SC, GATHER0 + NSC + GB_ROWS + 1):
                    experts(j, k)
            assert count == [DVE_STEPS[0], DVE_STEPS[1]], count
            j = B - 1
            count[:], roots[0] = (0, 0), 0
            attend_start(j)
            attend_context(j)
            attend_norm(j)
            route(j)
            sort(j)
            for k in range(GATHER0 + NSC + GB_ROWS + 1):
                experts(j, k)


_ORDER = ["x", "w_in", "conv_k", "w_xp", "w_dt", "w_dtn", "w_out", "b_out", "vecs", "norm_gamma", "w_qkv", "w_proj",
          "out_gamma", "w_gate", "w_exp", "before", "full", "running", "eye", "group", "heads", "mean", "iota", "copy", "fold"]


def kernel(**v):
    import numpy as _np
    import concourse.bacc as _bacc
    from concourse import mybir as _mybir
    from concourse.bass_utils import run_bass_kernel_spmd as _run

    v = {k: _np.asarray(x) for k, x in v.items()}
    s, t, f = "L0_conv_", "L1_attn_", "L1_ffn_"
    halves = lambda x: x.reshape(HV, P).T
    states = lambda x: _np.repeat(x, JB).reshape(P, 1)
    arrays = {
        "x": v["x"].reshape(B, L, D), "w_in": v[s + "W_in"], "conv_k": v[s + "conv_k"].reshape(1, 9 * DI),
        "w_xp": v[s + "W_xproj"], "w_dt": v[s + "W_dt"], "w_dtn": v[s + "W_dtN"], "w_out": v[s + "W_out"],
        "b_out": v[s + "b_out"].reshape(1, D),
        "vecs": _np.concatenate([halves(v[s + "b_dt"]), halves(v[s + "Dskip"]), halves(v[s + "ln_g"]), halves(v[s + "ln_b"]),
                                 states(v[s + "b_dtN"]), states(v[s + "A_log"])], axis=1),
        "norm_gamma": v[t + "norm_gamma"].reshape(P, 1), "w_qkv": v[t + "w_qkv"].T, "w_proj": v[t + "w_out"].T,
        "out_gamma": v[t + "out_gamma"].reshape(1, D), "w_gate": v[f + "Wg"],
        "w_exp": _np.concatenate([v[f + "W1"], v[f + "W3"], v[f + "W2"].reshape(NE, MF, P, D).transpose(0, 2, 1, 3).reshape(NE, P, F),
                                  v[f + "b3"].reshape(NE, MF, P).transpose(0, 2, 1)], axis=2),
        **constants(),
    }
    nc = _bacc.Bacc("TRN2", target_bir_lowering=False, num_devices=1, dynamic_dma_scratch_size=4096)
    given, aps = {}, {}
    for name in _ORDER:
        x = _np.ascontiguousarray(arrays[name])
        given[f"in_{name}"] = x
        aps[name] = nc.dram_tensor(f"in_{name}", x.shape, _mybir.dt.from_np(x.dtype), kind="ExternalInput").ap()
    aps["out"] = nc.dram_tensor("out_0", (B, L, D), F32, kind="ExternalOutput").ap()
    build(nc, aps)
    r = _run(nc, [given], core_ids=[0])
    return r.results[0]["out_0"].reshape(B, H, W, D)
```
